# Optimizing a Trainium2 kernel written in Bass

```python
import numpy as np
import jax
import jax.numpy as jnp

def _softmax(x, axis=-1):
    return jax.nn.softmax(x, axis=axis)

def _gelu(x):
    return jax.nn.gelu(x, approximate=True)

def _silu(x):
    return jax.nn.silu(x)

def _sigmoid(x):
    return jax.nn.sigmoid(x)

def _layernorm(x, axis=-1, eps=1e-05):
    m = jnp.mean(x, axis=axis, keepdims=True)
    v = jnp.var(x, axis=axis, keepdims=True)
    return (x - m) / jnp.sqrt(v + eps)

def _scatter_add(tgt, idx, src, axis=0):
    return tgt.at[idx].add(src)

def _segment_sum(src, seg, n):
    return jax.ops.segment_sum(src, seg, n)
kernel_name = 'mk_decoder_postln_d2_seqx_r8_aadd6a'

def setup_inputs(seed: int=0):
    np.random.seed(seed)
    _w = jnp.asarray

    def _rec_inputs():
        import jax
        import jax.numpy as jnp
        _rk = jax.random.key(seed)
        x = -0.000125 + 0.9999 * jax.random.normal(jax.random.fold_in(_rk, 1), (4, 256, 256), jnp.float32)
        _lenS = 256 - jax.random.randint(jax.random.fold_in(_rk, 7), (4,), 0, max(1, 256 // 4) + 1, jnp.int32)
        _lenS2 = 256 - jax.random.randint(jax.random.fold_in(_rk, 8), (4,), 0, max(1, 256 // 4) + 1, jnp.int32)
        itok_BxS_13_99985 = jax.random.randint(jax.random.fold_in(_rk, 11), (4, 256), 13, 99986, jnp.int32)
        _ctx_2048P = jax.random.normal(jax.random.fold_in(_rk, 12), (4, 16, 256), jnp.float32)
        _ctx_2048c = jax.random.dirichlet(jax.random.fold_in(_rk, 512), 0.3 * jnp.ones((16,), jnp.float32), (4, 256))
        _ctx_2048t = jnp.einsum('bsk,bkd->bsd', _ctx_2048c, _ctx_2048P)
        _ctx_2048t = _ctx_2048t * jax.lax.rsqrt(jnp.mean(jnp.square(_ctx_2048t)) + 1e-12) * 0.953939
        ctx_2048 = 6.82029e-06 + 0.0200006 * (_ctx_2048t + 0.3 * jax.random.normal(jax.random.fold_in(_rk, 612), (4, 256, 256), jnp.float32))
        return (x, itok_BxS_13_99985, ctx_2048)
    x, itok_BxS_13_99985, ctx_2048 = _rec_inputs()

    def _L0_attn_setup():
        import jax, jax.numpy as jnp
        import numpy as np
        HID = 256
        H = 16
        D = HID // H
        THETA = 10000.0

        def _rope(q, k):
            T = q.shape[1]
            half = D // 2
            inv_freq = 1.0 / THETA ** (jnp.arange(half, dtype=jnp.float32) / half)
            ang = jnp.arange(T, dtype=jnp.float32)[:, None] * inv_freq[None, :]
            cos = jnp.cos(ang)[None, :, None, :]
            sin = jnp.sin(ang)[None, :, None, :]

            def rot(x):
                x1, x2 = (x[..., :half], x[..., half:])
                return jnp.concatenate([x1 * cos - x2 * sin, x2 * cos + x1 * sin], axis=-1)
            return (rot(q), rot(k))
        key = jax.random.key(seed)
        ks = jax.random.split(key, 7)
        B, T = (1, 256)
        s = 1.0 / np.sqrt(HID)
        return {'hidden_states': jax.random.normal(ks[0], (B, T, HID), dtype=jnp.float32), 'Wq': jax.random.normal(ks[1], (HID, HID), dtype=jnp.float32) * s, 'Wk': jax.random.normal(ks[2], (HID, HID), dtype=jnp.float32) * s, 'Wv': jax.random.normal(ks[3], (HID, HID), dtype=jnp.float32) * s, 'Wb': jax.random.normal(ks[4], (HID, H), dtype=jnp.float32) * s, 'bb': jnp.zeros((H,), dtype=jnp.float32), 'Wo': jax.random.normal(ks[5], (HID, HID), dtype=jnp.float32) * s}
    _L0_attn_all = _L0_attn_setup()
    _L0_attn_in = {k: v for k, v in _L0_attn_all.items() if k in ('Wq', 'Wk', 'Wv', 'Wb', 'bb', 'Wo')}
    del _L0_attn_all

    def _L0_xattn_setup():
        import jax, jax.numpy as jnp
        import numpy as np
        B, S, D = (4, 512, 256)
        E = 4
        F = 1024 // E
        VOCAB = 12500
        key = jax.random.key(seed)
        k1, k2, k3, k4, k5 = jax.random.split(key, 5)
        hidden_states = jax.random.normal(k1, (B, S, D), dtype=jnp.float32)
        token_ids = jax.random.randint(k2, (B, S), 0, VOCAB, dtype=jnp.int64)
        Wg = jax.random.normal(k3, (E, F, D), dtype=jnp.float32) * 0.02
        Wu = jax.random.normal(k4, (E, F, D), dtype=jnp.float32) * 0.02
        Wd = jax.random.normal(k5, (E, D, F), dtype=jnp.float32) * 0.02
        return {'hidden_states': hidden_states, 'token_ids': token_ids, 'Wg': Wg, 'Wu': Wu, 'Wd': Wd}
    _L0_xattn_all = _L0_xattn_setup()
    _L0_xattn_in = {k: v for k, v in _L0_xattn_all.items() if k in ()}
    del _L0_xattn_all

    def _L0_ffn_setup():
        import jax, jax.numpy as jnp
        import numpy as np
        ALPHA = 1.702
        LIMIT = 7.0
        TOP_K = 4
        B, S, H = (1, 128, 256)
        E, D = (16, 256)
        key = jax.random.key(seed)
        ks = jax.random.split(key, 7)
        s = 0.02
        return {'hidden_states': jax.random.normal(ks[0], (B, S, H), dtype=jnp.float32), 'router_weight': jax.random.normal(ks[1], (E, H), dtype=jnp.float32) * s, 'router_bias': jax.random.normal(ks[2], (E,), dtype=jnp.float32) * s, 'gate_up_proj': jax.random.normal(ks[3], (E, H, 2 * D), dtype=jnp.float32) * s, 'gate_up_proj_bias': jax.random.normal(ks[4], (E, 2 * D), dtype=jnp.float32) * s, 'down_proj': jax.random.normal(ks[5], (E, D, H), dtype=jnp.float32) * s, 'down_proj_bias': jax.random.normal(ks[6], (E, H), dtype=jnp.float32) * s}
    _L0_ffn_all = _L0_ffn_setup()
    _L0_ffn_in = {k: v for k, v in _L0_ffn_all.items() if k in ('router_weight', 'router_bias', 'gate_up_proj', 'gate_up_proj_bias', 'down_proj', 'down_proj_bias')}
    del _L0_ffn_all

    def _L1_attn_setup():
        import jax, jax.numpy as jnp
        import numpy as np
        HIDDEN = 256
        HEAD_DIM = 64
        N_HEADS = HIDDEN // HEAD_DIM
        ROT_DIM = HEAD_DIM // 2
        THETA = 10000.0
        SCALE_BASE = 512.0
        EPS = 1e-05
        B, S = (1, 256)

        def _rotate_half(t):
            x1 = t[..., 0::2]
            x2 = t[..., 1::2]
            return jnp.stack([-x2, x1], axis=-1).reshape(t.shape)

        def _xpos_rotary(q, k, seqlen):
            dim = ROT_DIM
            inv_freq = 1.0 / THETA ** (jnp.arange(0, dim, 2, dtype=jnp.float32) / dim)
            t = jnp.arange(seqlen, dtype=jnp.float32)
            freqs = t[:, None] * inv_freq[None, :]
            freqs = jnp.repeat(freqs, 2, axis=-1)
            base_scale = (jnp.arange(0, dim, 2, dtype=jnp.float32) + 0.4 * dim) / (1.4 * dim)
            power = (t - seqlen // 2) / SCALE_BASE
            scale = base_scale[None, :] ** power[:, None]
            scale = jnp.concatenate([scale, scale], axis=-1)
            cos, sin = (jnp.cos(freqs), jnp.sin(freqs))

            def apply(x, sc):
                xr, xp = (x[..., :dim], x[..., dim:])
                xr = xr * cos * sc + _rotate_half(xr) * sin * sc
                return jnp.concatenate([xr, xp], axis=-1)
            return (apply(q, scale), apply(k, 1.0 / scale))

        def _msr_forward(x, wqkv, wg, wo, gn_weight, gn_bias):
            b, s, _ = x.shape
            qkv = x @ wqkv.T
            qkv = qkv.reshape(b, s, N_HEADS, 3 * HEAD_DIM).transpose(0, 2, 1, 3)
            q, k, v = jnp.split(qkv, 3, axis=-1)
            q, k = _xpos_rotary(q, k, s)
            gamma = 1.0 - 2.0 ** (-5.0 - jnp.arange(N_HEADS, dtype=jnp.float32))
            idx = jnp.arange(s)
            nm = idx[:, None] - idx[None, :]
            decay = jnp.where(nm >= 0, gamma[:, None, None] ** jnp.maximum(nm, 0).astype(jnp.float32), 0.0)
            scores = jnp.einsum('bhid,bhjd->bhij', q, k) * decay
            ret = jnp.einsum('bhij,bhjd->bhid', scores, v)
            mean = ret.mean(axis=(2, 3), keepdims=True)
            var = ret.var(axis=(2, 3), keepdims=True)
            ret = (ret - mean) / jnp.sqrt(var + EPS)
            ret = ret * gn_weight[None, :, None, None] + gn_bias[None, :, None, None]
            y = ret.transpose(0, 2, 1, 3).reshape(b, s, HIDDEN)
            g = x @ wg.T
            mish = g * jnp.tanh(jax.nn.softplus(g))
            return mish * y @ wo.T
        key = jax.random.key(seed)
        ks = jax.random.split(key, 4)
        std = HIDDEN ** (-0.5)
        x = jax.random.normal(ks[0], (B, S, HIDDEN), jnp.float32)
        wqkv = jax.random.normal(ks[1], (3 * HIDDEN, HIDDEN), jnp.float32) * std
        wg = jax.random.normal(ks[2], (HIDDEN, HIDDEN), jnp.float32) * std
        wo = jax.random.normal(ks[3], (HIDDEN, HIDDEN), jnp.float32) * std
        gn_weight = jnp.ones((N_HEADS,), jnp.float32)
        gn_bias = jnp.zeros((N_HEADS,), jnp.float32)
        return {'x': x, 'wqkv': wqkv, 'wg': wg, 'wo': wo, 'gn_weight': gn_weight, 'gn_bias': gn_bias}
    _L1_attn_all = _L1_attn_setup()
    _L1_attn_in = {k: v for k, v in _L1_attn_all.items() if k in ('wqkv', 'wg', 'wo', 'gn_weight', 'gn_bias')}
    del _L1_attn_all

    def _L1_xattn_setup():
        import jax, jax.numpy as jnp
        import numpy as np
        B_DIM, T_DIM, C_DIM = (16, 128, 256)

        def _wkv(w, u, k, v):
            Bn, Tn, Cn = k.shape
            NEG_INF = jnp.float32(-1e+38)

            def step(carry, kv_t):
                p, q, o = carry
                kt, vt = kv_t
                no = jnp.maximum(o, u + kt)
                A = jnp.exp(o - no)
                E = jnp.exp(u + kt - no)
                y = (A * p + E * vt) / (A * q + E)
                no2 = jnp.maximum(w + o, kt)
                A2 = jnp.exp(w + o - no2)
                E2 = jnp.exp(kt - no2)
                return ((A2 * p + E2 * vt, A2 * q + E2, no2), y)
            init = (jnp.zeros((Bn, Cn), k.dtype), jnp.zeros((Bn, Cn), k.dtype), jnp.full((Bn, Cn), NEG_INF, k.dtype))
            kT = jnp.moveaxis(k, 1, 0)
            vT = jnp.moveaxis(v, 1, 0)
            _, yT = jax.lax.scan(step, init, (kT, vT))
            return jnp.moveaxis(yT, 0, 1)
        key = jax.random.key(seed)
        k1, k2, k3, k4 = jax.random.split(key, 4)
        w = -jnp.exp(jax.random.normal(k1, (C_DIM,), jnp.float32))
        u = jax.random.normal(k2, (C_DIM,), jnp.float32)
        k = jax.random.normal(k3, (B_DIM, T_DIM, C_DIM), jnp.float32)
        v = jax.random.normal(k4, (B_DIM, T_DIM, C_DIM), jnp.float32)
        return {'B': B_DIM, 'T': T_DIM, 'C': C_DIM, 'w': w, 'u': u, 'k': k, 'v': v}
    _L1_xattn_all = _L1_xattn_setup()
    _L1_xattn_in = {k: v for k, v in _L1_xattn_all.items() if k in ('w', 'u')}
    del _L1_xattn_all

    def _L1_ffn_setup():
        import jax, jax.numpy as jnp
        import numpy as np
        B, T, C = (8, 256, 256)
        E, H = (32, 64)

        def _gating(hidden_states, sim_matrix, gates):
            seq_rep = jnp.mean(hidden_states, axis=1)
            sr_n = seq_rep / jnp.linalg.norm(seq_rep, axis=-1, keepdims=True)
            sm_n = sim_matrix / jnp.linalg.norm(sim_matrix, axis=0, keepdims=True)
            affinity = sr_n @ sm_n
            logits = affinity - jax.nn.sigmoid(gates)
            gated = jax.nn.relu(logits)
            mask = (gated > 0).astype(hidden_states.dtype)
            inactive = jnp.sum(mask, axis=1) == 0
            k_fb = E // 2
            _, fb_idx = jax.lax.top_k(logits, k_fb)
            fb_mask = jnp.sum(jax.nn.one_hot(fb_idx, E, dtype=mask.dtype), axis=1)
            mask = jnp.where(inactive[:, None], jnp.maximum(mask, fb_mask), mask)
            fallback_count = jnp.sum(inactive).astype(jnp.float32)
            neg = -jnp.finfo(hidden_states.dtype).max
            routing = jax.nn.softmax(jnp.where(mask > 0, gated, neg), axis=-1)
            return (routing, mask, fallback_count)
        key = jax.random.key(seed)
        ks = jax.random.split(key, 7)
        scale = 1.0 / np.sqrt(C)
        return {'hidden_states': jax.random.normal(ks[0], (B, T, C), dtype=jnp.float32), 'sim_matrix': jax.random.normal(ks[1], (C, E), dtype=jnp.float32), 'gates': jnp.zeros((E,), dtype=jnp.float32), 'w_q': jax.random.normal(ks[2], (E, H, C), dtype=jnp.float32) * scale, 'w_k': jax.random.normal(ks[3], (E, H, C), dtype=jnp.float32) * scale, 'w_v': jax.random.normal(ks[4], (E, H, C), dtype=jnp.float32) * scale, 'o_weights': jax.random.normal(ks[5], (E, H, C), dtype=jnp.float32)}
    _L1_ffn_all = _L1_ffn_setup()
    _L1_ffn_in = {k: v for k, v in _L1_ffn_all.items() if k in ('sim_matrix', 'gates', 'w_q', 'w_k', 'w_v', 'o_weights')}
    del _L1_ffn_all
    return {'x': x, 'itok_BxS_13_99985': itok_BxS_13_99985, 'ctx_2048': ctx_2048, 'L0_attn_Wq': _L0_attn_in['Wq'], 'L0_attn_Wk': _L0_attn_in['Wk'], 'L0_attn_Wv': _L0_attn_in['Wv'], 'L0_attn_Wb': _L0_attn_in['Wb'], 'L0_attn_bb': _L0_attn_in['bb'], 'L0_attn_Wo': _L0_attn_in['Wo'], 'L0_ffn_router_weight': _L0_ffn_in['router_weight'], 'L0_ffn_router_bias': _L0_ffn_in['router_bias'], 'L0_ffn_gate_up_proj': _L0_ffn_in['gate_up_proj'], 'L0_ffn_gate_up_proj_bias': _L0_ffn_in['gate_up_proj_bias'], 'L0_ffn_down_proj': _L0_ffn_in['down_proj'], 'L0_ffn_down_proj_bias': _L0_ffn_in['down_proj_bias'], 'L1_attn_wqkv': _L1_attn_in['wqkv'], 'L1_attn_wg': _L1_attn_in['wg'], 'L1_attn_wo': _L1_attn_in['wo'], 'L1_attn_gn_weight': _L1_attn_in['gn_weight'], 'L1_attn_gn_bias': _L1_attn_in['gn_bias'], 'L1_xattn_w': _L1_xattn_in['w'], 'L1_xattn_u': _L1_xattn_in['u'], 'L1_ffn_sim_matrix': _L1_ffn_in['sim_matrix'], 'L1_ffn_gates': _L1_ffn_in['gates'], 'L1_ffn_w_q': _L1_ffn_in['w_q'], 'L1_ffn_w_k': _L1_ffn_in['w_k'], 'L1_ffn_w_v': _L1_ffn_in['w_v'], 'L1_ffn_o_weights': _L1_ffn_in['o_weights']}

def reference(x, itok_BxS_13_99985, ctx_2048, L0_attn_Wq, L0_attn_Wk, L0_attn_Wv, L0_attn_Wb, L0_attn_bb, L0_attn_Wo, L0_ffn_router_weight, L0_ffn_router_bias, L0_ffn_gate_up_proj, L0_ffn_gate_up_proj_bias, L0_ffn_down_proj, L0_ffn_down_proj_bias, L1_attn_wqkv, L1_attn_wg, L1_attn_wo, L1_attn_gn_weight, L1_attn_gn_bias, L1_xattn_w, L1_xattn_u, L1_ffn_sim_matrix, L1_ffn_gates, L1_ffn_w_q, L1_ffn_w_k, L1_ffn_w_v, L1_ffn_o_weights):
    import jax
    import jax.numpy as jnp

    def _L0_attn_ref(hidden_states, Wq, Wk, Wv, Wb, bb, Wo):
        import jax, jax.numpy as jnp
        import numpy as np
        HID = 256
        H = 16
        D = HID // H
        THETA = 10000.0

        def _rope(q, k):
            T = q.shape[1]
            half = D // 2
            inv_freq = 1.0 / THETA ** (jnp.arange(half, dtype=jnp.float32) / half)
            ang = jnp.arange(T, dtype=jnp.float32)[:, None] * inv_freq[None, :]
            cos = jnp.cos(ang)[None, :, None, :]
            sin = jnp.sin(ang)[None, :, None, :]

            def rot(x):
                x1, x2 = (x[..., :half], x[..., half:])
                return jnp.concatenate([x1 * cos - x2 * sin, x2 * cos + x1 * sin], axis=-1)
            return (rot(q), rot(k))
        B, T, _ = hidden_states.shape
        scale = 1.0 / np.sqrt(D)
        q = (hidden_states @ Wq).reshape(B, T, H, D)
        k = (hidden_states @ Wk).reshape(B, T, H, D)
        v = (hidden_states @ Wv).reshape(B, T, H, D)
        beta = hidden_states @ Wb + bb
        q, k = _rope(q, k)
        s = jnp.einsum('bihd,bjhd->bhij', k, k) * scale
        idx = jnp.arange(T)
        strict = idx[:, None] > idx[None, :]
        s = jnp.where(strict, s, -jnp.inf)
        m = jnp.max(s, axis=-1, keepdims=True)
        e = jnp.exp(s - jnp.where(jnp.isfinite(m), m, 0.0))
        e = jnp.where(strict, e, 0.0)
        denom = jnp.sum(e, axis=-1, keepdims=True)
        p = e / jnp.where(denom == 0, 1.0, denom)
        L = p * beta.transpose(0, 2, 1)[..., None]
        A = L + jnp.eye(T, dtype=L.dtype)[None, None]
        u = jax.scipy.linalg.solve_triangular(A, v.transpose(0, 2, 1, 3), lower=True)
        sc = jnp.einsum('bihd,bjhd->bhij', q, k) * scale
        causal = idx[:, None] >= idx[None, :]
        sc = jnp.where(causal, sc, -jnp.inf)
        attn = jax.nn.softmax(sc, axis=-1)
        o = jnp.einsum('bhij,bhjd->bihd', attn, u).reshape(B, T, HID)
        return o @ Wo

    def _L0_xattn_ref(hidden_states, token_ids, Wg, Wu, Wd):
        import jax, jax.numpy as jnp
        import numpy as np
        B, S, D = (4, 512, 256)
        E = 4
        F = 1024 // E
        VOCAB = 12500
        tokens_per_expert = VOCAB // E
        tid = jnp.clip(token_ids, 0, VOCAB - 1)
        expert_ids = jnp.minimum(tid // tokens_per_expert, E - 1)
        out = jnp.zeros_like(hidden_states)
        for e in range(E):
            g = jax.nn.silu(jnp.einsum('bsd,fd->bsf', hidden_states, Wg[e]))
            u = jnp.einsum('bsd,fd->bsf', hidden_states, Wu[e])
            y = jnp.einsum('bsf,df->bsd', g * u, Wd[e])
            out = jnp.where((expert_ids == e)[..., None], y, out)
        return out

    def _L0_ffn_ref(hidden_states, router_weight, router_bias, gate_up_proj, gate_up_proj_bias, down_proj, down_proj_bias):
        import jax, jax.numpy as jnp
        import numpy as np
        ALPHA = 1.702
        LIMIT = 7.0
        TOP_K = 4
        B, S, H = (1, 128, 256)
        E, D = (16, 256)
        batch, seq, hdim = hidden_states.shape
        x = hidden_states.reshape(-1, hdim)
        T = x.shape[0]
        logits = x @ router_weight.T + router_bias
        top_val, top_idx = jax.lax.top_k(logits, TOP_K)
        top_val = jax.nn.softmax(top_val, axis=-1)
        router_scores = jnp.zeros_like(logits).at[jnp.arange(T)[:, None], top_idx].set(top_val)
        gate_up = jnp.einsum('th,ehd->etd', x, gate_up_proj) + gate_up_proj_bias[:, None, :]
        gate = gate_up[..., ::2]
        up = gate_up[..., 1::2]
        gate = jnp.minimum(gate, LIMIT)
        up = jnp.clip(up, -LIMIT, LIMIT)
        glu = gate * jax.nn.sigmoid(gate * ALPHA)
        out = jnp.einsum('etd,edh->eth', (up + 1.0) * glu, down_proj) + down_proj_bias[:, None, :]
        out = out * router_scores.T[:, :, None]
        out = out.sum(axis=0)
        return out.reshape(batch, seq, hdim)

    def _L1_attn_ref(x, wqkv, wg, wo, gn_weight, gn_bias):
        import jax, jax.numpy as jnp
        import numpy as np
        HIDDEN = 256
        HEAD_DIM = 64
        N_HEADS = HIDDEN // HEAD_DIM
        ROT_DIM = HEAD_DIM // 2
        THETA = 10000.0
        SCALE_BASE = 512.0
        EPS = 1e-05
        B, S = (1, 256)

        def _rotate_half(t):
            x1 = t[..., 0::2]
            x2 = t[..., 1::2]
            return jnp.stack([-x2, x1], axis=-1).reshape(t.shape)

        def _xpos_rotary(q, k, seqlen):
            dim = ROT_DIM
            inv_freq = 1.0 / THETA ** (jnp.arange(0, dim, 2, dtype=jnp.float32) / dim)
            t = jnp.arange(seqlen, dtype=jnp.float32)
            freqs = t[:, None] * inv_freq[None, :]
            freqs = jnp.repeat(freqs, 2, axis=-1)
            base_scale = (jnp.arange(0, dim, 2, dtype=jnp.float32) + 0.4 * dim) / (1.4 * dim)
            power = (t - seqlen // 2) / SCALE_BASE
            scale = base_scale[None, :] ** power[:, None]
            scale = jnp.concatenate([scale, scale], axis=-1)
            cos, sin = (jnp.cos(freqs), jnp.sin(freqs))

            def apply(x, sc):
                xr, xp = (x[..., :dim], x[..., dim:])
                xr = xr * cos * sc + _rotate_half(xr) * sin * sc
                return jnp.concatenate([xr, xp], axis=-1)
            return (apply(q, scale), apply(k, 1.0 / scale))

        def _msr_forward(x, wqkv, wg, wo, gn_weight, gn_bias):
            b, s, _ = x.shape
            qkv = x @ wqkv.T
            qkv = qkv.reshape(b, s, N_HEADS, 3 * HEAD_DIM).transpose(0, 2, 1, 3)
            q, k, v = jnp.split(qkv, 3, axis=-1)
            q, k = _xpos_rotary(q, k, s)
            gamma = 1.0 - 2.0 ** (-5.0 - jnp.arange(N_HEADS, dtype=jnp.float32))
            idx = jnp.arange(s)
            nm = idx[:, None] - idx[None, :]
            decay = jnp.where(nm >= 0, gamma[:, None, None] ** jnp.maximum(nm, 0).astype(jnp.float32), 0.0)
            scores = jnp.einsum('bhid,bhjd->bhij', q, k) * decay
            ret = jnp.einsum('bhij,bhjd->bhid', scores, v)
            mean = ret.mean(axis=(2, 3), keepdims=True)
            var = ret.var(axis=(2, 3), keepdims=True)
            ret = (ret - mean) / jnp.sqrt(var + EPS)
            ret = ret * gn_weight[None, :, None, None] + gn_bias[None, :, None, None]
            y = ret.transpose(0, 2, 1, 3).reshape(b, s, HIDDEN)
            g = x @ wg.T
            mish = g * jnp.tanh(jax.nn.softplus(g))
            return mish * y @ wo.T
        return _msr_forward(x, wqkv, wg, wo, gn_weight, gn_bias)

    def _L1_xattn_ref(B, T, C, w, u, k, v):
        import jax, jax.numpy as jnp
        import numpy as np
        B_DIM, T_DIM, C_DIM = (16, 128, 256)

        def _wkv(w, u, k, v):
            Bn, Tn, Cn = k.shape
            NEG_INF = jnp.float32(-1e+38)

            def step(carry, kv_t):
                p, q, o = carry
                kt, vt = kv_t
                no = jnp.maximum(o, u + kt)
                A = jnp.exp(o - no)
                E = jnp.exp(u + kt - no)
                y = (A * p + E * vt) / (A * q + E)
                no2 = jnp.maximum(w + o, kt)
                A2 = jnp.exp(w + o - no2)
                E2 = jnp.exp(kt - no2)
                return ((A2 * p + E2 * vt, A2 * q + E2, no2), y)
            init = (jnp.zeros((Bn, Cn), k.dtype), jnp.zeros((Bn, Cn), k.dtype), jnp.full((Bn, Cn), NEG_INF, k.dtype))
            kT = jnp.moveaxis(k, 1, 0)
            vT = jnp.moveaxis(v, 1, 0)
            _, yT = jax.lax.scan(step, init, (kT, vT))
            return jnp.moveaxis(yT, 0, 1)
        return _wkv(w, u, k, v)

    def _L1_ffn_ref(hidden_states, sim_matrix, gates, w_q, w_k, w_v, o_weights):
        import jax, jax.numpy as jnp
        import numpy as np
        B, T, C = (8, 256, 256)
        E, H = (32, 64)

        def _gating(hidden_states, sim_matrix, gates):
            seq_rep = jnp.mean(hidden_states, axis=1)
            sr_n = seq_rep / jnp.linalg.norm(seq_rep, axis=-1, keepdims=True)
            sm_n = sim_matrix / jnp.linalg.norm(sim_matrix, axis=0, keepdims=True)
            affinity = sr_n @ sm_n
            logits = affinity - jax.nn.sigmoid(gates)
            gated = jax.nn.relu(logits)
            mask = (gated > 0).astype(hidden_states.dtype)
            inactive = jnp.sum(mask, axis=1) == 0
            k_fb = E // 2
            _, fb_idx = jax.lax.top_k(logits, k_fb)
            fb_mask = jnp.sum(jax.nn.one_hot(fb_idx, E, dtype=mask.dtype), axis=1)
            mask = jnp.where(inactive[:, None], jnp.maximum(mask, fb_mask), mask)
            fallback_count = jnp.sum(inactive).astype(jnp.float32)
            neg = -jnp.finfo(hidden_states.dtype).max
            routing = jax.nn.softmax(jnp.where(mask > 0, gated, neg), axis=-1)
            return (routing, mask, fallback_count)
        routing, mask, fallback_count = _gating(hidden_states, sim_matrix, gates)
        v_all = jnp.einsum('btc,ehc->bteh', hidden_states, w_v)
        full_expert_outputs = v_all * mask[:, None, :, None]
        combined = jnp.einsum('be,bteh->bth', routing, full_expert_outputs)
        w_o_dyn = jnp.einsum('be,ehd->bhd', routing, o_weights)
        final_output = jnp.einsum('bth,bhd->btd', combined, w_o_dyn)
        return final_output
    x = _layernorm(x + _L0_attn_ref(x, L0_attn_Wq, L0_attn_Wk, L0_attn_Wv, L0_attn_Wb, L0_attn_bb, L0_attn_Wo), axis=-1)
    x = _layernorm(x + _L0_xattn_ref(x, itok_BxS_13_99985, ctx_2048, ctx_2048, ctx_2048), axis=-1)
    x = _layernorm(x + _L0_ffn_ref(x, L0_ffn_router_weight, L0_ffn_router_bias, L0_ffn_gate_up_proj, L0_ffn_gate_up_proj_bias, L0_ffn_down_proj, L0_ffn_down_proj_bias), axis=-1)
    x = _layernorm(x + _L1_attn_ref(x, L1_attn_wqkv, L1_attn_wg, L1_attn_wo, L1_attn_gn_weight, L1_attn_gn_bias), axis=-1)
    x = _layernorm(x + _L1_xattn_ref(4, 256, 256, L1_xattn_w, L1_xattn_u, x, ctx_2048), axis=-1)
    x = _layernorm(x + _L1_ffn_ref(x, L1_ffn_sim_matrix, L1_ffn_gates, L1_ffn_w_q, L1_ffn_w_k, L1_ffn_w_v, L1_ffn_o_weights), axis=-1)
    return x

_drawn_inputs = setup_inputs


def setup_inputs(seed=0):
    import zlib

    import numpy as np

    out = dict(_drawn_inputs(seed))
    spreads = {'L0_attn_bb': (0.0, 0.1),
     'L1_attn_gn_weight': (1.0, 0.2),
     'L1_attn_gn_bias': (0.0, 0.1),
     'L1_ffn_gates': (0.0, 0.1)}
    factors = {}
    for name, (base, spread) in spreads.items():
        noise = np.random.default_rng([zlib.crc32(name.encode()), seed]).standard_normal(out[name].shape)
        drawn = base * np.exp(spread * noise) if base else spread * noise
        out[name] = jnp.asarray(drawn.astype(out[name].dtype))
    for name, factor in factors.items():
        out[name] = (out[name] * factor).astype(out[name].dtype)
    return out
```

```python
from contextlib import ExitStack

import numpy as np

import concourse.bass as bass
from concourse import mybir
from concourse.alu_op_type import AluOpType as ALU

ACT = mybir.ActivationFunctionType
F32 = mybir.dt.float32
BF16 = mybir.dt.bfloat16
I32 = mybir.dt.int32
AX = mybir.AxisListType.X

P = 128
NB, T, C = 4, 256, 256
TB = T // P
CC = C // P
H, D = 16, 16
NP = H // 2
Q = 32
NQ = P // Q
LN_EPS = 1e-5
NEG = -1.0e30
FLOOR = -1.0e28
SLOTS = (0, 1, 4), (2, 3), (5,)
SLOTS_B = (0, 2, 5), (1, 3), (4,)


class Link:

    def __init__(self, eng, sem, per, it):
        self.eng, self.sem, self.per, self.it, self.n = eng, sem, per, it, 0

    def __call__(self, ins):
        self.n += 1
        ins.then_inc(self.sem, 1)
        self.eng.wait_ge(self.sem, self.it * self.per + self.n)

    def close(self):
        assert self.n == self.per, ("links", self.n, self.per)


def apart(eng, passed):
    eng.sem_inc(passed, 1)


def constants():
    f32 = np.float32
    half = D // 2
    inv = (f32(1.0) / np.power(f32(10000.0), np.arange(half, dtype=f32) / f32(half), dtype=f32)).astype(f32)
    ang = (np.arange(T, dtype=f32)[:, None] * inv[None, :]).astype(f32)
    cos, sin = np.cos(ang).astype(f32), np.sin(ang).astype(f32)
    rope = np.concatenate([cos, cos, -sin, sin], 1).reshape(TB, P, 4 * half).transpose(1, 0, 2)
    out = {"ident": np.eye(P, dtype=f32), "rope": np.ascontiguousarray(rope)}
    i, j = np.arange(P)[:, None], np.arange(P)[None, :]
    masks = np.zeros((P, 4, 2, P), f32)
    for n, ok in enumerate((j < i, j <= i, i < j, i <= j)):
        masks[:, n] = np.where(ok, 0.0, NEG)[:, None, :]
    out["masks"] = masks.reshape(P, -1)
    resets = np.ones((P, NB * TB, 16), f32)
    resets[:, :, 0] = 0.0
    out["resets"] = resets.reshape(P, -1)
    dim, heads = 32, 4
    inv = (f32(1.0) / np.power(f32(10000.0), np.arange(0, dim, 2, dtype=f32) / f32(dim), dtype=f32)).astype(f32)
    t = np.arange(T, dtype=f32)
    ang = np.repeat((t[:, None] * inv[None, :]).astype(f32), 2, axis=-1)
    base = ((np.arange(0, dim, 2, dtype=f32) + f32(0.4 * dim)) / f32(1.4 * dim)).astype(f32)
    scale = np.power(base[None, :], ((t - T // 2) / f32(512.0))[:, None], dtype=f32)
    scale = np.concatenate([scale, scale], axis=-1)
    sign = np.where(np.arange(dim) % 2, f32(1.0), f32(-1.0))
    xpos = np.stack([np.stack([np.cos(ang) * sc, np.sin(ang) * sc * sign], 1) for sc in (scale, f32(1.0) / scale)], 1)
    out["xpos"] = np.ascontiguousarray(xpos.astype(f32).reshape(TB, P, 2, 2, dim).transpose(1, 0, 2, 3, 4))
    gamma = (1.0 - 2.0 ** (-5.0 - np.arange(heads))).astype(f32)
    q, k = np.arange(T), np.arange(T)[:, None]
    dist = np.maximum(q - k, 0).astype(f32)
    full = np.stack([np.where(q >= k, np.power(gm, dist, dtype=f32), f32(0.0)) for gm in gamma], 1).astype(f32)
    out["decay"] = np.ascontiguousarray(np.concatenate([full[:P], full[P:, :, P:]], axis=-1))
    out["average"] = np.kron(np.eye(2, dtype=f32), np.full((64, 64), 1.0 / 64, f32))
    p2 = np.arange(P)
    out["halves"] = (np.arange(32)[:, None] % 2 == p2[None, :] // 64).astype(f32)
    out["fold"] = (p2[:, None] % 64 == np.arange(64)[None, :]).astype(f32)
    out["pick"] = (np.arange(32)[:, None] // 2 == np.arange(16)[None, :]).astype(f32)
    out["eye32"] = np.tile(np.eye(Q, dtype=f32).reshape(1, -1), (P, 1))
    return out


def build(nc, io, consts, out, debug=None):
    with ExitStack() as ctx:
        def sb(name, shape, dt=F32):
            return ctx.enter_context(nc.sbuf_tensor(name, shape, dt))

        ps = ctx.enter_context(nc.psum_tensor("ps", [P, 8 * 512], F32))

        def bank(n, k=1):
            return ps[:, 512 * n:512 * (n + k)]

        g = {
            "ident": sb("ident", [P, P]), "neg_half": sb("neg_half", [P, 8]),
            "xn": sb("xn", [P, NB, TB, C]), "xt": sb("xt", [P, CC, NB * T]),
            "ct": sb("ct", [P, NB, CC, T]),
        }
        g["passed"] = ctx.enter_context(nc.semaphore("passed"))
        g["ready"] = ctx.enter_context(nc.semaphore("ready"))
        layers = ((layer0_attention, "attn"), (layer0_experts_by_token, "xattn"), (layer0_experts_by_router, "ffn"),
                  (layer1_retention, "attn1"), (layer1_recurrence, "wkv"), (layer1_mixed_experts, "all"))
        for layer, name in layers:
            layer(nc, io, consts, bank, g, out)
            if debug == name and name != "all":
                finish = ctx.enter_context(nc.semaphore("finish"))
                with nc.Block() as block:
                    @block.sync
                    def _(sp):
                        sp.dma_start(out.rearrange("b (t p) c -> p b t c", p=P), g["xn"][:]).then_inc(finish, 16)
                        sp.wait_ge(finish, 16)
                return


def tools(nc, ctx, tag):
    def sb(name, shape, dt=F32):
        return ctx.enter_context(nc.sbuf_tensor(f"{tag}_{name}", shape, dt))

    def sem(name):
        return ctx.enter_context(nc.semaphore(f"{tag}_{name}"))

    def dram(name, shape, dt=F32):
        return nc.dram_tensor(f"{tag}_{name}", shape, dt, kind="Internal").ap()

    return sb, sem, dram


def layer0_attention(nc, io, consts, bank, g, out):
    with ExitStack() as ctx:
        layer0_attention_in(nc, io, consts, bank, g, *tools(nc, ctx, "l0a"))


def layer0_attention_in(nc, io, consts, bank, g, sb, sem, dram):
    ident, xn, xt, neg_half = (g[n] for n in ("ident", "xn", "xt", "neg_half"))
    identb, ready, passed = sb("identb", [P, P], BF16), g["ready"], g["passed"]
    rope = sb("rope", [P, TB, 2 * D])
    maskf = sb("maskf", [P, 8 * P])
    masks = sb("masks", [P, 4, 2 * P], BF16)
    eye32 = sb("eye32", [P, Q * Q])
    wqk = sb("wqk", [P, CC, 2 * C])
    wvb = sb("wvb", [P, CC, C + H])
    wo = sb("wo", [P, CC, C])
    bb = sb("bb", [P, H])
    x_in = sb("x_in", [P, TB, C])
    xs_t = sb("xs_t", [P, CC, T])
    v = sb("v", [P, TB, H, D])
    beta = sb("beta", [P, TB, H])
    roped = sb("roped", [P, TB, 2 * C])
    ropet = sb("ropet", [P, TB, 2 * C])
    left = sb("left", [P, TB, 2 * H, 6, D], BF16)
    right = sb("right", [P, TB, H, 6, D], BF16)
    left_t = sb("left_t", [99, 2, H, T], BF16)
    right_t = sb("right_t", [99, H, T], BF16)
    rowmax = sb("rowmax", [P, TB, 2, H])
    negmax = sb("negmax", [P, 2, H])
    nmf = sb("nmf", [P, TB, 2, H])
    nmr = sb("nmr", [P, TB, 2, H])
    nm3 = sb("nm3", [P, TB, 2, 3, H], BF16)
    nm_t = sb("nm_t", [96, T], BF16)
    e_nat = sb("e_nat", [P, H, 3 * P])
    e_t = sb("e_t", [P, 2, H, 3 * P])
    den = sb("den", [P, 2, H])
    gain = sb("gain", [P, 2, H])
    gtmp = sb("gtmp", [P, 2, H])
    diag = sb("diag", [P, 2, H, Q])
    low = sb("low", [P, Q, Q])
    inv = sb("inv", [P, Q, Q])
    invt = sb("invt", [P, Q * Q // 4])
    inv_t = sb("inv_t", [P, 2, H, Q])
    u1 = sb("u1", [P, TB, H, 2 * D])
    rhs = sb("rhs", [P, H, D])
    o_t = sb("o_t", [P, 4, T])
    rden = sb("rden", [P, TB, H])
    o_nat = sb("o_nat", [P, TB, C])
    on_t = sb("on_t", [P, CC, T])
    y = sb("y", [P, TB, C])
    ys = sb("ys", [P, TB, C])
    stats = sb("stats", [P, TB, 6])
    mv = sb("mv", [P, TB, 2])
    rstd = sb("rstd", [P, TB])
    low_d = dram("low_d", [NQ, Q, 2 * H, Q])
    inv_d = dram("inv_d", [NQ, 2 * H, Q, Q])

    consts_in, x_loaded, x_free = sem("consts_in"), sem("x_loaded"), sem("x_free")
    xt_psum, xt_sbuf = sem("xt_psum"), sem("xt_sbuf")
    qkv_psum, v_sbuf, part_s = sem("qkv_psum"), sem("v_sbuf"), sem("part_s")
    stack_s = sem("stack_s")
    turned, turned_act, turned_dve = sem("turned"), sem("turned_act"), sem("turned_dve")
    scores, neg_s, e_nat_s, max_q = sem("scores"), sem("neg_s"), sem("e_nat_s"), sem("max_q")
    nm3_s, nmt_psum, nmt_sbuf, nm_rows = sem("nm3_s"), sem("nmt_psum"), sem("nmt_sbuf"), sem("nm_rows")
    e_t_s = sem("e_t_s")
    diag_s, low_out, low_in, inv_s, inv_out, inv_in = (sem(n) for n in (
        "diag_s", "low_out", "low_in", "inv_s", "inv_out", "inv_in"))
    res_psum, rhs_s, sol_psum, sol_s = sem("res_psum"), sem("rhs_s"), sem("sol_psum"), sem("sol_s")
    o_psum, o_sbuf, ot_psum, onat_s, on_psum, on_sbuf, wo_psum = (sem(n) for n in (
        "o_psum", "o_sbuf", "ot_psum", "onat_s", "on_psum", "on_sbuf", "wo_psum"))
    var_s, rstd_s = sem("var_s"), sem("rstd_s")
    ys_s, yst_psum, dve_link, setup_s = (sem(n) for n in ("ys_s", "yst_psum", "dve_link", "setup_s"))

    NCONST = 12
    TURNS = 3 * TB * 2
    TURN_BANKS = (5, 6, 7, 0)
    SLOT = (1, 3, 5)
    NG = 2
    HG = H // NG
    RES_BANK, SOL_BANK = (0, 7), (1, 2)
    LINKS = 103

    x_dram = io["x"].rearrange("b (t p) c -> b p t c", p=P)

    with nc.Block() as block:
        @block.sync
        def _(sp):
            sp.dma_start(ident[:], consts["ident"]).then_inc(consts_in, 16)
            sp.dma_start(rope[:], consts["rope"]).then_inc(consts_in, 16)
            sp.dma_start(maskf[:], consts["masks"]).then_inc(consts_in, 16)
            sp.dma_start(eye32[:], consts["eye32"]).then_inc(consts_in, 16)
            for n, name in enumerate(("L0_attn_Wq", "L0_attn_Wk")):
                sp.dma_start(wqk[:, :, n * C:(n + 1) * C], io[name].rearrange("(k p) n -> p k n", p=P)).then_inc(consts_in, 16)
            sp.dma_start(wvb[:, :, 0:C], io["L0_attn_Wv"].rearrange("(k p) n -> p k n", p=P)).then_inc(consts_in, 16)
            sp.dma_start(wvb[:, :, C:C + H], io["L0_attn_Wb"].rearrange("(k p) n -> p k n", p=P)).then_inc(consts_in, 16)
            sp.dma_start(wo[:], io["L0_attn_Wo"].rearrange("(k p) n -> p k n", p=P)).then_inc(consts_in, 16)
            sp.dma_start(bb[:], io["L0_attn_bb"].rearrange("(a h) -> a h", a=1).broadcast_to([P, H])).then_inc(consts_in, 16)
            with sp.Fori(0, NB) as b:
                sp.wait_ge(x_free, b + 1)
                sp.dma_start(x_in[:], x_dram[b]).then_inc(x_loaded, 16)
                sp.wait_ge(nmt_sbuf, b + 1)
                for k in range(2):
                    sp.dma_start(left_t[96:99, k, :, :], nm_t[48 * k:48 * k + 48, :]).then_inc(nm_rows, 16)
                sp.wait_ge(diag_s, b + 1)
                for q in range(NQ):
                    sp.dma_start(low_d[q], diag[Q * q:Q * q + Q].rearrange("r s h j -> r (s h) j")).then_inc(low_out, 16)
                sp.wait_ge(low_out, b * 64 + 64)
                for q in range(NQ):
                    sp.dma_start(low[Q * q:Q * q + Q], low_d[q].rearrange("r g j -> g r j")).then_inc(low_in, 16)
                sp.wait_ge(inv_s, b + 1)
                for q in range(NQ):
                    sp.dma_start(inv_d[q], inv[Q * q:Q * q + Q]).then_inc(inv_out, 16)
                sp.wait_ge(inv_out, b * 64 + 64)
                for q in range(NQ):
                    sp.dma_start(inv_t[Q * q:Q * q + Q].rearrange("k s h r -> k (s h) r"),
                                 inv_d[q].rearrange("g k r -> k g r")).then_inc(inv_in, 16)

        @block.scalar
        def _(act):
            act.wait_ge(consts_in, 16 * 10)
            nc.scalar.copy(masks[:].rearrange("p a b -> p (a b)"), maskf[:]).then_inc(setup_s, 1)
            nc.scalar.copy(identb[:], ident[:]).then_inc(setup_s, 1)
            with act.Fori(0, NB) as b:
                act.wait_ge(xt_psum, b + 1)
                nc.scalar.copy(xs_t[:].rearrange("p a b -> p (a b)"), bank(0)).then_inc(xt_sbuf, 1)
                act.wait_ge(qkv_psum, b * 4 + 4)
                for t in range(TB):
                    cp = nc.scalar.copy(v[:, t].rearrange("p h d -> p (h d)"), bank(3 + t)[:, 0:C])
                cp.then_inc(v_sbuf, 1)
                for n, part in enumerate((SLOTS_B, SLOTS)):
                    for k in range(3):
                        act.wait_ge(part_s, b * 3 + k + 1)
                        src = left[:, :, :, SLOTS[k][0], :]
                        if n == 0:
                            for s in SLOTS_B[k]:
                                for t in range(TB):
                                    cp = nc.scalar.copy(right[:, t, :, s, :], src[:, t, H:2 * H, :])
                        else:
                            for s in SLOTS[k][1:]:
                                for t in range(TB):
                                    cp = nc.scalar.copy(left[:, t, :, s, :], src[:, t, :, :])
                cp.then_inc(stack_s, 1)
                for g in range(0, TURNS, 2):
                    act.wait_ge(turned, b * TURNS + g + 1)
                    turn_out(nc.scalar.copy, g, left_t, right_t, bank, TURN_BANKS).then_inc(turned_act, 1)
                for p in range(NP):
                    act.wait_ge(neg_s, b * NP + p + 1)
                    for h in (2 * p, 2 * p + 1):
                        sc = bank(SLOT[p % 3] + h % 2)
                        for s, (lo, hi) in enumerate(((0, 2 * P), (2 * P, 3 * P))):
                            ex = nc.scalar.activation(e_nat[:, h, lo:hi], sc[:, lo:hi], ACT.Exp, scale=0.25,
                                                      bias=negmax[:, s, h:h + 1], accum_out=den[:, s, h:h + 1])
                    ex.then_inc(e_nat_s, 1)
                act.wait_ge(nmt_psum, b + 1)
                nc.scalar.copy(nm_t[:], bank(7).bitcast(BF16)[0:96, 0:T]).then_inc(nmt_sbuf, 1)
                for n in range(2 * NP, 4 * NP):
                    k, p = divmod(n - 2 * NP, NP)
                    act.wait_ge(scores, b * 4 * NP + n + 1)
                    src = bank(SLOT[n % 3], 2).rearrange("p (h c) -> p h c", h=2)[:, :, 0:3 * P]
                    nc.scalar.activation(e_t[:, k, 2 * p:2 * p + 2, :], src, ACT.Exp, scale=0.25).then_inc(e_t_s, 1)
                for c in range(TB * NQ):
                    t, q = divmod(c, NQ)
                    for gr in range(NG):
                        act.wait_ge(sol_psum, b * 16 + c * NG + gr + 1)
                        nc.scalar.copy(u1[Q * q:Q * q + Q, t, HG * gr:HG * gr + HG, 0:D],
                                       bank(SOL_BANK[gr])[Q * q:Q * q + Q, 0:HG * D].rearrange("p (h d) -> p h d", d=D)).then_inc(sol_s, 1)
                act.wait_ge(o_psum, b + 1)
                nc.scalar.copy(o_t[:].rearrange("p a b -> p (a b)"), bank(3, 2)).then_inc(o_sbuf, 1)
                act.wait_ge(on_psum, b + 1)
                nc.scalar.copy(on_t[:].rearrange("p a b -> p (a b)"), bank(0)).then_inc(on_sbuf, 1)
                act.wait_ge(yst_psum, b + 1)
                apart(act, passed)
                nc.scalar.copy(xt[:, :, bass.ds(b * T, T)], bank(7).rearrange("p (c t) -> p c t", c=CC))

        @block.vector
        def _(dve):
            nc.vector.memset(right_t[96:99], 1.0).then_inc(setup_s, 1)
            nc.vector.memset(u1[:, :, :, D:2 * D], 1.0).then_inc(setup_s, 1)
            nc.vector.memset(neg_half[:], -0.5).then_inc(ready, 1)
            dve.sem_inc(x_free, 1)
            dve.wait_ge(consts_in, 16 * 10)
            with dve.Fori(0, NB) as b:
                link = Link(dve, dve_link, LINKS, b)
                for t in range(TB):
                    dve.wait_ge(qkv_psum, b * 4 + 2 * t + 1)
                    src = bank(1 + t).rearrange("p (h d) -> p h d", d=D)
                    dst = roped[:, t].rearrange("p (h d) -> p h d", d=D)
                    tmp = ropet[:, t].rearrange("p (h d) -> p h d", d=D)
                    tab = rope[:, t:t + 1, :]
                    nc.vector.tensor_tensor(dst, src, tab[:, :, 0:D].broadcast_to([P, 2 * H, D]), ALU.mult)
                    for a, z in ((0, D // 2), (D // 2, 0)):
                        mul = nc.vector.tensor_tensor(tmp[:, :, a:a + D // 2], src[:, :, z:z + D // 2],
                                                      tab[:, :, D + a:D + a + D // 2].broadcast_to([P, 2 * H, D // 2]), ALU.mult)
                    link(mul)
                    link(nc.vector.tensor_tensor(dst, dst, tmp, ALU.add))
                dve.wait_ge(v_sbuf, b + 1)
                for t in range(TB):
                    add = nc.vector.tensor_tensor(beta[:, 1 - t, :], bank(3 + t)[:, C:C + H], bb[:], ALU.add)
                link(add)
                rq = roped[:].rearrange("p t (h d) -> p (t h) d", d=D)
                rr = ropet[:].rearrange("p t (h d) -> p (t h) d", d=D)
                lf = left[:].rearrange("p t h s d -> p (t h) s d")
                nc.vector.tensor_copy(lf[:, :, 0, :], rq).then_inc(part_s, 1)
                dve.wait_ge(part_s, b * 3 + 1)
                link(nc.vector.tensor_tensor(rr, rq, lf[:, :, 0, :], ALU.subtract))
                nc.vector.tensor_copy(lf[:, :, 2, :], rr).then_inc(part_s, 1)
                dve.wait_ge(part_s, b * 3 + 2)
                nc.vector.tensor_tensor(lf[:, :, 5, :], rr, lf[:, :, 2, :], ALU.subtract).then_inc(part_s, 1)
                for g in range(1, TURNS, 2):
                    dve.wait_ge(turned, b * TURNS + g + 1)
                    turn_out(nc.vector.tensor_copy, g, left_t, right_t, bank, TURN_BANKS).then_inc(turned_dve, 1)
                for n in range(2 * NP):
                    k, p = divmod(n, NP)
                    dve.wait_ge(scores, b * 4 * NP + n + 1)
                    sc = bank(SLOT[n % 3], 2).rearrange("p (h c) -> p h c", h=2)
                    nc.vector.tensor_reduce(rowmax[:, 0, k, 2 * p:2 * p + 2], sc[:, :, 0:2 * P], AX, ALU.max)
                    rd = nc.vector.tensor_reduce(rowmax[:, 1, k, 2 * p:2 * p + 2], sc[:, :, 2 * P:3 * P], AX, ALU.max)
                    if k == 1:
                        rd.then_inc(max_q, 1)
                    else:
                        link(rd)
                        nc.vector.tensor_scalar(negmax[:, :, 2 * p:2 * p + 2], rowmax[:, :, 0, 2 * p:2 * p + 2], FLOOR, -0.25,
                                                ALU.max, ALU.mult).then_inc(neg_s, 1)
                dve.wait_ge(max_q, b * NP + NP)
                for s in range(2):
                    ts = nc.vector.tensor_scalar(nmf[:, 1 - s], rowmax[:, s], FLOOR, -1.0, ALU.max, ALU.mult)
                link(ts)
                link(nc.vector.tensor_copy(nm3[:, :, :, 0, :], nmf[:]))
                link(nc.vector.tensor_tensor(nmr[:], nmf[:], nm3[:, :, :, 0, :], ALU.subtract))
                link(nc.vector.tensor_copy(nm3[:, :, :, 1, :], nmr[:]))
                nc.vector.tensor_tensor(nm3[:, :, :, 2, :], nmr[:], nm3[:, :, :, 1, :], ALU.subtract).then_inc(nm3_s, 1)
                dve.wait_ge(e_nat_s, b * NP + NP)
                link(nc.vector.tensor_scalar(gtmp[:], den[:], 0.0, None, ALU.is_equal))
                link(nc.vector.tensor_tensor(gtmp[:], gtmp[:], den[:], ALU.add))
                link(nc.vector.reciprocal(gain[:], gtmp[:]))
                link(nc.vector.scalar_tensor_tensor(out=gain[:], in0=gain[:], scalar=-1.0, in1=beta[:], op0=ALU.mult, op1=ALU.mult))
                for q in range(NQ):
                    rows = slice(Q * q, Q * q + Q)
                    src = e_nat[rows, :, P:3 * P].rearrange("p h (s c) -> p s h c", s=2)[:, :, :, Q * q:Q * q + Q]
                    for s in range(2):
                        mul = nc.vector.tensor_tensor(diag[rows, s], src[:, s],
                                                      gain[rows, s, :].rearrange("p (h a) -> p h a", a=1).broadcast_to([Q, H, Q]), ALU.mult)
                mul.then_inc(diag_s, 1)
                link(nc.vector.tensor_copy(inv[:].rearrange("p k r -> p (k r)"), eye32[:]))
                dve.wait_ge(low_in, b * 64 + 64)
                for j in range(Q - 1):
                    k, r = j + 1, Q - 1 - j
                    tmp = invt[:, 0:k * r].rearrange("p (k r) -> p k r", k=k)
                    col = low[:, j + 1:Q, j:j + 1].rearrange("p r a -> p a r").broadcast_to([P, k, r])
                    row = inv[:, 0:k, j:j + 1].broadcast_to([P, k, r])
                    link(nc.vector.tensor_tensor(tmp, row, col, ALU.mult))
                    add = nc.vector.tensor_tensor(inv[:, 0:k, j + 1:Q], inv[:, 0:k, j + 1:Q], tmp, ALU.add)
                    if j < Q - 2:
                        link(add)
                add.then_inc(inv_s, 1)
                for c in range(TB * NQ):
                    t, q = divmod(c, NQ)
                    rows = slice(Q * q, Q * q + Q)
                    if c == 0:
                        continue
                    for gr in range(NG):
                        hs = slice(HG * gr, HG * gr + HG)
                        dve.wait_ge(res_psum, b * 14 + (c - 1) * NG + gr + 1)
                        src = bank(RES_BANK[gr])[rows, 0:HG * D].rearrange("p (h d) -> p h d", d=D)
                        gn = gain[rows, 1 - t, hs].rearrange("p (h a) -> p h a", a=1).broadcast_to([Q, HG, D])
                        link(nc.vector.tensor_tensor(rhs[rows, hs, :], src, gn, ALU.mult))
                        nc.vector.tensor_tensor(rhs[rows, hs, :], rhs[rows, hs, :], v[rows, t, hs, :], ALU.add).then_inc(rhs_s, 1)
                dve.wait_ge(ot_psum, b + 1)
                ot = bank(5, 2).rearrange("p (t h d) -> p t h d", t=TB, h=H)
                link(nc.vector.reciprocal(rden[:], ot[:, :, :, D]))
                nc.vector.tensor_tensor(o_nat[:].rearrange("p t (h d) -> p t h d", d=D), ot[:, :, :, 0:D],
                                        rden[:].rearrange("p t (h a) -> p t h a", a=1).broadcast_to([P, TB, H, D]), ALU.mult).then_inc(onat_s, 1)
                dve.wait_ge(wo_psum, b + 1)
                link(nc.vector.tensor_tensor(y[:].rearrange("p t c -> p (t c)"), bank(1), x_in[:].rearrange("p t c -> p (t c)"), ALU.add))
                dve.sem_inc(x_free, 1)
                layer_norm(nc, dve, link, y, stats, mv, rstd, ys, xn, b, ys_s, var_s, rstd_s, passed)
                link.close()

        @block.gpsimd
        def _(pool):
            pool.wait_ge(ready, 1)
            root_loop(nc, pool, neg_half, rstd, var_s, rstd_s)

        @block.tensor
        def _(pe):
            pe.wait_ge(consts_in, 16 * 10)
            pe.wait_ge(setup_s, 4)
            pe.wait_ge(ready, 1)
            with pe.Fori(0, NB) as b:
                pe.wait_ge(x_loaded, b * 16 + 16)
                for c in range(CC):
                    for t in range(TB):
                        mm = nc.tensor.transpose(bank(0)[:, c * T + t * P:c * T + t * P + P], x_in[:, t, c * P:c * P + P], ident[:])
                mm.then_inc(xt_psum, 1)
                pe.wait_ge(xt_sbuf, b + 1)
                for t in range(TB):
                    for w, dst in ((wqk, bank(1 + t)), (wvb, bank(3 + t)[:, 0:C + H])):
                        for c in range(CC):
                            mm = nc.tensor.matmul(dst, xs_t[:, c, t * P:t * P + P], w[:, c, :], start=(c == 0), stop=(c == CC - 1))
                        mm.then_inc(qkv_psum, 1)
                pe.wait_ge(stack_s, b + 1)
                for g in range(TURNS):
                    a, t, hh = g // 4, g // 2 % 2, g % 2
                    if g >= 4:
                        done, n = (turned_act, turned_dve)[g % 2], (g - 4) // 2 + 1
                        pe.wait_ge(done, b * (TURNS // 2) + n)
                    dst = bank(TURN_BANKS[g % 4]).bitcast(BF16)
                    for i in range(8):
                        h = 8 * hh + i
                        src = right[:, t, h] if a == 2 else left[:, t, (H if a == 0 else 0) + h]
                        mm = nc.tensor.transpose(dst[0:96, i * P:i * P + P], src.rearrange("p s d -> p (s d)"), identb[:])
                    mm.then_inc(turned, 1)
                pe.wait_ge(turned_act, b * (TURNS // 2) + TURNS // 2)
                pe.wait_ge(turned_dve, b * (TURNS // 2) + TURNS // 2)

                def free_slot(n):
                    if n < NP:
                        pe.wait_ge(e_nat_s, b * NP + n + 1)
                    elif n < 2 * NP:
                        pe.wait_ge(max_q, b * NP + n - NP + 1)
                    else:
                        pe.wait_ge(e_t_s, b * 2 * NP + n - 2 * NP + 1)

                for n in range(2 * NP):
                    k, p = divmod(n, NP)
                    if n >= 3:
                        free_slot(n - 3)
                    for h in (2 * p, 2 * p + 1):
                        dst = bank(SLOT[n % 3] + h % 2)
                        nc.tensor.matmul(dst[:, P:3 * P], identb[:], masks[:, k, :], start=True, stop=False, skip_group_check=True)
                        nc.tensor.matmul(dst[:, 0:2 * P], left_t[0:96, k, h, P:T], right_t[0:96, h, :], start=False, stop=True,
                                         skip_group_check=True)
                        mm = nc.tensor.matmul(dst[:, 2 * P:3 * P], left_t[0:96, k, h, 0:P], right_t[0:96, h, 0:P], start=False,
                                              stop=True, skip_group_check=True)
                    mm.then_inc(scores, 1)
                pe.wait_ge(nm3_s, b + 1)
                for t in range(TB):
                    mm = nc.tensor.transpose(bank(7).bitcast(BF16)[0:96, t * P:t * P + P], nm3[:, t].rearrange("p k a h -> p (k a h)"), identb[:])
                mm.then_inc(nmt_psum, 1)
                pe.wait_ge(nm_rows, b * 32 + 32)
                for n in range(2 * NP, 4 * NP):
                    k, p = divmod(n - 2 * NP, NP)
                    free_slot(n - 3)
                    for h in (2 * p, 2 * p + 1):
                        dst = bank(SLOT[n % 3] + h % 2)
                        two = dst[:, 0:4 * P].rearrange("p (a c) -> p a c", a=2)[:, :, 0:P]
                        nc.tensor.matmul(two, identb[:], masks[:, 2 + k, :].rearrange("p (a c) -> p a c", a=2), start=True, stop=False,
                                         skip_group_check=True)
                        nc.tensor.matmul(dst[:, 0:2 * P], right_t[:, h, 0:P], left_t[:, k, h, :], start=False, stop=True, skip_group_check=True)
                        mm = nc.tensor.matmul(dst[:, 2 * P:3 * P], right_t[:, h, P:T], left_t[:, k, h, P:T], start=False, stop=True,
                                              skip_group_check=True)
                    mm.then_inc(scores, 1)
                pe.wait_ge(inv_in, b * 64 + 64)
                pe.wait_ge(e_t_s, b * 2 * NP + 2 * NP)
                apart(pe, passed)
                for c in range(TB * NQ):
                    t, q = divmod(c, NQ)
                    rows = slice(Q * q, Q * q + Q)
                    if c:
                        for gr in range(NG):
                            pe.wait_ge(sol_s, b * 16 + (c - 1) * NG + gr + 1)
                            apart(pe, passed)
                            for i in range(HG):
                                h = HG * gr + i
                                dst = bank(RES_BANK[gr])[rows, i * D:i * D + D]
                                if t:
                                    mm = nc.tensor.matmul(dst, e_t[:, 0, h, P + Q * q:P + Q * q + Q], u1[:, 0, h, 0:D], start=True,
                                                          stop=(q == 0), tile_position=(0, Q * q))
                                if q:
                                    lo = 2 * P * t + Q * q
                                    mm = nc.tensor.matmul(dst, e_t[0:Q * q, 0, h, lo:lo + Q], u1[0:Q * q, t, h, 0:D], start=(t == 0),
                                                          stop=True, tile_position=(0, Q * q))
                            mm.then_inc(res_psum, 1)
                    for gr in range(NG):
                        if c:
                            pe.wait_ge(rhs_s, b * 14 + (c - 1) * NG + gr + 1)
                            apart(pe, passed)
                        for i in range(HG):
                            h = HG * gr + i
                            src = rhs[rows, h, :] if c else v[rows, 0, h, :]
                            mm = nc.tensor.matmul(bank(SOL_BANK[gr])[rows, i * D:i * D + D], inv_t[rows, 1 - t, h, :], src, start=True,
                                                  stop=True, tile_position=(Q * q, Q * q))
                        mm.then_inc(sol_psum, 1)
                pe.wait_ge(sol_s, b * 16 + 16)
                for h in range(H):
                    dst = bank(3, 2)[Q * (h % 4):Q * (h % 4) + Q, (h // 4) * T:(h // 4) * T + T]
                    nc.tensor.matmul(dst, u1[:, 0, h, :], e_t[:, 1, h, 0:T], start=True, stop=False, tile_position=(0, Q * (h % 4)))
                    mm = nc.tensor.matmul(dst[:, P:T], u1[:, 1, h, :], e_t[:, 1, h, T:T + P], start=False, stop=True,
                                          tile_position=(0, Q * (h % 4)))
                mm.then_inc(o_psum, 1)
                pe.wait_ge(o_sbuf, b + 1)
                for t in range(TB):
                    for g in range(4):
                        mm = nc.tensor.transpose(bank(5 + t)[:, g * P:g * P + P], o_t[:, g, t * P:t * P + P], ident[:])
                mm.then_inc(ot_psum, 1)
                pe.wait_ge(onat_s, b + 1)
                for c in range(CC):
                    for t in range(TB):
                        mm = nc.tensor.transpose(bank(0)[:, c * T + t * P:c * T + t * P + P], o_nat[:, t, c * P:c * P + P], ident[:])
                mm.then_inc(on_psum, 1)
                pe.wait_ge(on_sbuf, b + 1)
                for t in range(TB):
                    for c in range(CC):
                        mm = nc.tensor.matmul(bank(1)[:, t * C:t * C + C], on_t[:, c, t * P:t * P + P], wo[:, c, :], start=(c == 0),
                                              stop=(c == CC - 1))
                mm.then_inc(wo_psum, 1)
                pe.wait_ge(ys_s, b + 1)
                for c in range(CC):
                    for t in range(TB):
                        mm = nc.tensor.transpose(bank(7)[:, c * T + t * P:c * T + t * P + P], ys[:, t, c * P:c * P + P], ident[:])
                mm.then_inc(yst_psum, 1)


def turn_out(copy, g, left_t, right_t, bank, banks):
    a, t, hh = g // 4, g // 2 % 2, g % 2
    src = bank(banks[g % 4]).bitcast(BF16)[0:96, :].rearrange("p (h t) -> p h t", h=8)
    dst = right_t[0:96] if a == 2 else left_t[0:96, a]
    return copy(dst[:, 8 * hh:8 * hh + 8, t * P:t * P + P], src)


def root_loop(nc, pool, neg_half, rstd, var_s, rstd_s):
    with pool.Fori(0, NB) as b:
        pool.wait_ge(var_s, b + 1)
        nc.gpsimd.tensor_tensor(rstd[:], rstd[:], neg_half[:, 0:TB], ALU.pow).then_inc(rstd_s, 1)


def layer_norm(nc, dve, link, y, stats, mv, rstd, ys, xn, b, ys_s, var_s, rstd_s, passed):
    for t in range(TB):
        st = nc.vector.bn_stats(stats[:, t, :], y[:, t, :])
    link(st)
    apart(dve, passed)
    for t in range(TB):
        ag = nc.vector.bn_aggr(mv[:, t, :], stats[:, t, :])
    link(ag)
    nc.vector.tensor_scalar(rstd[:], mv[:, :, 1], LN_EPS, None, ALU.add).then_inc(var_s, 1)
    dve.wait_ge(rstd_s, b + 1)
    for t in range(TB):
        sc = nc.vector.tensor_scalar(ys[:, t, :], y[:, t, :], mv[:, t, 0:1], rstd[:, t:t + 1], ALU.subtract, ALU.mult)
    sc.then_inc(ys_s, 1)
    dve.wait_ge(ys_s, b + 1)
    apart(dve, passed)
    link(nc.vector.tensor_copy(xn[:, b], ys[:]))


class Norm:

    def __init__(self, nc, g, sb, sem, out_bank):
        self.nc, self.bank = nc, out_bank
        self.xn, self.xt, self.ident, self.neg_half, self.passed = (g[n] for n in ("xn", "xt", "ident", "neg_half", "passed"))
        self.y, self.ys = sb("y", [P, TB, C]), sb("ys", [P, TB, C])
        self.stats, self.mv, self.rstd = sb("stats", [P, TB, 6]), sb("mv", [P, TB, 2]), sb("rstd", [P, TB])
        self.var_s, self.rstd_s, self.ys_s = sem("var_s"), sem("rstd_s"), sem("ys_s")
        self.turn_s, self.xt_s = sem("turn_s"), sem("xt_s")

    def vector(self, dve, link, b, y, last=False):
        nc = self.nc
        for t in range(TB):
            st = nc.vector.bn_stats(self.stats[:, t, :], y[:, t, :])
        link(st)
        apart(dve, self.passed)
        for t in range(TB):
            ag = nc.vector.bn_aggr(self.mv[:, t, :], self.stats[:, t, :])
        link(ag)
        nc.vector.tensor_scalar(self.rstd[:], self.mv[:, :, 1], LN_EPS, None, ALU.add).then_inc(self.var_s, 1)
        dve.wait_ge(self.rstd_s, b + 1)
        dve.wait_ge(self.turn_s, b + 1)
        for t in range(TB):
            sc = nc.vector.tensor_scalar(self.ys[:, t, :], y[:, t, :], self.mv[:, t, 0:1], self.rstd[:, t:t + 1],
                                         ALU.subtract, ALU.mult)
        sc.then_inc(self.ys_s, 1)
        if not last:
            dve.wait_ge(self.ys_s, b + 1)
            apart(dve, self.passed)
            link(nc.vector.tensor_copy(self.xn[:, b], self.ys[:]))

    def gpsimd(self, pool, b):
        pool.wait_ge(self.var_s, b + 1)
        self.nc.gpsimd.tensor_tensor(self.rstd[:], self.rstd[:], self.neg_half[:, 0:TB], ALU.pow).then_inc(self.rstd_s, 1)

    def tensor(self, pe, b):
        pe.wait_ge(self.ys_s, b + 1)
        pe.wait_ge(self.xt_s, b + 1)
        for c in range(CC):
            for t in range(TB):
                mm = self.nc.tensor.transpose(self.bank[:, c * T + t * P:c * T + t * P + P], self.ys[:, t, c * P:c * P + P],
                                              self.ident[:])
        mm.then_inc(self.turn_s, 1)

    def scalar(self, act, b):
        act.wait_ge(self.turn_s, b + 2)
        apart(act, self.passed)
        self.nc.scalar.copy(self.xt[:, :, bass.ds(b * T, T)], self.bank.rearrange("p (c t) -> p c t", c=CC)).then_inc(self.xt_s, 1)


def layer0_experts_by_token(nc, io, consts, bank, g, out):
    with ExitStack() as ctx:
        layer0_experts_by_token_in(nc, io, bank, g, *tools(nc, ctx, "l0x"))


def layer0_experts_by_token_in(nc, io, bank, g, sb, sem, dram):
    E, VOCAB = NB, 12500
    SHARE = VOCAB // E
    ident, xn, xt, ct = (g[n] for n in ("ident", "xn", "xt", "ct"))
    ctx_n = sb("ctx_n", [P, E, TB, C])
    ids = sb("ids", [P, NB * T], I32)
    idf = sb("idf", [P, NB * T])
    mask = sb("mask", [P, E, NB * T])
    z = sb("z", [P, E, 2 * T])
    sz = sb("sz", [P, E, 2 * T])
    hid = sb("hid", [P, E, 2, T])
    norm = Norm(nc, g, sb, sem, bank(6))
    ctx_in, ids_in, ct_psum, ct_s, mask_s = (sem(n) for n in ("ctx_in", "ids_in", "ct_psum", "ct_s", "mask_s"))
    z_psum, z_s, sz_s, hid_s, y_psum, y_s, link_s = (sem(n) for n in ("z_psum", "z_s", "sz_s", "hid_s", "y_psum", "y_s", "link_s"))
    LINKS = 3

    with nc.Block() as block:
        @block.sync
        def _(sp):
            sp.dma_start(ctx_n[:], io["ctx_2048"].rearrange("e (t p) c -> p e t c", p=P)).then_inc(ctx_in, 16)
            sp.dma_start(ids[:], io["itok_BxS_13_99985"].rearrange("(a b) t -> a (b t)", a=1).broadcast_to([P, NB * T])).then_inc(ids_in, 16)

        @block.scalar
        def _(act):
            for e in range(E):
                act.wait_ge(ct_psum, e + 1)
                nc.scalar.copy(ct[:, e].rearrange("p k q -> p (k q)"), bank(e)).then_inc(ct_s, 1)
            act.sem_inc(norm.xt_s, 1)
            with act.Fori(0, NB) as b:
                for e in range(E):
                    act.wait_ge(z_s, b * E + e + 1 + E)
                    nc.scalar.activation(sz[:, e], z[:, e], ACT.Silu).then_inc(sz_s, 1)
                norm.scalar(act, b)

        @block.vector
        def _(dve):
            dve.wait_ge(ids_in, 16)
            nc.vector.tensor_copy(idf[:], ids[:]).then_inc(mask_s, 1)
            dve.wait_ge(mask_s, 1)
            nc.vector.tensor_scalar(mask[:, 0], idf[:], float(SHARE), None, ALU.is_lt)
            for e in range(1, E):
                nc.vector.tensor_scalar(mask[:, e], idf[:], float(SHARE * e), None, ALU.is_ge).then_inc(mask_s, 1)
            dve.wait_ge(mask_s, E)
            for e in range(1, E - 1):
                nc.vector.scalar_tensor_tensor(out=mask[:, e], in0=idf[:], scalar=float(SHARE * (e + 1)), in1=mask[:, e],
                                               op0=ALU.is_lt, op1=ALU.mult).then_inc(mask_s, 1)
            dve.wait_ge(mask_s, 2 * E - 2)
            dve.sem_inc(z_s, E)
            dve.sem_inc(y_s, 1)
            with dve.Fori(0, NB) as b:
                link = Link(dve, link_s, LINKS, b)

                def keep(e):
                    dve.wait_ge(z_psum, b * E + e + 1)
                    m = mask[:, e:e + 1, bass.ds(b * T, T)].broadcast_to([P, 2, T])
                    nc.vector.tensor_tensor(z[:, e].rearrange("p (f t) -> p f t", f=2), bank(e).rearrange("p (f t) -> p f t", f=2),
                                            m, ALU.mult).then_inc(z_s, 1)

                def gate(e):
                    dve.wait_ge(sz_s, b * E + e + 1)
                    dve.wait_ge(y_psum, b + 1)
                    nc.vector.tensor_tensor(hid[:, e].rearrange("p f t -> p (f t)"), sz[:, e], z[:, e], ALU.mult).then_inc(hid_s, 1)

                keep(0)
                for e in range(1, E):
                    keep(e)
                    gate(e - 1)
                gate(E - 1)
                dve.wait_ge(y_psum, b + 2)
                y2 = bank(4, 2).rearrange("p (t c) -> p t c", t=TB)[:, :, 0:C]
                nc.vector.tensor_tensor(norm.y[:], y2, xn[:, b], ALU.add).then_inc(y_s, 1)
                dve.wait_ge(y_s, b + 2)
                norm.vector(dve, link, b, norm.y)
                link.close()

        @block.gpsimd
        def _(pool):
            with pool.Fori(0, NB) as b:
                norm.gpsimd(pool, b)

        @block.tensor
        def _(pe):
            pe.wait_ge(ctx_in, 16)
            for e in range(E):
                for k in range(CC):
                    for t in range(TB):
                        mm = nc.tensor.transpose(bank(e)[:, k * T + t * P:k * T + t * P + P], ctx_n[:, e, t, k * P:k * P + P], ident[:])
                mm.then_inc(ct_psum, 1)
            pe.wait_ge(ct_s, E)
            pe.sem_inc(y_psum, 1)
            pe.sem_inc(norm.turn_s, 1)
            with pe.Fori(0, NB) as b:
                for e in range(E):
                    pe.wait_ge(z_s, b * E + e + 1)
                    for f in range(2):
                        for k in range(CC):
                            mm = nc.tensor.matmul(bank(e)[:, f * T:f * T + T], ct[:, e, k, f * P:f * P + P], xt[:, k, bass.ds(b * T, T)],
                                                  start=(k == 0), stop=(k == CC - 1))
                    mm.then_inc(z_psum, 1)
                pe.wait_ge(y_s, b + 1)
                for e in range(E):
                    pe.wait_ge(hid_s, b * E + e + 1)
                    for t in range(TB):
                        for f in range(2):
                            mm = nc.tensor.matmul(bank(4 + t)[:, 0:C], hid[:, e, f, t * P:t * P + P], ct[:, e, f, :],
                                                  start=(e == 0 and f == 0), stop=(e == E - 1 and f == 1))
                mm.then_inc(y_psum, 1)
                norm.tensor(pe, b)


def layer0_experts_by_router(nc, io, consts, bank, g, out):
    with ExitStack() as ctx:
        layer0_experts_by_router_in(nc, io, consts, bank, g, *tools(nc, ctx, "l0f"))


def layer0_experts_by_router_in(nc, io, consts, bank, g, sb, sem, dram):
    E, F, K_TOP, ALPHA, LIMIT = 16, 256, 4, 1.702, 7.0
    NT = NB * TB
    HT = NB * T // 2
    ident, xn, xt = (g[n] for n in ("ident", "xn", "xt"))
    rw, rwt, rb = sb("rw", [E, C]), sb("rwt", [P, CC, E]), sb("rb", [P, E])
    gub, gubt = sb("gub", [E, 2 * F]), sb("gubt", [P, E, 4])
    bd = sb("bd", [E, C])
    resets = sb("resets", [P, NT * E])
    logits, eq, gt, cum, sel = (sb(n, [P, NT, E]) for n in ("logits", "eq", "gt", "cum", "sel"))
    top = sb("top", [P, NT, 8])
    count = sb("count", [P, NT])
    score = sb("score", [P, E, NT])
    score_t = sb("score_t", [E, NT * P])
    acc = sb("acc", [P, NB, TB, C])
    wgu, wd = sb("wgu", [P, 2, CC, 2 * F]), sb("wd", [P, 2, 2, C])
    bias2, score2 = sb("bias2", [P, 2, 4]), sb("score2", [P, 2, NT])
    gate, sig, gs, up = (sb(n, [P, 2, HT]) for n in ("gate", "sig", "gs", "up"))
    hid = sb("hid", [P, 2, NB * T])
    norm = Norm(nc, g, sb, sem, bank(6))
    small_in = sem("small_in")
    w_in = [sem("w_in_even"), sem("w_in_odd")]
    rt_psum, rt_s, lg_psum, score_s, st_psum, st_s, bd_psum, acc0_s = (
        sem(n) for n in ("rt_psum", "rt_s", "lg_psum", "score_s", "st_psum", "st_s", "bd_psum", "acc0_s"))
    gate_psum, up_psum, gate_s, sig_s, gs_s, up_s, hid_s, down_psum, acc_s = (
        sem(n) for n in ("gate_psum", "up_psum", "gate_s", "sig_s", "gs_s", "up_s", "hid_s", "down_psum", "acc_s"))
    route_s, stage_s, link_s = sem("route_s"), sem("stage_s"), sem("link_s")
    UNITS = 8

    with nc.Block() as block:
        @block.sync
        def _(sp):
            sp.dma_start(rw[:], io["L0_ffn_router_weight"]).then_inc(small_in, 16)
            sp.dma_start(rb[:], io["L0_ffn_router_bias"].rearrange("(a e) -> a e", a=1).broadcast_to([P, E])).then_inc(small_in, 16)
            sp.dma_start(gub[:], io["L0_ffn_gate_up_proj_bias"]).then_inc(small_in, 16)
            sp.dma_start(bd[:], io["L0_ffn_down_proj_bias"]).then_inc(small_in, 16)
            sp.dma_start(resets[:], consts["resets"]).then_inc(small_in, 16)
            with sp.Fori(0, E // 2) as it:
                for e in range(2):
                    sp.wait_ge(down_psum, it * 8 + e * 4 + 4)
                    sp.dma_start(wgu[:, e], io["L0_ffn_gate_up_proj"].rearrange("e (k p) n -> e p k n", p=P)[it * 2 + e]).then_inc(w_in[e], 16)
                    sp.dma_start(wd[:, e], io["L0_ffn_down_proj"].rearrange("e (k p) n -> e p k n", p=P)[it * 2 + e]).then_inc(w_in[e], 16)

        @block.scalar
        def _(act):
            act.wait_ge(rt_psum, 1)
            nc.scalar.copy(rwt[:].rearrange("p k e -> p (k e)"), bank(0)[:, 0:CC * E]).then_inc(rt_s, 1)
            nc.scalar.copy(gubt[:].rearrange("p e n -> p n e"), bank(0)[:, CC * E:(CC + 4) * E].rearrange("p (n e) -> p n e", e=E)).then_inc(rt_s, 1)
            act.wait_ge(route_s, 9)
            nc.scalar.activation(eq[:], cum[:], ACT.Exp).then_inc(score_s, 1)
            act.wait_ge(st_psum, 1)
            nc.scalar.copy(score_t[:], bank(2, 2)[0:E, :]).then_inc(st_s, 1)
            with act.Fori(0, E // 2) as it:
                for n in range(UNITS):
                    act.wait_ge(gate_s, it * UNITS + n + 1)
                    nc.scalar.activation(sig[:, n % 2], gate[:, n % 2], ACT.Sigmoid, scale=ALPHA).then_inc(sig_s, 1)
            act.sem_inc(norm.xt_s, 1)
            with act.Fori(0, NB) as b:
                norm.scalar(act, b)

        @block.vector
        def _(dve):
            n = [0]

            def route(ins):
                n[0] += 1
                ins.then_inc(route_s, 1)
                dve.wait_ge(route_s, n[0])

            dve.wait_ge(lg_psum, 1)
            route(nc.vector.tensor_tensor(logits[:], bank(1)[:, 0:NT * E].rearrange("p (t e) -> p t e", e=E),
                                          rb[:].rearrange("p (a e) -> p a e", a=1).broadcast_to([P, NT, E]), ALU.add))
            for t in range(NT):
                mx = nc.vector.max(top[:, t, :], logits[:, t, :])
            route(mx)
            fourth = top[:, :, K_TOP - 1:K_TOP].broadcast_to([P, NT, E])
            nc.vector.tensor_tensor(gt[:], logits[:], fourth, ALU.is_gt)
            route(nc.vector.tensor_tensor(eq[:], logits[:], fourth, ALU.is_equal))
            route(nc.vector.tensor_reduce(count[:], gt[:], AX, ALU.add))
            route(nc.vector.tensor_tensor_scan(cum[:].rearrange("p t e -> p (t e)"), resets[:], eq[:].rearrange("p t e -> p (t e)"),
                                               0.0, ALU.mult, ALU.add))
            route(nc.vector.tensor_tensor(cum[:], cum[:], count[:].rearrange("p (t a) -> p t a", a=1).broadcast_to([P, NT, E]), ALU.add))
            route(nc.vector.scalar_tensor_tensor(out=sel[:], in0=cum[:], scalar=float(K_TOP), in1=eq[:], op0=ALU.is_le, op1=ALU.mult))
            route(nc.vector.tensor_tensor(sel[:], sel[:], gt[:], ALU.add))
            route(nc.vector.tensor_tensor(cum[:], logits[:], top[:, :, 0:1].broadcast_to([P, NT, E]), ALU.subtract))
            dve.wait_ge(score_s, 1)
            route(nc.vector.tensor_tensor(sel[:], sel[:], eq[:], ALU.mult))
            route(nc.vector.tensor_reduce(count[:], sel[:], AX, ALU.add))
            route(nc.vector.reciprocal(count[:], count[:]))
            nc.vector.tensor_tensor(score[:].rearrange("p e t -> p t e"), sel[:],
                                    count[:].rearrange("p (t a) -> p t a", a=1).broadcast_to([P, NT, E]), ALU.mult).then_inc(score_s, 1)
            dve.wait_ge(bd_psum, 1)
            nc.vector.tensor_tensor(acc[:].rearrange("p b t c -> p (b t c)"), bank(4, 4), xn[:].rearrange("p b t c -> p (b t c)"),
                                    ALU.add).then_inc(acc0_s, 1)
            dve.wait_ge(acc0_s, 1)
            dve.wait_ge(rt_s, 2)
            dve.sem_inc(up_s, 2)
            dve.sem_inc(hid_s, 2)
            dve.sem_inc(acc_s, 4)
            with dve.Fori(0, E // 2) as it:
                dve.wait_ge(acc_s, it * 8 + 4)
                nc.vector.tensor_copy(score2[:], score[:, bass.ds(it * 2, 2), :])
                nc.vector.tensor_copy(bias2[:], gubt[:, bass.ds(it * 2, 2), :]).then_inc(stage_s, 1)
                dve.wait_ge(stage_s, it * 2 + 1)
                nc.vector.tensor_scalar(bias2[:, :, 2:4], bias2[:, :, 2:4], 1.0, None, ALU.add).then_inc(stage_s, 1)
                dve.wait_ge(stage_s, it * 2 + 2)

                def take(n):
                    e, w = n // 4, n % 2
                    dve.wait_ge(gate_psum, it * UNITS + n + 1)
                    nc.vector.tensor_scalar(gate[:, n % 2], bank(2 * (n % 2)), bias2[:, e, w:w + 1], LIMIT, ALU.add, ALU.min).then_inc(gate_s, 1)
                    dve.wait_ge(up_psum, it * UNITS + n + 1)
                    dve.wait_ge(hid_s, it * UNITS + n + 1)
                    nc.vector.tensor_scalar(up[:, n % 2], bank(2 * (n % 2) + 1), bias2[:, e, 2 + w:3 + w], 1.0 - LIMIT, ALU.add,
                                            ALU.max).then_inc(up_s, 1)

                def combine(n):
                    half, w = n // 2 % 2, n % 2
                    dve.wait_ge(gs_s, it * UNITS + n + 1)
                    dve.wait_ge(up_s, it * UNITS + n + 3)
                    nc.vector.scalar_tensor_tensor(out=hid[:, w, half * HT:half * HT + HT], in0=up[:, n % 2], scalar=1.0 + LIMIT,
                                                   in1=gs[:, n % 2], op0=ALU.min, op1=ALU.mult).then_inc(hid_s, 1)

                for e in range(2):
                    take(4 * e)
                    for n in range(4 * e + 1, 4 * e + 4):
                        take(n)
                        combine(n - 1)
                    combine(4 * e + 3)
                    for k in range(4):
                        dve.wait_ge(down_psum, it * 8 + e * 4 + k + 9)
                        dve.wait_ge(acc_s, it * 8 + e * 4 + k + 1)
                        for t in range(TB):
                            add = nc.vector.scalar_tensor_tensor(out=acc[:, k, t, :], in0=bank(4 + k)[:, t * C:t * C + C],
                                                                 scalar=score2[:, e, 2 * k + t:2 * k + t + 1], in1=acc[:, k, t, :],
                                                                 op0=ALU.mult, op1=ALU.add)
                        add.then_inc(acc_s, 1)
            dve.wait_ge(acc_s, 4 * E + 4)
            with dve.Fori(0, NB) as b:
                link = Link(dve, link_s, 3, b)
                norm.vector(dve, link, b, acc[:, b])
                link.close()

        @block.gpsimd
        def _(pool):
            with pool.Fori(0, E // 2) as it:
                for n in range(UNITS):
                    pool.wait_ge(sig_s, it * UNITS + n + 1)
                    nc.gpsimd.tensor_tensor(gs[:, n % 2], gate[:, n % 2], sig[:, n % 2], ALU.mult).then_inc(gs_s, 1)
            with pool.Fori(0, NB) as b:
                norm.gpsimd(pool, b)

        @block.tensor
        def _(pe):
            pe.wait_ge(small_in, 16 * 5)
            for k in range(CC):
                nc.tensor.transpose(bank(0)[:, k * E:k * E + E], rw[:, k * P:k * P + P], ident[0:E, 0:E])
            for n in range(4):
                w, kind = n % 2, n // 2
                src = gub[:, w * 2 * P:(w + 1) * 2 * P].rearrange("e (p two) -> e two p", two=2)[:, kind, :]
                mm = nc.tensor.transpose(bank(0)[:, (CC + n) * E:(CC + n + 1) * E], src, ident[0:E, 0:E])
            mm.then_inc(rt_psum, 1)
            pe.wait_ge(rt_s, 1)
            for t in range(NT):
                for k in range(CC):
                    mm = nc.tensor.matmul(bank(1)[:, t * E:t * E + E], xt[:, k, t * P:t * P + P], rwt[:, k, :], start=(k == 0), stop=(k == CC - 1))
            mm.then_inc(lg_psum, 1)
            pe.wait_ge(score_s, 2)
            for t in range(NT):
                mm = nc.tensor.transpose(bank(2, 2)[0:E, t * P:t * P + P], score[:, :, t], ident[:])
            mm.then_inc(st_psum, 1)
            pe.wait_ge(st_s, 1)
            for t in range(NT):
                mm = nc.tensor.matmul(bank(4, 4)[:, t * C:t * C + C], score_t[:, t * P:t * P + P], bd[:], start=True, stop=True)
            mm.then_inc(bd_psum, 1)
            pe.wait_ge(acc0_s, 1)
            pe.sem_inc(down_psum, 8)
            with pe.Fori(0, E // 2) as it:
                for e in range(2):
                    pe.wait_ge(w_in[e], it * 32 + 32)
                    for n in range(4 * e, 4 * e + 4):
                        half, w = n // 2 % 2, n % 2
                        pe.wait_ge(up_s, it * UNITS + n + 1)
                        for kind, done in ((0, gate_psum), (1, up_psum)):
                            wk = wgu[:, e].rearrange("p k (n two) -> p k two n", two=2)[:, :, kind, w * P:w * P + P]
                            for k in range(CC):
                                mm = nc.tensor.matmul(bank(2 * (n % 2) + kind), wk[:, k], xt[:, k, half * HT:half * HT + HT],
                                                      start=(k == 0), stop=(k == CC - 1))
                            mm.then_inc(done, 1)
                    for k in range(4):
                        pe.wait_ge(acc_s, it * 8 + e * 4 + k + 1)
                        pe.wait_ge(hid_s, it * UNITS + e * 4 + (4 if k < 2 else 6))
                        for t in (2 * k, 2 * k + 1):
                            for w in range(2):
                                mm = nc.tensor.matmul(bank(4 + k)[:, t % 2 * C:t % 2 * C + C], hid[:, w, t * P:t * P + P], wd[:, e, w, :],
                                                      start=(w == 0), stop=(w == 1))
                        mm.then_inc(down_psum, 1)
            pe.sem_inc(norm.turn_s, 1)
            with pe.Fori(0, NB) as b:
                norm.tensor(pe, b)


def layer1_retention(nc, io, consts, bank, g, out):
    with ExitStack() as ctx:
        layer1_retention_in(nc, io, consts, bank, g, *tools(nc, ctx, "l1r"))


def layer1_retention_in(nc, io, consts, bank, g, sb, sem, dram):
    RH, RD = 4, 64
    ROT = RD // 2
    ident, xn, xt, neg_half = (g[n] for n in ("ident", "xn", "xt", "neg_half"))
    w_nat = sb("w_nat", [P, 10, C])
    w_t = sb("w_t", [P, 10, CC, P])
    xpos = sb("xpos", [P, TB, 2, 2, ROT])
    decay = sb("decay", [P, RH, 3 * P])
    average = sb("average", [P, P])
    gnw, gnb = sb("gnw", [P, 2]), sb("gnb", [P, 2])
    xs_t = sb("xs_t", [P, CC, T])
    qk = sb("qk", [P, TB, 2, RH, RD])
    rot = sb("rot", [P, TB, 2, RH, ROT])
    v = sb("v", [P, TB, RH, RD])
    qk_t = sb("qk_t", [P, 2, 2, T])
    s_t = sb("s_t", [P, RH, 3 * P])
    st6, mom, tot = sb("st6", [P, 2, 6]), sb("mom", [P, 2, 2]), sb("tot", [P, 2, 2])
    msq, vr, aw, ab = (sb(n, [P, 2]) for n in ("msq", "vr", "aw", "ab"))
    ge, gn, gd = (sb(n, [P, 2 * T]) for n in ("ge", "gn", "gd"))
    ret = sb("ret", [P, 2, T])
    norm = Norm(nc, g, sb, sem, bank(7))
    c_in, wt_psum, wt_s = sem("c_in"), sem("wt_psum"), sem("wt_s")
    xs_s, qkv_psum, g_psum, v_s, rot_s, qkt_psum, qkt_s = (
        sem(n) for n in ("xs_s", "qkv_psum", "g_psum", "v_s", "rot_s", "qkt_psum", "qkt_s"))
    sc_psum, st_s, ret_psum, mom_s, tot_psum, gvar_s, gstd_s, gmin_s, gexp_s, ym_s, y_psum, link_s = (
        sem(n) for n in ("sc_psum", "st_s", "ret_psum", "mom_s", "tot_psum", "gvar_s", "gstd_s", "gmin_s", "gexp_s", "ym_s",
                         "y_psum", "link_s"))
    LINKS = 20

    with nc.Block() as block:
        @block.sync
        def _(sp):
            sp.dma_start(w_nat[:, 0:6], io["L1_attn_wqkv"].rearrange("(n p) c -> p n c", p=P)).then_inc(c_in, 16)
            sp.dma_start(w_nat[:, 6:8], io["L1_attn_wg"].rearrange("(n p) c -> p n c", p=P)).then_inc(c_in, 16)
            sp.dma_start(w_nat[:, 8:10], io["L1_attn_wo"].rearrange("(n p) c -> p n c", p=P)).then_inc(c_in, 16)
            sp.dma_start(xpos[:], consts["xpos"]).then_inc(c_in, 16)
            sp.dma_start(decay[:], consts["decay"]).then_inc(c_in, 16)
            sp.dma_start(average[:], consts["average"]).then_inc(c_in, 16)
            for dst, name in ((gnw, "L1_attn_gn_weight"), (gnb, "L1_attn_gn_bias")):
                for half in range(2):
                    src = io[name].rearrange("(a k two) -> a two k", a=1, two=2)[:, half, :]
                    sp.dma_start(dst[RD * half:RD * half + RD, :], src.broadcast_to([RD, 2]), allow_slow_non_contiguous=True).then_inc(c_in, 16)

        @block.scalar
        def _(act):
            for n in range(5):
                act.wait_ge(wt_psum, n + 1)
                nc.scalar.copy(w_t[:, 2 * n:2 * n + 2].rearrange("p n k c -> p (n k c)"), bank(n)).then_inc(wt_s, 1)
            act.sem_inc(norm.xt_s, 1)
            with act.Fori(0, NB) as b:
                nc.scalar.copy(xs_t[:], xt[:, :, bass.ds(b * T, T)]).then_inc(xs_s, 1)
                for t in range(TB):
                    act.wait_ge(qkv_psum, b * TB + t + 1)
                    src = bank(2 * t, 2)[:, 0:3 * C].rearrange("p (h x d) -> p x h d", h=RH, x=3)
                    nc.scalar.copy(v[:, t], src[:, 2])
                    nc.scalar.copy(qk[:, t, :, :, ROT:RD], src[:, 0:2, :, ROT:RD]).then_inc(v_s, 1)
                act.wait_ge(gmin_s, b + 1)
                nc.scalar.activation(ge[:], gd[:], ACT.Exp).then_inc(gexp_s, 1)
                act.wait_ge(qkt_psum, b + 1)
                nc.scalar.copy(qk_t[:].rearrange("p x k t -> p (x k t)"), bank(5, 2)).then_inc(qkt_s, 1)
                norm.scalar(act, b)

        @block.vector
        def _(dve):
            dve.wait_ge(c_in, 16 * 10)
            with dve.Fori(0, NB) as b:
                link = Link(dve, link_s, LINKS, b)
                for t in range(TB):
                    dve.wait_ge(v_s, b * TB + t + 1)
                    src = bank(2 * t, 2)[:, 0:3 * C].rearrange("p (h x d) -> p x h d", h=RH, x=3)[:, 0:2, :, 0:ROT]
                    for x in range(2):
                        tab = xpos[:, t, x:x + 1]
                        nc.vector.tensor_tensor(qk[:, t, x, :, 0:ROT], src[:, x], tab[:, :, 0, :].broadcast_to([P, RH, ROT]), ALU.mult)
                        pair = src[:, x].rearrange("p h (n two) -> p h n two", two=2)
                        dst = rot[:, t, x].rearrange("p h (n two) -> p h n two", two=2)
                        sin = tab[:, :, 1, :].rearrange("p a (n two) -> p a n two", two=2)
                        for one in range(2):
                            mul = nc.vector.tensor_tensor(dst[:, :, :, one], pair[:, :, :, 1 - one],
                                                          sin[:, :, :, one].broadcast_to([P, RH, ROT // 2]), ALU.mult)
                    link(mul)
                    add = nc.vector.tensor_tensor(qk[:, t, :, :, 0:ROT], qk[:, t, :, :, 0:ROT], rot[:, t], ALU.add)
                add.then_inc(rot_s, 1)
                dve.wait_ge(g_psum, b + 1)
                nc.vector.tensor_scalar(gd[:], bank(4), 20.0, None, ALU.min).then_inc(gmin_s, 1)
                for h in range(RH):
                    dve.wait_ge(sc_psum, b * RH + h + 1)
                    nc.vector.tensor_tensor(s_t[:, h], bank(h)[:, 0:3 * P], decay[:, h], ALU.mult).then_inc(st_s, 1)
                dve.wait_ge(gexp_s, b + 1)
                link(nc.vector.scalar_tensor_tensor(out=gn[:], in0=ge[:], scalar=2.0, in1=ge[:], op0=ALU.add, op1=ALU.mult))
                link(nc.vector.tensor_scalar(gd[:], gn[:], 2.0, None, ALU.add))
                link(nc.vector.reciprocal(ge[:], gd[:]))
                link(nc.vector.tensor_tensor(gn[:], gn[:], ge[:], ALU.mult))
                link(nc.vector.tensor_tensor(gn[:], gn[:], bank(4), ALU.mult))
                dve.wait_ge(ret_psum, b + 1)
                for k in range(2):
                    bs = nc.vector.bn_stats(st6[:, k], bank(5)[:, k * T:k * T + T])
                link(bs)
                apart(dve, norm.passed)
                for k in range(2):
                    ag = nc.vector.bn_aggr(mom[:, k], st6[:, k])
                link(ag)
                link(nc.vector.tensor_tensor(msq[:], mom[:, :, 0], mom[:, :, 0], ALU.mult))
                nc.vector.tensor_tensor(mom[:, :, 1], mom[:, :, 1], msq[:], ALU.add).then_inc(mom_s, 1)
                dve.wait_ge(tot_psum, b + 1)
                link(nc.vector.tensor_copy(tot[:].rearrange("p k m -> p (k m)"), bank(6)[:, 0:4]))
                link(nc.vector.tensor_tensor(msq[:], tot[:, :, 0], tot[:, :, 0], ALU.mult))
                nc.vector.scalar_tensor_tensor(out=vr[:], in0=tot[:, :, 1], scalar=LN_EPS, in1=msq[:], op0=ALU.add,
                                               op1=ALU.subtract).then_inc(gvar_s, 1)
                dve.wait_ge(gstd_s, b + 1)
                link(nc.vector.tensor_tensor(aw[:], vr[:], gnw[:], ALU.mult))
                link(nc.vector.tensor_tensor(ab[:], tot[:, :, 0], aw[:], ALU.mult))
                link(nc.vector.tensor_tensor(ab[:], gnb[:], ab[:], ALU.subtract))
                for k in range(2):
                    ts = nc.vector.tensor_scalar(ret[:, k], bank(5)[:, k * T:k * T + T], aw[:, k:k + 1], ab[:, k:k + 1], ALU.mult, ALU.add)
                link(ts)
                nc.vector.tensor_tensor(ret[:].rearrange("p k t -> p (k t)"), ret[:].rearrange("p k t -> p (k t)"), gn[:],
                                        ALU.mult).then_inc(ym_s, 1)
                dve.wait_ge(y_psum, b + 1)
                y2 = bank(0, 2).rearrange("p (t c) -> p t c", t=TB)[:, :, 0:C]
                link(nc.vector.tensor_tensor(norm.y[:], y2, xn[:, b], ALU.add))
                norm.vector(dve, link, b, norm.y)
                link.close()

        @block.gpsimd
        def _(pool):
            with pool.Fori(0, NB) as b:
                pool.wait_ge(gvar_s, b + 1)
                nc.gpsimd.tensor_tensor(vr[:], vr[:], neg_half[:, 0:2], ALU.pow).then_inc(gstd_s, 1)
                norm.gpsimd(pool, b)

        @block.tensor
        def _(pe):
            pe.wait_ge(c_in, 16 * 10)
            for n in range(10):
                for k in range(CC):
                    mm = nc.tensor.transpose(bank(n // 2)[:, (n % 2) * C + k * P:(n % 2) * C + k * P + P], w_nat[:, n, k * P:k * P + P], ident[:])
                if n % 2:
                    mm.then_inc(wt_psum, 1)
            pe.wait_ge(wt_s, 5)
            pe.sem_inc(norm.turn_s, 1)
            with pe.Fori(0, NB) as b:
                pe.wait_ge(xs_s, b + 1)
                for t in range(TB):
                    for n0, n1 in ((0, 4), (4, 6)):
                        for k in range(CC):
                            mm = nc.tensor.matmul(bank(2 * t, 2)[:, n0 * P:n1 * P], xs_t[:, k, t * P:t * P + P], w_t[:, n0:n1, k, :],
                                                  start=(k == 0), stop=(k == CC - 1))
                    mm.then_inc(qkv_psum, 1)
                for n in range(2):
                    for k in range(CC):
                        mm = nc.tensor.matmul(bank(4)[:, n * T:n * T + T], w_t[:, 6 + n, k, :], xs_t[:, k, :], start=(k == 0), stop=(k == CC - 1))
                mm.then_inc(g_psum, 1)
                pe.wait_ge(rot_s, b + 1)
                for x in range(2):
                    for k in range(2):
                        for t in range(TB):
                            mm = nc.tensor.transpose(bank(5 + x)[:, k * T + t * P:k * T + t * P + P],
                                                     qk[:, t, x, 2 * k:2 * k + 2, :].rearrange("p h d -> p (h d)"), ident[:])
                mm.then_inc(qkt_psum, 1)
                pe.wait_ge(qkt_s, b + 1)
                for h in range(RH):
                    rows, k = slice(RD * (h % 2), RD * (h % 2) + RD), h // 2
                    nc.tensor.matmul(bank(h)[:, 0:T], qk_t[rows, 1, k, 0:P], qk_t[rows, 0, k, :], start=True, stop=True)
                    mm = nc.tensor.matmul(bank(h)[:, T:T + P], qk_t[rows, 1, k, P:T], qk_t[rows, 0, k, P:T], start=True, stop=True)
                    mm.then_inc(sc_psum, 1)
                for h in range(RH):
                    pe.wait_ge(st_s, b * RH + h + 1)
                    rows, k = slice(RD * (h % 2), RD * (h % 2) + RD), h // 2
                    dst = bank(5)[rows, k * T:k * T + T]
                    nc.tensor.matmul(dst, v[:, 0, h, :], s_t[:, h, 0:T], start=True, stop=False, tile_position=(0, RD * (h % 2)))
                    mm = nc.tensor.matmul(dst[:, P:T], v[:, 1, h, :], s_t[:, h, T:T + P], start=False, stop=True,
                                          tile_position=(0, RD * (h % 2)))
                mm.then_inc(ret_psum, 1)
                pe.wait_ge(mom_s, b + 1)
                nc.tensor.matmul(bank(6)[:, 0:4], average[:], mom[:].rearrange("p k m -> p (k m)"), start=True, stop=True).then_inc(tot_psum, 1)
                pe.wait_ge(ym_s, b + 1)
                for t in range(TB):
                    for k in range(2):
                        mm = nc.tensor.matmul(bank(t)[:, 0:C], ret[:, k, t * P:t * P + P], w_t[:, 8:10, k, :], start=(k == 0), stop=(k == 1))
                mm.then_inc(y_psum, 1)
                norm.tensor(pe, b)


def layer1_recurrence(nc, io, consts, bank, g, out):
    with ExitStack() as ctx:
        layer1_recurrence_in(nc, io, bank, g, *tools(nc, ctx, "l1w"))


def layer1_recurrence_in(nc, io, bank, g, sb, sem, dram):
    START = -1.0e38
    ident, xn, xt, ct = (g[n] for n in ("ident", "xn", "xt", "ct"))
    w, u = sb("w", [P, CC]), sb("u", [P, CC])
    o1, p1, q1 = (sb(n, [P, CC, T + 1]) for n in ("o1", "p1", "q1"))
    uk, top = sb("uk", [P, CC, T]), sb("top", [P, CC, T])
    e4 = sb("e4", [P, 4, CC, T])
    pv, ev = sb("pv", [P, CC, T]), sb("ev", [P, CC, T])
    num, dnm = sb("num", [P, CC, T]), sb("dnm", [P, CC, T])
    y_t = sb("y_t", [P, CC, T])
    norm = Norm(nc, g, sb, sem, bank(6))
    c_in, set_s, uk_s, o_s, exps_s, exp_s, ev_s, pv_s, yt_s, y_psum, link_s = (
        sem(n) for n in ("c_in", "set_s", "uk_s", "o_s", "exps_s", "exp_s", "ev_s", "pv_s", "yt_s", "y_psum", "link_s"))
    LINKS = 13

    with nc.Block() as block:
        @block.sync
        def _(sp):
            with nc.allow_non_contiguous_dma("two short vectors"):
                sp.dma_start(w[:], io["L1_xattn_w"].rearrange("(k p) -> p k", p=P)).then_inc(c_in, 16)
                sp.dma_start(u[:], io["L1_xattn_u"].rearrange("(k p) -> p k", p=P)).then_inc(c_in, 16)

        @block.scalar
        def _(act):
            act.sem_inc(norm.xt_s, 1)
            with act.Fori(0, NB) as b:
                act.wait_ge(exps_s, b + 1)
                nc.scalar.activation(e4[:].rearrange("p n k t -> p (n k t)"), e4[:].rearrange("p n k t -> p (n k t)"), ACT.Exp).then_inc(exp_s, 1)
                norm.scalar(act, b)

        @block.vector
        def _(dve):
            nc.vector.memset(o1[:, :, 0:1], START).then_inc(set_s, 1)
            nc.vector.memset(p1[:, :, 0:1], 0.0).then_inc(set_s, 1)
            nc.vector.memset(q1[:, :, 0:1], 0.0).then_inc(set_s, 1)
            dve.wait_ge(set_s, 3)
            dve.wait_ge(c_in, 32)
            dve.sem_inc(yt_s, 1)
            with dve.Fori(0, NB) as b:
                link = Link(dve, link_s, LINKS, b)
                kt = xt[:, :, bass.ds(b * T, T)]
                vt = ct[:, b]
                before = o1[:, :, 0:T]
                for k in range(CC):
                    sc = nc.vector.tensor_tensor_scan(o1[:, k, 1:T + 1], w[:, k:k + 1].broadcast_to([P, T]), kt[:, k, :], START, ALU.add, ALU.max)
                link(sc)
                dve.wait_ge(uk_s, b + 1)
                link(nc.vector.tensor_tensor(top[:], before, uk[:], ALU.max))
                nc.vector.tensor_tensor(e4[:, 0], before, top[:], ALU.subtract)
                nc.vector.tensor_tensor(e4[:, 1], uk[:], top[:], ALU.subtract)
                for k in range(CC):
                    nc.vector.scalar_tensor_tensor(out=e4[:, 2, k], in0=o1[:, k, 0:T], scalar=w[:, k:k + 1], in1=o1[:, k, 1:T + 1],
                                                   op0=ALU.add, op1=ALU.subtract)
                nc.vector.tensor_tensor(e4[:, 3], kt, o1[:, :, 1:T + 1], ALU.subtract).then_inc(exps_s, 1)
                dve.wait_ge(exp_s, b + 1)
                for k in range(CC):
                    sc = nc.vector.tensor_tensor_scan(q1[:, k, 1:T + 1], e4[:, 2, k], e4[:, 3, k], 0.0, ALU.mult, ALU.add)
                link(sc)
                link(nc.vector.tensor_tensor(dnm[:], e4[:, 0], q1[:, :, 0:T], ALU.mult))
                link(nc.vector.tensor_tensor(dnm[:], dnm[:], e4[:, 1], ALU.add))
                link(nc.vector.reciprocal(dnm[:], dnm[:]))
                dve.wait_ge(pv_s, b + 1)
                for k in range(CC):
                    sc = nc.vector.tensor_tensor_scan(p1[:, k, 1:T + 1], e4[:, 2, k], pv[:, k], 0.0, ALU.mult, ALU.add)
                link(sc)
                link(nc.vector.tensor_tensor(num[:], e4[:, 0], p1[:, :, 0:T], ALU.mult))
                dve.wait_ge(ev_s, b + 1)
                link(nc.vector.tensor_tensor(num[:], num[:], ev[:], ALU.add))
                nc.vector.tensor_tensor(y_t[:], num[:], dnm[:], ALU.mult).then_inc(yt_s, 1)
                dve.wait_ge(y_psum, b + 1)
                dve.wait_ge(yt_s, b + 2)
                link(nc.vector.tensor_tensor(norm.y[:].rearrange("p t c -> p (t c)"), bank(0), xn[:, b].rearrange("p t c -> p (t c)"), ALU.add))
                norm.vector(dve, link, b, norm.y)
                link.close()

        @block.gpsimd
        def _(pool):
            pool.wait_ge(c_in, 32)
            with pool.Fori(0, NB) as b:
                pool.wait_ge(yt_s, b + 1)
                ub = u[:].rearrange("p (k a) -> p k a", a=1).broadcast_to([P, CC, T])
                nc.gpsimd.tensor_tensor(uk[:], xt[:, :, bass.ds(b * T, T)], ub, ALU.add).then_inc(uk_s, 1)
                pool.wait_ge(exp_s, b + 1)
                nc.gpsimd.tensor_tensor(pv[:], e4[:, 3], ct[:, b], ALU.mult).then_inc(pv_s, 1)
                nc.gpsimd.tensor_tensor(ev[:], e4[:, 1], ct[:, b], ALU.mult).then_inc(ev_s, 1)
                norm.gpsimd(pool, b)

        @block.tensor
        def _(pe):
            pe.sem_inc(norm.turn_s, 1)
            with pe.Fori(0, NB) as b:
                pe.wait_ge(yt_s, b + 2)
                for t in range(TB):
                    for k in range(CC):
                        mm = nc.tensor.transpose(bank(0)[:, t * C + k * P:t * C + k * P + P], y_t[:, k, t * P:t * P + P], ident[:])
                mm.then_inc(y_psum, 1)
                norm.tensor(pe, b)


def layer1_mixed_experts(nc, io, consts, bank, g, out):
    with ExitStack() as ctx:
        layer1_mixed_experts_in(nc, io, consts, bank, g, out, *tools(nc, ctx, "l1m"))


def layer1_mixed_experts_in(nc, io, consts, bank, g, out, sb, sem, dram):
    E, EH = 32, 64
    KE = E * EH // P
    TOP = E // 2
    GONE = -3.0e38
    ident, xn, xt, neg_half = (g[n] for n in ("ident", "xn", "xt", "neg_half"))
    wv, wo = sb("wv", [P, KE, C]), sb("wo", [P, KE, C])
    sim, sim2 = sb("sim", [P, CC, E]), sb("sim2", [P, CC, E])
    gates = sb("gates", [NB, E])
    ones = sb("ones", [P, NB])
    halves, fold, pick = sb("halves", [E, P]), sb("fold", [P, EH]), sb("pick", [E, KE])
    mean, mean2 = sb("mean", [P, CC, NB]), sb("mean2", [P, CC, NB])
    sq, rn = sb("sq", [NB, 1 + E]), sb("rn", [NB, 1 + E])
    raw, lg, gated, mask, fb, ra, rb2 = (sb(n, [NB, E]) for n in ("raw", "lg", "gated", "mask", "fb", "ra", "rb2"))
    top = sb("top", [NB, 2, 8])
    one = sb("one", [NB, 4])
    r_t, r_d, r_p = sb("r_t", [E, NB]), sb("r_d", [E, KE, NB]), sb("r_p", [P, KE, NB])
    mix = sb("mix", [P, KE, NB, EH])
    sums = sb("sums", [P, 2, 2, C])
    m = sb("m", [P, NB, CC, C])
    y, fin = sb("y", [P, NB, TB, C]), sb("fin", [P, NB, TB, C])
    stats, mv, rstd = sb("stats", [P, NB, TB, 6]), sb("mv", [P, NB, TB, 2]), sb("rstd", [P, NB * TB])
    s_in, w_in, mean_s, aff_psum, sq_s, rn_s, ex_s, exx_s, r_s, rt_psum, rt_s, rp_psum, mix_s = (
        sem(n) for n in ("s_in", "w_in", "mean_s", "aff_psum", "sq_s", "rn_s", "ex_s", "exx_s", "r_s", "rt_psum", "rt_s",
                         "rp_psum", "mix_s"))
    sum_psum, sum_s, m_psum, m_s, y_psum, var_s, rstd_s, fin_s, out_s, chain = (
        sem(n) for n in ("sum_psum", "sum_s", "m_psum", "m_s", "y_psum", "var_s", "rstd_s", "fin_s", "out_s", "chain"))

    with nc.Block() as block:
        @block.sync
        def _(sp):
            sp.dma_start(sim[:], io["L1_ffn_sim_matrix"].rearrange("(k p) e -> p k e", p=P)).then_inc(s_in, 16)
            sp.dma_start(gates[:], io["L1_ffn_gates"].rearrange("(a e) -> a e", a=1).broadcast_to([NB, E])).then_inc(s_in, 16)
            sp.dma_start(halves[:], consts["halves"]).then_inc(s_in, 16)
            sp.dma_start(fold[:], consts["fold"]).then_inc(s_in, 16)
            sp.dma_start(pick[:], consts["pick"]).then_inc(s_in, 16)
            sp.dma_start(wv[:], io["L1_ffn_w_v"].rearrange("(k e) h c -> (e h) k c", e=2)).then_inc(w_in, 16)
            sp.dma_start(wo[:], io["L1_ffn_o_weights"].rearrange("(k e) h c -> (e h) k c", e=2)).then_inc(w_in, 16)
            for b in range(NB):
                sp.wait_ge(fin_s, b + 1)
                sp.dma_start(out[b].rearrange("(t p) c -> p t c", p=P), fin[:, b]).then_inc(out_s, 16)
            sp.wait_ge(out_s, 16 * NB)

        @block.scalar
        def _(act):
            act.wait_ge(s_in, 16 * 5)
            nc.scalar.activation(gates[:], gates[:], ACT.Sigmoid).then_inc(exx_s, 1)
            act.wait_ge(ex_s, 1)
            nc.scalar.activation(ra[:], ra[:], ACT.Exp).then_inc(exx_s, 1)
            for n in range(4):
                act.wait_ge(sum_psum, n + 1)
                nc.scalar.copy(sums[:, n % 2, n // 2], bank(n)[:, 0:C]).then_inc(sum_s, 1)
            for b in range(NB):
                act.wait_ge(m_psum, b + 1)
                nc.scalar.copy(m[:, b].rearrange("p k c -> p (k c)"), bank(4 + b)).then_inc(m_s, 1)

        @block.vector
        def _(dve):
            n = [0]

            def step(ins):
                n[0] += 1
                ins.then_inc(chain, 1)
                dve.wait_ge(chain, n[0])

            step(nc.vector.memset(ones[:], 1.0))
            dve.wait_ge(s_in, 16 * 5)
            nc.vector.tensor_tensor(sim2[:], sim[:], sim[:], ALU.mult)
            step(nc.vector.tensor_reduce(mean[:], xt[:].rearrange("p k (b t) -> p k b t", b=NB), AX, ALU.add))
            step(nc.vector.tensor_scalar(mean[:], mean[:], 1.0 / T, None, ALU.mult))
            nc.vector.tensor_tensor(mean2[:], mean[:], mean[:], ALU.mult).then_inc(mean_s, 1)
            dve.wait_ge(aff_psum, 1)
            nc.vector.tensor_copy(raw[:], bank(0)[0:NB, 0:E])
            nc.vector.tensor_copy(sq[:], bank(0)[0:NB, E:2 * E + 1]).then_inc(sq_s, 1)
            dve.wait_ge(rn_s, 1)
            step(nc.vector.tensor_scalar(raw[:], raw[:], rn[:, E:E + 1], None, ALU.mult))
            step(nc.vector.tensor_tensor(raw[:], raw[:], rn[:, 0:E], ALU.mult))
            dve.wait_ge(exx_s, 1)
            step(nc.vector.tensor_tensor(lg[:], raw[:], gates[:], ALU.subtract))
            step(nc.vector.tensor_scalar(gated[:], lg[:], 0.0, None, ALU.max))
            step(nc.vector.tensor_scalar(mask[:], gated[:], 0.0, None, ALU.is_gt))
            step(nc.vector.tensor_reduce(one[:, 0:1], mask[:], AX, ALU.max))
            step(nc.vector.tensor_scalar(one[:, 0:1], one[:, 0:1], 0.0, None, ALU.is_equal))
            step(nc.vector.max(top[:, 0], lg[:]))
            step(nc.vector.match_replace(fb[:], top[:, 0], lg[:], GONE))
            step(nc.vector.max(top[:, 1], fb[:]))
            step(nc.vector.match_replace(fb[:], top[:, 1], fb[:], GONE))
            step(nc.vector.tensor_scalar(fb[:], fb[:], GONE, one[:, 0:1], ALU.is_equal, ALU.mult))
            step(nc.vector.tensor_tensor(mask[:], mask[:], fb[:], ALU.max))
            step(nc.vector.tensor_reduce(one[:, 1:2], gated[:], AX, ALU.max))
            nc.vector.tensor_scalar(ra[:], gated[:], one[:, 1:2], None, ALU.subtract).then_inc(ex_s, 1)
            dve.wait_ge(exx_s, 2)
            step(nc.vector.tensor_tensor(ra[:], ra[:], mask[:], ALU.mult))
            step(nc.vector.tensor_reduce(one[:, 2:3], ra[:], AX, ALU.add))
            step(nc.vector.reciprocal(one[:, 3:4], one[:, 2:3]))
            nc.vector.tensor_scalar(rb2[:], ra[:], one[:, 3:4], None, ALU.mult).then_inc(r_s, 1)
            dve.wait_ge(rt_psum, 1)
            step(nc.vector.tensor_copy(r_t[:], bank(1)[0:E, 0:NB]))
            nc.vector.tensor_tensor(r_d[:], r_t[:].rearrange("e (a b) -> e a b", a=1).broadcast_to([E, KE, NB]),
                                    pick[:].rearrange("e (k a) -> e k a", a=1).broadcast_to([E, KE, NB]), ALU.mult).then_inc(rt_s, 1)
            dve.wait_ge(rp_psum, 1)
            step(nc.vector.tensor_copy(r_p[:].rearrange("p k b -> p (k b)"), bank(1)[:, 64:64 + KE * NB]))
            for k in range(0, KE, 4):
                nc.vector.tensor_tensor(mix[:, k:k + 4].rearrange("p k b h -> p (k b) h"),
                                        r_p[:, k:k + 4].rearrange("p k (b a) -> p (k b) a", a=1).broadcast_to([P, 4 * NB, EH]),
                                        fold[:].rearrange("p (a h) -> p a h", a=1).broadcast_to([P, 4 * NB, EH]), ALU.mult).then_inc(mix_s, 1)
            for b in range(NB):
                dve.wait_ge(y_psum, b + 1)
                step(nc.vector.tensor_tensor(y[:, b].rearrange("p t c -> p (t c)"), bank(b), xn[:, b].rearrange("p t c -> p (t c)"), ALU.add))
                for t in range(TB):
                    st = nc.vector.bn_stats(stats[:, b, t], y[:, b, t])
                step(st)
                for t in range(TB):
                    ag = nc.vector.bn_aggr(mv[:, b, t], stats[:, b, t])
                step(ag)
                nc.vector.tensor_scalar(rstd[:, 2 * b:2 * b + 2], mv[:, b, :, 1], LN_EPS, None, ALU.add).then_inc(var_s, 1)
                dve.wait_ge(rstd_s, b + 1)
                for t in range(TB):
                    ts = nc.vector.tensor_scalar(fin[:, b, t], y[:, b, t], mv[:, b, t, 0:1], rstd[:, 2 * b + t:2 * b + t + 1],
                                                 ALU.subtract, ALU.mult)
                ts.then_inc(fin_s, 1)

        @block.gpsimd
        def _(pool):
            pool.wait_ge(sq_s, 1)
            nc.gpsimd.tensor_tensor(rn[:], sq[:], neg_half[0:NB, 0:1].broadcast_to([NB, 1 + E]), ALU.pow).then_inc(rn_s, 1)
            for b in range(NB):
                pool.wait_ge(var_s, b + 1)
                nc.gpsimd.tensor_tensor(rstd[:, 2 * b:2 * b + 2], rstd[:, 2 * b:2 * b + 2], neg_half[:, 0:TB], ALU.pow).then_inc(rstd_s, 1)

        @block.tensor
        def _(pe):
            pe.wait_ge(mean_s, 1)
            for dst, lhs, rhs in ((bank(0)[0:NB, 0:E], mean, sim), (bank(0)[0:NB, E:2 * E], None, sim2),
                                  (bank(0)[0:NB, 2 * E:2 * E + 1], mean2, None)):
                for k in range(CC):
                    mm = nc.tensor.matmul(dst, ones[:] if lhs is None else lhs[:, k], ones[:, 0:1] if rhs is None else rhs[:, k],
                                          start=(k == 0), stop=(k == CC - 1))
            mm.then_inc(aff_psum, 1)
            pe.wait_ge(r_s, 1)
            nc.tensor.transpose(bank(1)[0:E, 0:NB], rb2[:], ident[0:NB, 0:NB]).then_inc(rt_psum, 1)
            pe.wait_ge(rt_s, 1)
            nc.tensor.matmul(bank(1)[:, 64:64 + KE * NB], halves[:], r_d[:].rearrange("e k b -> e (k b)"), start=True, stop=True).then_inc(rp_psum, 1)
            pe.wait_ge(w_in, 32)
            pe.wait_ge(mix_s, KE // 4)
            for n in range(4):
                pair, w = n // 2, (wv, wo)[n % 2]
                for k in range(KE):
                    mm = nc.tensor.matmul(bank(n)[:, 0:C], mix[:, k, 2 * pair:2 * pair + 2].rearrange("p b h -> p (b h)"), w[:, k],
                                          start=(k == 0), stop=(k == KE - 1))
                mm.then_inc(sum_psum, 1)
            for b in range(NB):
                pe.wait_ge(sum_s, 2 * (b // 2) + 2)
                rows = slice(EH * (b % 2), EH * (b % 2) + EH)
                for k in range(CC):
                    mm = nc.tensor.matmul(bank(4 + b)[:, k * C:k * C + C], sums[rows, 0, b // 2, k * P:k * P + P], sums[rows, 1, b // 2, :],
                                          start=True, stop=True)
                mm.then_inc(m_psum, 1)
            for b in range(NB):
                pe.wait_ge(m_s, b + 1)
                for t in range(TB):
                    for k in range(CC):
                        mm = nc.tensor.matmul(bank(b)[:, t * C:t * C + C], xt[:, k, b * T + t * P:b * T + t * P + P], m[:, b, k],
                                              start=(k == 0), stop=(k == CC - 1))
                mm.then_inc(y_psum, 1)


_OUT = (NB, T, C)


def kernel(**inputs):
    import concourse.bacc as bacc
    from concourse.bass_utils import run_bass_kernel_spmd

    nc = bacc.Bacc("TRN2", target_bir_lowering=False, num_devices=1)
    arrays, io = {}, {}
    for name, a in inputs.items():
        a = np.ascontiguousarray(a)
        arrays[f"in_{name}"] = a
        io[name] = nc.dram_tensor(f"in_{name}", a.shape, mybir.dt.from_np(a.dtype), kind="ExternalInput").ap()
    consts = {}
    for name, a in constants().items():
        arrays[f"const_{name}"] = a
        consts[name] = nc.dram_tensor(f"const_{name}", a.shape, mybir.dt.from_np(a.dtype), kind="ExternalInput").ap()
    out = nc.dram_tensor("out", _OUT, F32, kind="ExternalOutput").ap()
    build(nc, io, consts, out)
    return run_bass_kernel_spmd(nc, [arrays], core_ids=[0]).results[0]["out"]
```

```python
from contextlib import ExitStack

import numpy as np

import concourse.bass as bass
from concourse import mybir
from concourse.alu_op_type import AluOpType as ALU

ACT = mybir.ActivationFunctionType
F32 = mybir.dt.float32
BF16 = mybir.dt.bfloat16
F32R = mybir.dt.float32r
I32 = mybir.dt.int32
AX = mybir.AxisListType.X

P = 128
NB, T, C = 4, 256, 256
TB = T // P
CC = C // P
H, D = 16, 16
NP = H // 2
Q = 32
NQ = P // Q
LN_EPS = 1e-5
NEG = -1.0e30
FLOOR = -1.0e28
SLOTS = (0, 1, 4), (2, 3), (5,)
SLOTS_B = (0, 2, 5), (1, 3), (4,)


class Link:

    def __init__(self, eng, sem, per, it):
        self.eng, self.sem, self.per, self.it, self.n = eng, sem, per, it, 0

    def __call__(self, ins, behind=0):
        self.n += 1
        ins.then_inc(self.sem, 1)
        self.eng.wait_ge(self.sem, self.it * self.per + self.n - behind)

    def wait(self):
        self.eng.wait_ge(self.sem, self.it * self.per + self.n)

    def close(self):
        assert self.n == self.per, ("links", self.n, self.per)


def apart(eng, passed):
    eng.sem_inc(passed, 1)


def constants():
    f32 = np.float32
    half = D // 2
    inv = (f32(1.0) / np.power(f32(10000.0), np.arange(half, dtype=f32) / f32(half), dtype=f32)).astype(f32)
    ang = (np.arange(T, dtype=f32)[:, None] * inv[None, :]).astype(f32)
    cos, sin = np.cos(ang).astype(f32), np.sin(ang).astype(f32)
    rope = np.concatenate([cos, cos, -sin, sin], 1).reshape(TB, P, 4 * half).transpose(1, 0, 2)
    out = {"ident": np.eye(P, dtype=f32), "rope": np.ascontiguousarray(rope)}
    i, j = np.arange(P)[:, None], np.arange(P)[None, :]
    masks = np.zeros((P, 4, 2, P), f32)
    for n, ok in enumerate((j < i, j <= i, i < j, i <= j)):
        masks[:, n] = np.where(ok, 0.0, NEG)[:, None, :]
    out["masks"] = masks.reshape(P, -1)
    resets = np.ones((P, NB * TB, 16), f32)
    resets[:, :, 0] = 0.0
    out["resets"] = resets.reshape(P, -1)
    dim, heads = 32, 4
    inv = (f32(1.0) / np.power(f32(10000.0), np.arange(0, dim, 2, dtype=f32) / f32(dim), dtype=f32)).astype(f32)
    t = np.arange(T, dtype=f32)
    ang = np.repeat((t[:, None] * inv[None, :]).astype(f32), 2, axis=-1)
    base = ((np.arange(0, dim, 2, dtype=f32) + f32(0.4 * dim)) / f32(1.4 * dim)).astype(f32)
    scale = np.power(base[None, :], ((t - T // 2) / f32(512.0))[:, None], dtype=f32)
    scale = np.concatenate([scale, scale], axis=-1)
    sign = np.where(np.arange(dim) % 2, f32(1.0), f32(-1.0))
    xpos = np.stack([np.stack([np.cos(ang) * sc, np.sin(ang) * sc * sign], 1) for sc in (scale, f32(1.0) / scale)], 1)
    out["xpos"] = np.ascontiguousarray(xpos.astype(f32).reshape(TB, P, 2, 2, dim).transpose(1, 0, 2, 3, 4))
    gamma = (1.0 - 2.0 ** (-5.0 - np.arange(heads))).astype(f32)
    q, k = np.arange(T), np.arange(T)[:, None]
    dist = np.maximum(q - k, 0).astype(f32)
    full = np.stack([np.where(q >= k, np.power(gm, dist, dtype=f32), f32(0.0)) for gm in gamma], 1).astype(f32)
    out["decay"] = np.ascontiguousarray(np.concatenate([full[:P], full[P:, :, P:]], axis=-1))
    out["average"] = np.kron(np.eye(2, dtype=f32), np.full((64, 64), 1.0 / 64, f32))
    p2 = np.arange(P)
    out["halves"] = (np.arange(32)[:, None] % 2 == p2[None, :] // 64).astype(f32)
    out["fold"] = (p2[:, None] % 64 == np.arange(64)[None, :]).astype(f32)
    out["pick"] = (np.arange(32)[:, None] // 2 == np.arange(16)[None, :]).astype(f32)
    out["eye32"] = np.tile(np.eye(Q, dtype=f32).reshape(1, -1), (P, 1))
    return out


def build(nc, io, consts, out, debug=None):
    with ExitStack() as ctx:
        def sb(name, shape, dt=F32):
            return ctx.enter_context(nc.sbuf_tensor(name, shape, dt))

        ps = ctx.enter_context(nc.psum_tensor("ps", [P, 8 * 512], F32))

        def bank(n, k=1):
            return ps[:, 512 * n:512 * (n + k)]

        g = {
            "ident": sb("ident", [P, P]), "neg_half": sb("neg_half", [P, 8]),
            "xn": sb("xn", [P, NB, TB, C]), "xt": sb("xt", [P, CC, NB * T]),
            "ct": sb("ct", [P, NB, CC, T]),
        }
        g["passed"] = ctx.enter_context(nc.semaphore("passed"))
        g["ready"] = ctx.enter_context(nc.semaphore("ready"))
        g["norm_sems"] = [ctx.enter_context(nc.semaphore(f"norm_{n}")) for n in ("var_s", "rstd_s", "ys_s", "turn_s", "xt_s")]
        layers = ((layer0_attention, "attn"), (layer0_experts_by_token, "xattn"), (layer0_experts_by_router, "ffn"),
                  (layer1_retention, "attn1"), (layer1_recurrence, "wkv"), (layer1_mixed_experts, "all"))
        for layer, name in layers:
            layer(nc, io, consts, bank, g, out)
            if debug == name and name != "all":
                finish = ctx.enter_context(nc.semaphore("finish"))
                with nc.Block() as block:
                    @block.sync
                    def _(sp):
                        sp.dma_start(out.rearrange("b (t p) c -> p b t c", p=P), g["xn"][:]).then_inc(finish, 16)
                        sp.wait_ge(finish, 16)
                return


def tools(nc, ctx, tag):
    def sb(name, shape, dt=F32):
        return ctx.enter_context(nc.sbuf_tensor(f"{tag}_{name}", shape, dt))

    def sem(name):
        return ctx.enter_context(nc.semaphore(f"{tag}_{name}"))

    def dram(name, shape, dt=F32):
        return nc.dram_tensor(f"{tag}_{name}", shape, dt, kind="Internal").ap()

    return sb, sem, dram


def layer0_attention(nc, io, consts, bank, g, out):
    with ExitStack() as ctx:
        layer0_attention_in(nc, io, consts, bank, g, *tools(nc, ctx, "l0a"))


def layer0_attention_in(nc, io, consts, bank, g, sb, sem, dram):
    ident, xn, xt, neg_half = (g[n] for n in ("ident", "xn", "xt", "neg_half"))
    identb, ready, passed = sb("identb", [P, P], BF16), g["ready"], g["passed"]
    rope = sb("rope", [P, TB, 2 * D])
    masks = sb("masks", [P, 4, 2 * P], BF16)
    eye32 = sb("eye32", [P, Q * Q])
    wqk = sb("wqk", [P, CC, 2 * C])
    wvb = sb("wvb", [P, CC, C + H])
    wo = sb("wo", [P, CC, C])
    bb = sb("bb", [P, H])
    x_in = sb("x_in", [P, TB, C])
    x_res = sb("x_res", [P, TB, C])
    xs_t = sb("xs_t", [P, CC, T])
    v_first = sb("v_first", [P, TB, H, D])
    v_next = sb("v_next", [P, TB, H, D])
    v = sb("v", [P, TB, H, D])
    beta = sb("beta", [P, TB, H])
    roped = sb("roped", [P, TB, 2 * C])
    ropet = sb("ropet", [P, TB, 2 * C])
    left = sb("left", [P, TB, 2 * H, 6, D], BF16)
    right = sb("right", [P, TB, H, 6, D], BF16)
    left_t = sb("left_t", [99, 2, H, T], BF16)
    right_t = sb("right_t", [99, H, T], BF16)
    rowmax = sb("rowmax", [P, TB, 2, H])
    negmax = sb("negmax", [P, 2, H])
    nmf = sb("nmf", [P, TB, 2, H])
    nmr = sb("nmr", [P, TB, 2, H])
    nm3 = sb("nm3", [P, TB, 2, 3, H], BF16)
    nm_t = sb("nm_t", [96, T], BF16)
    e_nat = sb("e_nat", [P, H, 3 * P])
    e_t = sb("e_t", [P, 2, H, 3 * P])
    den = sb("den", [P, 2, H])
    gain = sb("gain", [P, 2, H])
    gtmp = sb("gtmp", [P, 2, H])
    gain_next = sb("gain_next", [P, 2 * H])
    gain_t = sb("gain_t", [2 * H, P])
    gain_rows = sb("gain_rows", [P, Q])
    low = sb("low", [P, Q, Q])
    inv = sb("inv", [P, Q, Q])
    invt = sb("invt", [P, 2, 136])
    inv_t = sb("inv_t", [P, 2, H, Q])
    u1 = sb("u1", [P, TB, H, 2 * D])
    rhs = sb("rhs", [P, H, D])
    rden = sb("rden", [P, TB, H])
    maskf = e_nat[:].rearrange("p h c -> p (h c)")[:, 0:8 * P]
    o_t = g["ct"][:].rearrange("p b k t -> p (b k t)")[:, 0:4 * T].rearrange("p (a t) -> p a t", a=4)
    o_nat = g["ct"][:, 2].rearrange("p k t -> p (k t)").rearrange("p (t c) -> p t c", t=TB)
    on_t = g["ct"][:, 3]
    low_d = dram("low_d", [NQ, Q, 2 * H, Q])
    inv_d = dram("inv_d", [NQ, 2 * H, Q, Q])

    consts_in, x_loaded, x_res_in, moved = (sem(n) for n in ("consts_in", "x_loaded", "x_res_in", "moved"))
    xt_psum, xt_sbuf = sem("xt_psum"), sem("xt_sbuf")
    qkv_psum, v_sbuf, part_s = sem("qkv_psum"), sem("v_sbuf"), sem("part_s")
    beta_s, stack_s = sem("beta_s"), sem("stack_s")
    turned, turned_act, turned_dve = sem("turned"), sem("turned_act"), sem("turned_dve")
    scores, neg_s, e_nat_s, max_q = sem("scores"), sem("neg_s"), sem("e_nat_s"), sem("max_q")
    nm3_s, nmt_psum, nmt_sbuf, nm_rows = sem("nm3_s"), sem("nmt_psum"), sem("nmt_sbuf"), sem("nm_rows")
    e_t_s = sem("e_t_s")
    gain_s, gain_psum, gain_sbuf, low_out, low_in, inv_s, inv_out, inv_in = (sem(n) for n in (
        "gain_s", "gain_psum", "gain_sbuf", "low_out", "low_in", "inv_s", "inv_out", "inv_in"))
    res_psum, rhs_s, sol_psum, sol_s = sem("res_psum"), sem("rhs_s"), sem("sol_psum"), sem("sol_s")
    o_psum, o_sbuf, ot_psum, onat_s, on_psum, on_sbuf, wo_psum = (sem(n) for n in (
        "o_psum", "o_sbuf", "ot_psum", "onat_s", "on_psum", "on_sbuf", "wo_psum"))
    project_link, front_link, back_link, setup_s = (sem(n) for n in ("project_link", "front_link", "back_link", "setup_s"))

    TURNS = 3 * TB * 2
    TURN_BANKS = (5, 0, 1, 2)
    SLOT = (0, 2, 4)
    NG = 2
    HG = H // NG
    SOLVE_BANK = (6, 7)
    STEPS = TB * NQ
    DESCENT = (0, 4, 7, 10, 13, 16, 19, 22, 25, 28, Q - 1)
    PROJECT_LINKS, FRONT_LINKS, BACK_LINKS = 5, 139, 19
    norm = Norm(nc, g, sb, bank(6), 0)

    x_dram = io["x"].rearrange("b (t p) c -> b p t c", p=P)

    BESIDE_SOLVE = ((("turn", 2),), (("scores", 0),), (("scores", 1),), (("scores", 2),), (("scores", 3),), (("scores", 4),),
                    (("scores", 5), ("weigh",)), (("scores", 6), ("turn_gain",)), (("scores", 7),), (("project", 0), ("project", 1)),
                    (("project", 2),), (("project", 3), ("descend", 0)), (("descend", 1),), (("descend", 2),),
                    (("descend", 3),), (("descend", 4),))

    BESIDE_NUMERATORS = (0, 1, 2, 5)

    with nc.Block() as block:
        def run(**stages):
            eng = stages.pop("eng")

            def go(name, *at):
                if name in stages:
                    stages[name](*at)

            def beside_solve(i, stage, third):
                for name, *at in stage:
                    if name != "project":
                        go(name, i, *at)
                    elif third:
                        go(name, i + 1, *at)

            def body(b, second=True, third=True):
                if second:
                    go("turn", b + 1, 0)
                    go("turn", b + 1, 1)
                for c in range(STEPS):
                    for half, name in ((0, "residual"), (1, "solution")):
                        go(name, b, c)
                        if second:
                            beside_solve(b + 1, BESIDE_SOLVE[2 * c + half], third)
                go("outputs", b, 0)
                if second:
                    after_scores(b + 1, third, lambda n: n in BESIDE_NUMERATORS and go("outputs", b, 1 + BESIDE_NUMERATORS.index(n)))
                else:
                    for n in range(1, 5):
                        go("outputs", b, n)

            def after_scores(i, third, beside=None):
                go("invert", i, third)
                for n in range(NP):
                    if beside:
                        beside(n)
                    go("numerators", i, n)
                    if 1 <= n < 6:
                        go("descend", i, n + 4)
                go("finish", i)

            for n in range(4):
                go("project", 0, n)
            for n in range(2):
                go("turn", 0, n)
            for stage in BESIDE_SOLVE:
                beside_solve(0, stage, True)
            after_scores(0, True)
            with eng.Fori(0, NB - 2) as b:
                body(b)
            body(NB - 2, third=False)
            body(NB - 1, second=False)

        @block.sync
        def _(sp):
            sp.dma_start(x_in[:], x_dram[0]).then_inc(x_loaded, 16)
            sp.dma_start(ident[:], consts["ident"]).then_inc(consts_in, 16)
            for n, name in enumerate(("L0_attn_Wq", "L0_attn_Wk")):
                sp.dma_start(wqk[:, :, n * C:(n + 1) * C], io[name].rearrange("(k p) n -> p k n", p=P)).then_inc(consts_in, 16)
            sp.dma_start(wvb[:, :, 0:C], io["L0_attn_Wv"].rearrange("(k p) n -> p k n", p=P)).then_inc(consts_in, 16)
            sp.dma_start(wvb[:, :, C:C + H], io["L0_attn_Wb"].rearrange("(k p) n -> p k n", p=P)).then_inc(consts_in, 16)
            sp.dma_start(rope[:], consts["rope"]).then_inc(consts_in, 16)
            sp.dma_start(maskf, consts["masks"]).then_inc(consts_in, 16)
            sp.dma_start(eye32[:], consts["eye32"]).then_inc(consts_in, 16)
            sp.dma_start(wo[:], io["L0_attn_Wo"].rearrange("(k p) n -> p k n", p=P)).then_inc(consts_in, 16)
            sp.dma_start(bb[:], io["L0_attn_bb"].rearrange("(a h) -> a h", a=1).broadcast_to([P, H])).then_inc(consts_in, 16)

            def residual(b, c):
                if c == 0:
                    sp.wait_ge(norm.turn_s, b + 1)
                    sp.dma_start(x_res[:], x_dram[b]).then_inc(x_res_in, 16)

            def weigh(i):
                if type(i) is not int or i < NB - 1:
                    sp.wait_ge(xt_psum, i + 1)
                    sp.dma_start(x_in[:], x_dram[i + 1]).then_inc(x_loaded, 16)
                sp.wait_ge(e_nat_s, i * NP + NP)
                for q in range(NQ):
                    src = e_nat[Q * q:Q * q + Q, :, P:3 * P].rearrange("r h (s c) -> r h s c", s=2)
                    for s in range(2):
                        sp.dma_start(low_d[q].rearrange("r (s h) j -> r s h j", s=2)[:, s],
                                     src[:, :, s, Q * q:Q * q + Q]).then_inc(low_out, 16)
                sp.wait_ge(low_out, i * 128 + 128)
                for q in range(NQ):
                    sp.dma_start(low[Q * q:Q * q + Q], low_d[q].rearrange("r g j -> g r j")).then_inc(low_in, 16)
                sp.wait_ge(gain_sbuf, i + 1)
                for q in range(NQ):
                    sp.dma_start(gain_rows[Q * q:Q * q + Q], gain_t[:, Q * q:Q * q + Q]).then_inc(low_in, 16)

            def invert(i, third):
                sp.wait_ge(nmt_sbuf, i + 1)
                for k in range(2):
                    sp.dma_start(left_t[96:99, k, :, :], nm_t[48 * k:48 * k + 48, :]).then_inc(nm_rows, 16)

            def finish(i):
                sp.wait_ge(inv_s, i + 1)
                for q in range(NQ):
                    sp.dma_start(inv_d[q], inv[Q * q:Q * q + Q]).then_inc(inv_out, 16)
                sp.wait_ge(inv_out, i * 64 + 64)
                for q in range(NQ):
                    sp.dma_start(inv_t[Q * q:Q * q + Q].rearrange("k s h r -> k (s h) r"),
                                 inv_d[q].rearrange("g k r -> k g r")).then_inc(inv_in, 16)

            run(eng=sp, residual=residual, weigh=weigh, invert=invert, finish=finish)

        @block.scalar
        def _(act):
            act.wait_ge(consts_in, 16 * 10)
            nc.scalar.copy(masks[:].rearrange("p a b -> p (a b)"), maskf).then_inc(setup_s, 1)
            nc.scalar.copy(identb[:], ident[:]).then_inc(setup_s, 1)
            act.sem_inc(norm.xt_s, 1)

            def project(i, n):
                if n == 0:
                    act.wait_ge(xt_psum, i + 1)
                    nc.scalar.copy(xs_t[:].rearrange("p a b -> p (a b)"), bank(0)).then_inc(xt_sbuf, 1)
                elif n == 2:
                    act.wait_ge(beta_s, i + 1)
                    if type(i) is not int or i:
                        act.wait_ge(moved, 2 * i - 1)
                    for t in range(TB):
                        cp = nc.scalar.copy(v_first[:, t].rearrange("p h d -> p (h d)"), bank(3 + t)[:, 0:C])
                    cp.then_inc(v_sbuf, 1)
                elif n == 3:
                    for k in range(2):
                        act.wait_ge(part_s, i * 3 + k + 1)
                        for s in SLOTS[k][1:]:
                            for t in range(TB):
                                cp = nc.scalar.copy(left[:, t, :, s, :], left[:, t, :, SLOTS[k][0], :])
                    cp.then_inc(stack_s, 1)

            def turn(i, n):
                for gr in (4 * n, 4 * n + 2):
                    act.wait_ge(turned, i * TURNS + gr + 1)
                    turn_out(nc.scalar.copy, gr, left_t, right_t, bank, TURN_BANKS).then_inc(turned_act, 1)

            def turn_gain(i):
                act.wait_ge(gain_psum, i + 1)
                nc.scalar.copy(gain_t[:], bank(5)[0:2 * H, 3 * P:4 * P]).then_inc(gain_sbuf, 1)

            def scores_(i, n):
                if n < 4:
                    for p in (2 * n, 2 * n + 1):
                        act.wait_ge(neg_s, i * NP + p + 1)
                        for h in (2 * p, 2 * p + 1):
                            sc = bank(SLOT[p % 3] + h % 2)
                            for s, (lo, hi) in enumerate(((0, 2 * P), (2 * P, 3 * P))):
                                ex = nc.scalar.activation(e_nat[:, h, lo:hi], sc[:, lo:hi], ACT.Exp, scale=0.25,
                                                          bias=negmax[:, s, h:h + 1], accum_out=den[:, s, h:h + 1])
                        ex.then_inc(e_nat_s, 1)

            def solution(i, c):
                t, q = divmod(c, NQ)
                for gr in range(NG):
                    act.wait_ge(sol_psum, i * 16 + c * NG + gr + 1)
                    nc.scalar.copy(u1[Q * q:Q * q + Q, t, HG * gr:HG * gr + HG, 0:D],
                                   bank(SOLVE_BANK[gr])[Q * q:Q * q + Q, 0:HG * D].rearrange("p (h d) -> p h d", d=D)).then_inc(sol_s, 1)

            def invert(i, third):
                act.wait_ge(nmt_psum, i + 1)
                nc.scalar.copy(nm_t[:], bank(2).bitcast(BF16)[0:96, 0:T]).then_inc(nmt_sbuf, 1)

            def numerators(i, n):
                for m in (2 * n, 2 * n + 1):
                    k, p = divmod(m, NP)
                    act.wait_ge(scores, i * 4 * NP + 2 * NP + m + 1)
                    src = bank(SLOT[(m + 2 * NP) % 3], 2).rearrange("p (h c) -> p h c", h=2)[:, :, 0:3 * P]
                    nc.scalar.activation(e_t[:, k, 2 * p:2 * p + 2, :], src, ACT.Exp, scale=0.25).then_inc(e_t_s, 1)

            def outputs(b, n):
                if n == 0:
                    act.wait_ge(o_psum, b + 1)
                    nc.scalar.copy(o_t.rearrange("p a b -> p (a b)"), bank(6, 2)).then_inc(o_sbuf, 1)
                elif n == 2:
                    act.wait_ge(on_psum, b + 1)
                    nc.scalar.copy(on_t.rearrange("p a b -> p (a b)"), bank(6)).then_inc(on_sbuf, 1)
                elif n == 4:
                    norm.scalar(act, b)

            run(eng=act, project=project, turn=turn, scores=scores_, turn_gain=turn_gain, solution=solution, invert=invert,
                numerators=numerators, outputs=outputs)

        @block.vector
        def _(dve):
            nc.vector.memset(right_t[96:99], 1.0).then_inc(setup_s, 1)
            nc.vector.memset(u1[:, :, :, D:2 * D], 1.0).then_inc(setup_s, 1)
            nc.vector.memset(neg_half[:], -0.5).then_inc(ready, 1)
            dve.wait_ge(consts_in, 16 * 10)
            plink, flink, blink = (Link(dve, link, per, 0) for link, per in (
                (project_link, PROJECT_LINKS), (front_link, FRONT_LINKS), (back_link, BACK_LINKS)))

            def project(i, n):
                if n == 0:
                    if plink.n:
                        plink.close()
                    plink.it, plink.n = i, 0
                if n in (1, 2):
                    t = n - 1
                    dve.wait_ge(qkv_psum, i * 4 + 2 * n)
                    add = nc.vector.tensor_tensor(beta[:, 1 - t, :], bank(3 + t)[:, C:C + H], bb[:], ALU.add)
                    if n == 2:
                        add.then_inc(beta_s, 1)
                    src = bank(1 + t).rearrange("p (h d) -> p h d", d=D)
                    dst = roped[:, t].rearrange("p (h d) -> p h d", d=D)
                    tmp = ropet[:, t].rearrange("p (h d) -> p h d", d=D)
                    tab = rope[:, t:t + 1, :]
                    nc.vector.tensor_tensor(dst, src, tab[:, :, 0:D].broadcast_to([P, 2 * H, D]), ALU.mult)
                    for a, z in ((0, D // 2), (D // 2, 0)):
                        mul = nc.vector.tensor_tensor(tmp[:, :, a:a + D // 2], src[:, :, z:z + D // 2],
                                                      tab[:, :, D + a:D + a + D // 2].broadcast_to([P, 2 * H, D // 2]), ALU.mult)
                    plink(mul)
                    plink(nc.vector.tensor_tensor(dst, dst, tmp, ALU.add))
                elif n == 3:
                    rq = roped[:].rearrange("p t (h d) -> p (t h) d", d=D)
                    rr = ropet[:].rearrange("p t (h d) -> p (t h) d", d=D)
                    lf = left[:].rearrange("p t h s d -> p (t h) s d")
                    nc.vector.tensor_copy(lf[:, :, 0, :], rq).then_inc(part_s, 1)
                    dve.wait_ge(part_s, i * 3 + 1)
                    plink(nc.vector.tensor_tensor(rr, rq, lf[:, :, 0, :], ALU.subtract))
                    nc.vector.tensor_copy(lf[:, :, 2, :], rr).then_inc(part_s, 1)
                    dve.wait_ge(part_s, i * 3 + 2)
                    nc.vector.tensor_tensor(lf[:, :, 5, :], rr, lf[:, :, 2, :], ALU.subtract).then_inc(part_s, 1)

            def turn(i, n):
                if n == 0:
                    if flink.n:
                        flink.close()
                    flink.it, flink.n = i, 0
                for gr in (4 * n + 1, 4 * n + 3):
                    dve.wait_ge(turned, i * TURNS + gr + 1)
                    turn_out(nc.vector.tensor_copy, gr, left_t, right_t, bank, TURN_BANKS).then_inc(turned_dve, 1)

            def scores_(i, n):
                if n >= 0:
                    for m in (2 * n, 2 * n + 1):
                        k, p = divmod(m, NP)
                        dve.wait_ge(scores, i * 4 * NP + m + 1)
                        sc = bank(SLOT[m % 3], 2).rearrange("p (h c) -> p h c", h=2)
                        nc.vector.tensor_reduce(rowmax[:, 0, k, 2 * p:2 * p + 2], sc[:, :, 0:2 * P], AX, ALU.max)
                        rd = nc.vector.tensor_reduce(rowmax[:, 1, k, 2 * p:2 * p + 2], sc[:, :, 2 * P:3 * P], AX, ALU.max)
                        if k == 1:
                            rd.then_inc(max_q, 1)
                        else:
                            flink(rd)
                            nc.vector.tensor_scalar(negmax[:, :, 2 * p:2 * p + 2], rowmax[:, :, 0, 2 * p:2 * p + 2], FLOOR, -0.25,
                                                    ALU.max, ALU.mult).then_inc(neg_s, 1)

            def residual(b, c):
                if c == 0:
                    if blink.n:
                        blink.close()
                    blink.it, blink.n = b, 0
                    return
                t, q = divmod(c, NQ)
                rows = slice(Q * q, Q * q + Q)
                for gr in range(NG):
                    hs = slice(HG * gr, HG * gr + HG)
                    dve.wait_ge(res_psum, b * 14 + (c - 1) * NG + gr + 1)
                    src = bank(SOLVE_BANK[gr])[rows, 0:HG * D].rearrange("p (h d) -> p h d", d=D)
                    gn = gain[rows, 1 - t, hs].rearrange("p (h a) -> p h a", a=1).broadcast_to([Q, HG, D])
                    blink(nc.vector.tensor_tensor(rhs[rows, hs, :], src, gn, ALU.mult))
                    nc.vector.tensor_tensor(rhs[rows, hs, :], rhs[rows, hs, :], v[rows, t, hs, :], ALU.add).then_inc(rhs_s, 1)

            def weigh(i):
                dve.wait_ge(e_nat_s, i * NP + NP)
                flink(nc.vector.tensor_scalar(gtmp[:], den[:], 0.0, None, ALU.is_equal))
                flink(nc.vector.tensor_tensor(gtmp[:], gtmp[:], den[:], ALU.add))
                flink(nc.vector.reciprocal(gtmp[:], gtmp[:]))
                nc.vector.scalar_tensor_tensor(out=gain_next[:].rearrange("p (s h) -> p s h", s=2), in0=gtmp[:], scalar=-1.0, in1=beta[:],
                                               op0=ALU.mult, op1=ALU.mult).then_inc(gain_s, 1)

            def invert(i, third):
                dve.wait_ge(gain_s, i + 1)
                flink(nc.vector.tensor_copy(gain[:].rearrange("p s h -> p (s h)"), gain_next[:]))
                dve.wait_ge(max_q, i * NP + NP)
                for s in range(2):
                    ts = nc.vector.tensor_scalar(nmf[:, 1 - s], rowmax[:, s], FLOOR, -1.0, ALU.max, ALU.mult)
                flink(ts)
                flink(nc.vector.tensor_copy(nm3[:, :, :, 0, :], nmf[:]))
                flink(nc.vector.tensor_tensor(nmr[:], nmf[:], nm3[:, :, :, 0, :], ALU.subtract))
                flink(nc.vector.tensor_copy(nm3[:, :, :, 1, :], nmr[:]))
                nc.vector.tensor_tensor(nm3[:, :, :, 2, :], nmr[:], nm3[:, :, :, 1, :], ALU.subtract).then_inc(nm3_s, 1)

            def descend(i, n):
                if n == 0:
                    flink(nc.vector.tensor_copy(inv[:].rearrange("p k r -> p (k r)"), eye32[:]))
                    dve.wait_ge(low_in, i * 128 + 128)
                    flink(nc.vector.tensor_tensor(low[:], low[:], gain_rows[:].rearrange("p (r a) -> p r a", a=1).broadcast_to([P, Q, Q]),
                                                  ALU.mult))
                for j in range(DESCENT[n], DESCENT[n + 1]):
                    k, mid = j + 1, (j + 1 + Q) // 2
                    parts = [(lo, hi, tmp) for lo, hi, tmp in ((j + 1, mid, invt[:, 0]), (mid, Q, invt[:, 1])) if hi > lo]
                    if len(parts) == 1:
                        flink.wait()
                    for op in (0, 1):
                        for lo, hi, tmp in parts:
                            tmp = tmp[:, 0:k * (hi - lo)].rearrange("p (k r) -> p k r", k=k)
                            part = inv[:, 0:k, lo:hi]
                            if op:
                                ins = nc.vector.tensor_tensor(part, part, tmp, ALU.add)
                            else:
                                col = low[:, lo:hi, j:j + 1].rearrange("p r a -> p a r").broadcast_to([P, k, hi - lo])
                                ins = nc.vector.tensor_tensor(tmp, inv[:, 0:k, j:j + 1].broadcast_to([P, k, hi - lo]), col, ALU.mult)
                            if j == Q - 2 and op:
                                ins.then_inc(inv_s, 1)
                            else:
                                flink(ins, behind=len(parts) - 1)
                if n < 9:
                    flink.wait()

            def outputs(b, n):
                if n == 1:
                    dve.wait_ge(ot_psum, b + 1)
                    ot = bank(6, 2).rearrange("p (t h d) -> p t h d", t=TB, h=H)
                    blink(nc.vector.reciprocal(rden[:], ot[:, :, :, D]))
                    nc.vector.tensor_tensor(o_nat.rearrange("p t (h d) -> p t h d", d=D), ot[:, :, :, 0:D],
                                            rden[:].rearrange("p t (h a) -> p t h a", a=1).broadcast_to([P, TB, H, D]), ALU.mult).then_inc(onat_s, 1)
                elif n == 3:
                    dve.wait_ge(wo_psum, b + 1)
                    dve.wait_ge(x_res_in, b * 16 + 16)
                    blink(nc.vector.tensor_tensor(norm.y[:].rearrange("p t c -> p (t c)"), bank(7), x_res[:].rearrange("p t c -> p (t c)"), ALU.add))
                    norm.vector(dve, blink, b, norm.y)

            run(eng=dve, project=project, turn=turn, scores=scores_, weigh=weigh, residual=residual, invert=invert,
                descend=descend, outputs=outputs)
            plink.close()
            flink.close()
            blink.close()

        @block.gpsimd
        def _(pool):
            pool.wait_ge(ready, 1)

            def invert(i, third):
                if type(i) is not int or i:
                    pool.wait_ge(sol_s, i * 16)
                else:
                    carry(0)
                pool.wait_ge(moved, 2 * i + 1)
                apart(pool, passed)
                nc.gpsimd.tensor_copy(v[:], v_next[:]).then_inc(moved, 1)
                if third:
                    pool.wait_ge(moved, 2 * i + 2)
                    carry(i + 1)

            def carry(i):
                pool.wait_ge(v_sbuf, i + 1)
                apart(pool, passed)
                nc.gpsimd.tensor_copy(v_next[:], v_first[:]).then_inc(moved, 1)

            def project(i, n):
                if n == 3:
                    for k in range(3):
                        pool.wait_ge(part_s, i * 3 + k + 1)
                        apart(pool, passed)
                        src = left[:, :, H:2 * H, SLOTS[k][0], :]
                        for s in SLOTS_B[k]:
                            cp = nc.gpsimd.tensor_copy(right[:, :, :, s, :], src)
                    cp.then_inc(stack_s, 1)

            def outputs(b, n):
                if n == 3:
                    norm.gpsimd(pool, b)

            run(eng=pool, project=project, invert=invert, outputs=outputs)

        @block.tensor
        def _(pe):
            pe.wait_ge(consts_in, 16 * 10)
            pe.wait_ge(setup_s, 4)
            pe.wait_ge(ready, 1)
            pe.sem_inc(norm.turn_s, 1)

            def free_slot(i, n):
                if n < NP:
                    pe.wait_ge(e_nat_s, i * NP + n + 1)
                elif n < 2 * NP:
                    pe.wait_ge(max_q, i * NP + n - NP + 1)
                else:
                    pe.wait_ge(e_t_s, i * 2 * NP + n - 2 * NP + 1)

            def project(i, n):
                if n == 0:
                    if type(i) is not int or i:
                        pe.wait_ge(max_q, i * NP)
                    pe.wait_ge(x_loaded, i * 16 + 16)
                    for c in range(CC):
                        for t in range(TB):
                            mm = nc.tensor.transpose(bank(0)[:, c * T + t * P:c * T + t * P + P], x_in[:, t, c * P:c * P + P], ident[:])
                    mm.then_inc(xt_psum, 1)
                elif n in (1, 2):
                    pe.wait_ge(xt_sbuf, i + 1)
                    for t in (n - 1,):
                        for w, dst in ((wqk, bank(1 + t)), (wvb, bank(3 + t)[:, 0:C + H])):
                            for c in range(CC):
                                mm = nc.tensor.matmul(dst, xs_t[:, c, t * P:t * P + P], w[:, c, :], start=(c == 0), stop=(c == CC - 1))
                            mm.then_inc(qkv_psum, 1)

            def turn(i, n):
                if n >= 0:
                    if n == 0 and (type(i) is not int or i):
                        pe.wait_ge(e_t_s, i * 2 * NP)
                    pe.wait_ge(stack_s, i * 2 + 2)
                    for gr in range(4 * n, 4 * n + 4):
                        a, t, hh = gr // 4, gr // 2 % 2, gr % 2
                        if gr >= 4:
                            done, m = (turned_act, turned_dve)[gr % 2], (gr - 4) // 2 + 1
                            pe.wait_ge(done, i * (TURNS // 2) + m)
                        dst = bank(TURN_BANKS[gr % 4]).bitcast(BF16)
                        for j in range(8):
                            h = 8 * hh + j
                            src = right[:, t, h] if a == 2 else left[:, t, (H if a == 0 else 0) + h]
                            mm = nc.tensor.transpose(dst[0:96, j * P:j * P + P], src.rearrange("p s d -> p (s d)"), identb[:])
                        mm.then_inc(turned, 1)

            def scores_(i, n):
                if n >= 0:
                    if n == 0:
                        pe.wait_ge(turned_act, i * (TURNS // 2) + TURNS // 2)
                        pe.wait_ge(turned_dve, i * (TURNS // 2) + TURNS // 2)
                    for m in (2 * n, 2 * n + 1):
                        k, p = divmod(m, NP)
                        if m == NP + 6:
                            pe.wait_ge(gain_sbuf, i + 1)
                        elif m >= 3:
                            free_slot(i, m - 3)
                        for h in (2 * p, 2 * p + 1):
                            dst = bank(SLOT[m % 3] + h % 2)
                            nc.tensor.matmul(dst[:, P:3 * P], identb[:], masks[:, k, :], start=True, stop=False, skip_group_check=True)
                            nc.tensor.matmul(dst[:, 0:2 * P], left_t[0:96, k, h, P:T], right_t[0:96, h, :], start=False, stop=True,
                                             skip_group_check=True)
                            mm = nc.tensor.matmul(dst[:, 2 * P:3 * P], left_t[0:96, k, h, 0:P], right_t[0:96, h, 0:P], start=False,
                                                  stop=True, skip_group_check=True)
                        mm.then_inc(scores, 1)

            def turn_gain(i):
                pe.wait_ge(gain_s, i + 1)
                free_slot(i, NP + 3)
                nc.tensor.transpose(bank(5)[0:2 * H, 3 * P:4 * P], gain_next[:], ident[:]).then_inc(gain_psum, 1)

            def invert(i, third):
                if third:
                    pe.wait_ge(v_sbuf, i + 2)
                    pe.wait_ge(part_s, i * 3 + 4)
                pe.wait_ge(nm3_s, i + 1)
                for t in range(TB):
                    mm = nc.tensor.transpose(bank(2).bitcast(BF16)[0:96, t * P:t * P + P], nm3[:, t].rearrange("p k a h -> p (k a h)"), identb[:])
                mm.then_inc(nmt_psum, 1)

            def numerators(i, n):
                if n == 0:
                    pe.wait_ge(nm_rows, i * 32 + 32)
                for m in (2 * n, 2 * n + 1):
                    k, p = divmod(m, NP)
                    free_slot(i, 2 * NP + m - 3)
                    for h in (2 * p, 2 * p + 1):
                        dst = bank(SLOT[(m + 2 * NP) % 3] + h % 2)
                        two = dst[:, 0:4 * P].rearrange("p (a c) -> p a c", a=2)[:, :, 0:P]
                        nc.tensor.matmul(two, identb[:], masks[:, 2 + k, :].rearrange("p (a c) -> p a c", a=2), start=True, stop=False,
                                         skip_group_check=True)
                        nc.tensor.matmul(dst[:, 0:2 * P], right_t[:, h, 0:P], left_t[:, k, h, :], start=False, stop=True, skip_group_check=True)
                        mm = nc.tensor.matmul(dst[:, 2 * P:3 * P], right_t[:, h, P:T], left_t[:, k, h, P:T], start=False, stop=True,
                                              skip_group_check=True)
                    mm.then_inc(scores, 1)

            def residual(b, c):
                if c == 0:
                    pe.wait_ge(inv_in, b * 64 + 64)
                    pe.wait_ge(e_t_s, b * 2 * NP + 2 * NP)
                    pe.wait_ge(moved, 2 * b + 2)
                    return
                t, q = divmod(c, NQ)
                rows = slice(Q * q, Q * q + Q)
                for gr in range(NG):
                    pe.wait_ge(sol_s, b * 16 + (c - 1) * NG + gr + 1)
                    apart(pe, passed)
                    for i in range(HG):
                        h = HG * gr + i
                        dst = bank(SOLVE_BANK[gr])[rows, i * D:i * D + D]
                        if t:
                            mm = nc.tensor.matmul(dst, e_t[:, 0, h, P + Q * q:P + Q * q + Q], u1[:, 0, h, 0:D], start=True,
                                                  stop=(q == 0), tile_position=(0, Q * q))
                        if q:
                            lo = 2 * P * t + Q * q
                            mm = nc.tensor.matmul(dst, e_t[0:Q * q, 0, h, lo:lo + Q], u1[0:Q * q, t, h, 0:D], start=(t == 0),
                                                  stop=True, tile_position=(0, Q * q))
                    mm.then_inc(res_psum, 1)

            def solution(b, c):
                t, q = divmod(c, NQ)
                rows = slice(Q * q, Q * q + Q)
                for gr in range(NG):
                    if c:
                        pe.wait_ge(rhs_s, b * 14 + (c - 1) * NG + gr + 1)
                    apart(pe, passed)
                    for i in range(HG):
                        h = HG * gr + i
                        src = rhs[rows, h, :] if c else v[rows, 0, h, :]
                        mm = nc.tensor.matmul(bank(SOLVE_BANK[gr])[rows, i * D:i * D + D], inv_t[rows, 1 - t, h, :], src, start=True,
                                              stop=True, tile_position=(Q * q, Q * q))
                    mm.then_inc(sol_psum, 1)

            def outputs(b, n):
                if n == 0:
                    pe.wait_ge(sol_s, b * 16 + 16)
                    for h in range(H):
                        dst = bank(6, 2)[Q * (h % 4):Q * (h % 4) + Q, (h // 4) * T:(h // 4) * T + T]
                        nc.tensor.matmul(dst, u1[:, 0, h, :], e_t[:, 1, h, 0:T], start=True, stop=False, tile_position=(0, Q * (h % 4)))
                        mm = nc.tensor.matmul(dst[:, P:T], u1[:, 1, h, :], e_t[:, 1, h, T:T + P], start=False, stop=True,
                                              tile_position=(0, Q * (h % 4)))
                    mm.then_inc(o_psum, 1)
                elif n == 1:
                    pe.wait_ge(o_sbuf, b + 1)
                    for t in range(TB):
                        for gr in range(4):
                            mm = nc.tensor.transpose(bank(6 + t)[:, gr * P:gr * P + P], o_t[:, gr, t * P:t * P + P], ident[:])
                    mm.then_inc(ot_psum, 1)
                elif n == 2:
                    pe.wait_ge(onat_s, b + 1)
                    for c in range(CC):
                        for t in range(TB):
                            mm = nc.tensor.transpose(bank(6)[:, c * T + t * P:c * T + t * P + P], o_nat[:, t, c * P:c * P + P], ident[:])
                    mm.then_inc(on_psum, 1)
                elif n == 3:
                    pe.wait_ge(on_sbuf, b + 1)
                    for t in range(TB):
                        for c in range(CC):
                            mm = nc.tensor.matmul(bank(7)[:, t * C:t * C + C], on_t[:, c, t * P:t * P + P], wo[:, c, :], start=(c == 0),
                                                  stop=(c == CC - 1))
                    mm.then_inc(wo_psum, 1)
                elif n == 4:
                    norm.tensor(pe, b)

            run(eng=pe, project=project, turn=turn, scores=scores_, turn_gain=turn_gain, residual=residual, solution=solution,
                invert=invert, numerators=numerators, outputs=outputs)


def turn_out(copy, g, left_t, right_t, bank, banks):
    a, t, hh = g // 4, g // 2 % 2, g % 2
    src = bank(banks[g % 4]).bitcast(BF16)[0:96, :].rearrange("p (h t) -> p h t", h=8)
    dst = right_t[0:96] if a == 2 else left_t[0:96, a]
    return copy(dst[:, 8 * hh:8 * hh + 8, t * P:t * P + P], src)


class Norm:

    def __init__(self, nc, g, sb, out_bank, before):
        self.nc, self.bank = nc, out_bank
        self.xn, self.xt, self.ident, self.neg_half, self.passed = (g[n] for n in ("xn", "xt", "ident", "neg_half", "passed"))
        self.y, self.ys = sb("y", [P, TB, C]), sb("ys", [P, TB, C])
        self.stats, self.mv, self.rstd = sb("stats", [P, TB, 6]), sb("mv", [P, TB, 2]), sb("rstd", [P, TB])
        self.var_s, self.rstd_s, self.ys_s, self.turn_s, self.xt_s = g["norm_sems"]
        self.before = NB * before

    def vector(self, dve, link, b, y, last=False):
        nc = self.nc
        for t in range(TB):
            st = nc.vector.bn_stats(self.stats[:, t, :], y[:, t, :])
        link(st)
        apart(dve, self.passed)
        for t in range(TB):
            ag = nc.vector.bn_aggr(self.mv[:, t, :], self.stats[:, t, :])
        link(ag)
        nc.vector.tensor_scalar(self.rstd[:], self.mv[:, :, 1], LN_EPS, None, ALU.add).then_inc(self.var_s, 1)
        dve.wait_ge(self.rstd_s, b + (self.before + 1))
        dve.wait_ge(self.turn_s, b + (self.before + 1))
        for t in range(TB):
            sc = nc.vector.tensor_scalar(self.ys[:, t, :], y[:, t, :], self.mv[:, t, 0:1], self.rstd[:, t:t + 1],
                                         ALU.subtract, ALU.mult)
        sc.then_inc(self.ys_s, 1)
        if not last:
            dve.wait_ge(self.ys_s, b + (self.before + 1))
            apart(dve, self.passed)
            link(nc.vector.tensor_copy(self.xn[:, b], self.ys[:]))

    def gpsimd(self, pool, b):
        pool.wait_ge(self.var_s, b + (self.before + 1))
        self.nc.gpsimd.tensor_tensor(self.rstd[:], self.rstd[:], self.neg_half[:, 0:TB], ALU.pow).then_inc(self.rstd_s, 1)

    def tensor(self, pe, b):
        pe.wait_ge(self.ys_s, b + (self.before + 1))
        pe.wait_ge(self.xt_s, b + (self.before + 1))
        for c in range(CC):
            for t in range(TB):
                mm = self.nc.tensor.transpose(self.bank[:, c * T + t * P:c * T + t * P + P], self.ys[:, t, c * P:c * P + P],
                                              self.ident[:])
        mm.then_inc(self.turn_s, 1)

    def scalar(self, act, b):
        act.wait_ge(self.turn_s, b + (self.before + 2))
        apart(act, self.passed)
        self.nc.scalar.copy(self.xt[:, :, bass.ds(b * T, T)], self.bank.rearrange("p (c t) -> p c t", c=CC)).then_inc(self.xt_s, 1)


def layer0_experts_by_token(nc, io, consts, bank, g, out):
    with ExitStack() as ctx:
        layer0_experts_by_token_in(nc, io, bank, g, *tools(nc, ctx, "l0x"))


def layer0_experts_by_token_in(nc, io, bank, g, sb, sem, dram):
    E, VOCAB = NB, 12500
    SHARE = VOCAB // E
    ident, xn, xt, ct = (g[n] for n in ("ident", "xn", "xt", "ct"))
    ctx_n = sb("ctx_n", [P, E, TB, C])
    ids = sb("ids", [P, NB * T], I32)
    idf = sb("idf", [P, NB * T])
    mask = sb("mask", [P, E, NB * T])
    z = sb("z", [P, E, 2 * T])
    sz = sb("sz", [P, E, 2 * T])
    hid = sb("hid", [P, E, 2, T])
    norm = Norm(nc, g, sb, bank(6), 1)
    ctx_in, ids_in, ct_psum, ct_s, mask_s = (sem(n) for n in ("ctx_in", "ids_in", "ct_psum", "ct_s", "mask_s"))
    z_psum, z_s, sz_s, hid_s, y_psum, y_s, link_s = (sem(n) for n in ("z_psum", "z_s", "sz_s", "hid_s", "y_psum", "y_s", "link_s"))
    LINKS = 3

    with nc.Block() as block:
        @block.sync
        def _(sp):
            sp.dma_start(ctx_n[:], io["ctx_2048"].rearrange("e (t p) c -> p e t c", p=P)).then_inc(ctx_in, 16)
            sp.dma_start(ids[:], io["itok_BxS_13_99985"].rearrange("(a b) t -> a (b t)", a=1).broadcast_to([P, NB * T])).then_inc(ids_in, 16)

        @block.scalar
        def _(act):
            for e in range(E):
                act.wait_ge(ct_psum, e + 1)
                nc.scalar.copy(ct[:, e].rearrange("p k q -> p (k q)"), bank(e)).then_inc(ct_s, 1)
            with act.Fori(0, NB) as b:
                for e in range(E):
                    act.wait_ge(z_s, b * E + e + 1 + E)
                    nc.scalar.activation(sz[:, e], z[:, e], ACT.Silu).then_inc(sz_s, 1)
                norm.scalar(act, b)

        @block.vector
        def _(dve):
            dve.wait_ge(ids_in, 16)
            nc.vector.tensor_copy(idf[:], ids[:]).then_inc(mask_s, 1)
            dve.wait_ge(mask_s, 1)
            nc.vector.tensor_scalar(mask[:, 0], idf[:], float(SHARE), None, ALU.is_lt)
            for e in range(1, E):
                nc.vector.tensor_scalar(mask[:, e], idf[:], float(SHARE * e), None, ALU.is_ge).then_inc(mask_s, 1)
            dve.wait_ge(mask_s, E)
            for e in range(1, E - 1):
                nc.vector.scalar_tensor_tensor(out=mask[:, e], in0=idf[:], scalar=float(SHARE * (e + 1)), in1=mask[:, e],
                                               op0=ALU.is_lt, op1=ALU.mult).then_inc(mask_s, 1)
            dve.wait_ge(mask_s, 2 * E - 2)
            dve.sem_inc(z_s, E)
            dve.sem_inc(y_s, 1)
            with dve.Fori(0, NB) as b:
                link = Link(dve, link_s, LINKS, b)

                def keep(e):
                    dve.wait_ge(z_psum, b * E + e + 1)
                    m = mask[:, e:e + 1, bass.ds(b * T, T)].broadcast_to([P, 2, T])
                    nc.vector.tensor_tensor(z[:, e].rearrange("p (f t) -> p f t", f=2), bank(e).rearrange("p (f t) -> p f t", f=2),
                                            m, ALU.mult).then_inc(z_s, 1)

                def gate(e):
                    dve.wait_ge(sz_s, b * E + e + 1)
                    dve.wait_ge(y_psum, b + 1)
                    nc.vector.tensor_tensor(hid[:, e].rearrange("p f t -> p (f t)"), sz[:, e], z[:, e], ALU.mult).then_inc(hid_s, 1)

                keep(0)
                for e in range(1, E):
                    keep(e)
                    gate(e - 1)
                gate(E - 1)
                dve.wait_ge(y_psum, b + 2)
                y2 = bank(4, 2).rearrange("p (t c) -> p t c", t=TB)[:, :, 0:C]
                nc.vector.tensor_tensor(norm.y[:], y2, xn[:, b], ALU.add).then_inc(y_s, 1)
                dve.wait_ge(y_s, b + 2)
                norm.vector(dve, link, b, norm.y)
                link.close()

        @block.gpsimd
        def _(pool):
            with pool.Fori(0, NB) as b:
                norm.gpsimd(pool, b)

        @block.tensor
        def _(pe):
            pe.wait_ge(ctx_in, 16)
            for e in range(E):
                for k in range(CC):
                    for t in range(TB):
                        mm = nc.tensor.transpose(bank(e)[:, k * T + t * P:k * T + t * P + P], ctx_n[:, e, t, k * P:k * P + P], ident[:])
                mm.then_inc(ct_psum, 1)
            pe.wait_ge(ct_s, E)
            pe.sem_inc(y_psum, 1)
            with pe.Fori(0, NB) as b:
                for e in range(E):
                    pe.wait_ge(z_s, b * E + e + 1)
                    for f in range(2):
                        for k in range(CC):
                            mm = nc.tensor.matmul(bank(e)[:, f * T:f * T + T], ct[:, e, k, f * P:f * P + P], xt[:, k, bass.ds(b * T, T)],
                                                  start=(k == 0), stop=(k == CC - 1))
                    mm.then_inc(z_psum, 1)
                pe.wait_ge(y_s, b + 1)
                for e in range(E):
                    pe.wait_ge(hid_s, b * E + e + 1)
                    for t in range(TB):
                        for f in range(2):
                            mm = nc.tensor.matmul(bank(4 + t)[:, 0:C], hid[:, e, f, t * P:t * P + P], ct[:, e, f, :],
                                                  start=(e == 0 and f == 0), stop=(e == E - 1 and f == 1))
                mm.then_inc(y_psum, 1)
                norm.tensor(pe, b)


def layer0_experts_by_router(nc, io, consts, bank, g, out):
    with ExitStack() as ctx:
        layer0_experts_by_router_in(nc, io, consts, bank, g, *tools(nc, ctx, "l0f"))


def layer0_experts_by_router_in(nc, io, consts, bank, g, sb, sem, dram):
    E, F, K_TOP, ALPHA, LIMIT = 16, 256, 4, 1.702, 7.0
    NT = NB * TB
    HT = NB * T // 2
    ident, xn, xt, passed = (g[n] for n in ("ident", "xn", "xt", "passed"))
    rw, rwt, rb = sb("rw", [E, C]), sb("rwt", [P, CC, E]), sb("rb", [P, E])
    gub, gubt = sb("gub", [E, 2 * F]), sb("gubt", [P, E, 4])
    bd = sb("bd", [E, C])
    resets = sb("resets", [P, NT * E])
    logits, eq, gt, cum, sel = (sb(n, [P, NT, E]) for n in ("logits", "eq", "gt", "cum", "sel"))
    top = sb("top", [P, NT, 8])
    count = sb("count", [P, NT])
    score = sb("score", [P, E, NT])
    score_t = sb("score_t", [E, NT * P])
    acc = sb("acc", [P, NB, TB, C])
    wgu, wd = sb("wgu", [P, 2, CC, 2 * F]), sb("wd", [P, 2, 2, C])
    x_high, x_rest = sb("x_high", [P, CC, NB * T], F32R), sb("x_rest", [P, CC, NB * T], F32R)
    w_high, w_rest = sb("w_high", [P, 2, 3, 2 * F], F32R), sb("w_rest", [P, 2, 3, 2 * F], F32R)
    hid_high, hid_rest = sb("hid_high", [P, 2, NB * T], F32R), sb("hid_rest", [P, 2, NB * T], F32R)
    bias2, score2 = sb("bias2", [P, 2, 4]), sb("score2", [P, 2, NT])
    gate, sig, gs, up = (sb(n, [P, 2, HT]) for n in ("gate", "sig", "gs", "up"))
    hid = sb("hid", [P, 2, HT])
    norm = Norm(nc, g, sb, bank(6), 2)
    small_in = sem("small_in")
    w_in = [sem("w_in_even"), sem("w_in_odd")]
    rt_psum, rt_s, lg_psum, score_s, st_psum, st_s, bd_psum, acc0_s = (
        sem(n) for n in ("rt_psum", "rt_s", "lg_psum", "score_s", "st_psum", "st_s", "bd_psum", "acc0_s"))
    gate_psum, up_psum, gate_s, sig_s, gs_s, up_s, hid_s, down_psum, acc_s = (
        sem(n) for n in ("gate_psum", "up_psum", "gate_s", "sig_s", "gs_s", "up_s", "hid_s", "down_psum", "acc_s"))
    route_s, stage_s, link_s = sem("route_s"), sem("stage_s"), sem("link_s")
    x_high_s, x_rest_s, w_high_s, w_rest_s, hid_high_s, hid_rest_s = (
        sem(n) for n in ("x_high_s", "x_rest_s", "w_high_s", "w_rest_s", "hid_high_s", "hid_rest_s"))
    UNITS = 4

    def each_expert(eng, expert):
        expert(0, 0, True, False)
        expert(1, 1, False, False)
        with eng.Fori(1, E // 2 - 1) as it:
            for e in range(2):
                expert(it * 2 + e, e, False, False)
        expert(E - 2, 0, False, False)
        expert(E - 1, 1, False, True)

    def raw(e, part):
        if part < CC:
            return wgu[:, e, part].rearrange("p (n two) -> p two n", two=2)
        return wd[:, e].rearrange("p w c -> p (w c)").rearrange("p (a n) -> p a n", a=2)

    def split(buf, e, part):
        return buf[:, e, part].rearrange("p (a n) -> p a n", a=2)

    with nc.Block() as block:
        @block.sync
        def _(sp):
            sp.dma_start(rw[:], io["L0_ffn_router_weight"]).then_inc(small_in, 16)
            sp.dma_start(rb[:], io["L0_ffn_router_bias"].rearrange("(a e) -> a e", a=1).broadcast_to([P, E])).then_inc(small_in, 16)
            sp.dma_start(gub[:], io["L0_ffn_gate_up_proj_bias"]).then_inc(small_in, 16)
            sp.dma_start(bd[:], io["L0_ffn_down_proj_bias"]).then_inc(small_in, 16)
            sp.dma_start(resets[:], consts["resets"]).then_inc(small_in, 16)
            with sp.Fori(0, E // 2) as it:
                for e in range(2):
                    sp.wait_ge(w_rest_s, it * 6 + e * 3 + 3)
                    sp.dma_start(wgu[:, e], io["L0_ffn_gate_up_proj"].rearrange("e (k p) n -> e p k n", p=P)[it * 2 + e]).then_inc(w_in[e], 16)
                    sp.dma_start(wd[:, e], io["L0_ffn_down_proj"].rearrange("e (k p) n -> e p k n", p=P)[it * 2 + e]).then_inc(w_in[e], 16)

        @block.scalar
        def _(act):
            nc.scalar.copy(x_high[:], xt[:]).then_inc(x_high_s, 1)

            def high_weights(x, e, part):
                if part == 0:
                    act.wait_ge(w_in[e], (x - e) * 16 + 32)
                    if type(x) is not int or x > 1:
                        act.wait_ge(down_psum, x * 4 + 4)
                    apart(act, passed)
                nc.scalar.copy(split(w_high, e, part), raw(e, part)).then_inc(w_high_s, 1)

            for part in range(3):
                high_weights(0, 0, part)
            act.wait_ge(rt_psum, 1)
            nc.scalar.copy(rwt[:].rearrange("p k e -> p (k e)"), bank(0)[:, 0:CC * E]).then_inc(rt_s, 1)
            nc.scalar.copy(gubt[:].rearrange("p e n -> p n e"), bank(0)[:, CC * E:(CC + 4) * E].rearrange("p (n e) -> p n e", e=E)).then_inc(rt_s, 1)
            act.wait_ge(route_s, 9)
            nc.scalar.activation(eq[:], cum[:], ACT.Exp).then_inc(score_s, 1)
            act.wait_ge(st_psum, 1)
            nc.scalar.copy(score_t[:], bank(2, 2)[0:E, :]).then_inc(st_s, 1)

            def expert(x, e, first, last):
                def high(x, n):
                    half, w = n // 2, n % 2
                    act.wait_ge(hid_s, x * UNITS + n + 3)
                    apart(act, passed)
                    nc.scalar.copy(hid_high[:, w, half * HT:half * HT + HT], hid[:, n % 2]).then_inc(hid_high_s, 1)

                for n in range(UNITS):
                    act.wait_ge(gate_s, x * UNITS + n + 1)
                    nc.scalar.activation(sig[:, n % 2], gate[:, n % 2], ACT.Sigmoid, scale=ALPHA).then_inc(sig_s, 1)
                    if n:
                        high(x, n - 1)
                    elif not first:
                        high(x - 1, UNITS - 1)
                    if n < 3 and not last:
                        high_weights(x + 1, 1 - e, n)
                if last:
                    high(x, UNITS - 1)

            each_expert(act, expert)
            with act.Fori(0, NB) as b:
                norm.scalar(act, b)

        @block.vector
        def _(dve):
            n = [0]

            def route(ins):
                n[0] += 1
                ins.then_inc(route_s, 1)
                dve.wait_ge(route_s, n[0])

            dve.wait_ge(x_high_s, 1)
            nc.vector.tensor_tensor(x_rest[:], xt[:], x_high[:].bitcast(F32), ALU.subtract).then_inc(x_rest_s, 1)
            dve.wait_ge(lg_psum, 1)
            route(nc.vector.tensor_tensor(logits[:], bank(1)[:, 0:NT * E].rearrange("p (t e) -> p t e", e=E),
                                          rb[:].rearrange("p (a e) -> p a e", a=1).broadcast_to([P, NT, E]), ALU.add))
            for t in range(NT):
                mx = nc.vector.max(top[:, t, :], logits[:, t, :])
            route(mx)
            fourth = top[:, :, K_TOP - 1:K_TOP].broadcast_to([P, NT, E])
            nc.vector.tensor_tensor(gt[:], logits[:], fourth, ALU.is_gt)
            route(nc.vector.tensor_tensor(eq[:], logits[:], fourth, ALU.is_equal))
            route(nc.vector.tensor_reduce(count[:], gt[:], AX, ALU.add))
            route(nc.vector.tensor_tensor_scan(cum[:].rearrange("p t e -> p (t e)"), resets[:], eq[:].rearrange("p t e -> p (t e)"),
                                               0.0, ALU.mult, ALU.add))
            route(nc.vector.tensor_tensor(cum[:], cum[:], count[:].rearrange("p (t a) -> p t a", a=1).broadcast_to([P, NT, E]), ALU.add))
            route(nc.vector.scalar_tensor_tensor(out=sel[:], in0=cum[:], scalar=float(K_TOP), in1=eq[:], op0=ALU.is_le, op1=ALU.mult))
            route(nc.vector.tensor_tensor(sel[:], sel[:], gt[:], ALU.add))
            route(nc.vector.tensor_tensor(cum[:], logits[:], top[:, :, 0:1].broadcast_to([P, NT, E]), ALU.subtract))
            dve.wait_ge(score_s, 1)
            route(nc.vector.tensor_tensor(sel[:], sel[:], eq[:], ALU.mult))
            route(nc.vector.tensor_reduce(count[:], sel[:], AX, ALU.add))
            route(nc.vector.reciprocal(count[:], count[:]))
            nc.vector.tensor_tensor(score[:].rearrange("p e t -> p t e"), sel[:],
                                    count[:].rearrange("p (t a) -> p t a", a=1).broadcast_to([P, NT, E]), ALU.mult).then_inc(score_s, 1)
            dve.wait_ge(bd_psum, 1)
            nc.vector.tensor_tensor(acc[:].rearrange("p b t c -> p (b t c)"), bank(4, 4), xn[:].rearrange("p b t c -> p (b t c)"),
                                    ALU.add).then_inc(acc0_s, 1)
            dve.wait_ge(acc0_s, 1)
            dve.wait_ge(rt_s, 2)
            dve.sem_inc(up_s, 2)
            dve.sem_inc(hid_s, 2)
            dve.sem_inc(acc_s, 4)
            dve.sem_inc(hid_rest_s, 2)

            def expert(x, e, first, last):
                def take(n):
                    w = n % 2
                    dve.wait_ge(gate_psum, x * UNITS + n + 1)
                    nc.vector.tensor_scalar(gate[:, n % 2], bank(2 * (n % 2)), bias2[:, e, w:w + 1], LIMIT, ALU.add, ALU.min).then_inc(gate_s, 1)
                    dve.wait_ge(up_psum, x * UNITS + n + 1)
                    dve.wait_ge(hid_s, x * UNITS + n + 1)
                    nc.vector.tensor_scalar(up[:, n % 2], bank(2 * (n % 2) + 1), bias2[:, e, 2 + w:3 + w], 1.0 - LIMIT, ALU.add,
                                            ALU.max).then_inc(up_s, 1)

                def combine(x, n):
                    dve.wait_ge(gs_s, x * UNITS + n + 1)
                    dve.wait_ge(up_s, x * UNITS + n + 3)
                    dve.wait_ge(hid_rest_s, x * UNITS + n + 1)
                    nc.vector.scalar_tensor_tensor(out=hid[:, n % 2], in0=up[:, n % 2], scalar=1.0 + LIMIT,
                                                   in1=gs[:, n % 2], op0=ALU.min, op1=ALU.mult).then_inc(hid_s, 1)

                def rest(x, n):
                    half, w = n // 2, n % 2
                    part = slice(half * HT, half * HT + HT)
                    dve.wait_ge(hid_high_s, x * UNITS + n + 1)
                    nc.vector.tensor_tensor(hid_rest[:, w, part], hid[:, n % 2], hid_high[:, w, part].bitcast(F32),
                                            ALU.subtract).then_inc(hid_rest_s, 1)

                def accumulate(x, e, k):
                    dve.wait_ge(down_psum, x * 4 + k + 9)
                    dve.wait_ge(acc_s, x * 4 + k + 1)
                    for t in range(TB):
                        add = nc.vector.scalar_tensor_tensor(out=acc[:, k, t, :], in0=bank(4 + k)[:, t * C:t * C + C],
                                                             scalar=score2[:, e, 2 * k + t:2 * k + t + 1], in1=acc[:, k, t, :],
                                                             op0=ALU.mult, op1=ALU.add)
                    add.then_inc(acc_s, 1)

                def finish(x, e):
                    combine(x, 3)
                    rest(x, 2)
                    rest(x, 3)
                    for k in range(4):
                        accumulate(x, e, k)

                if type(x) is not int or x:
                    dve.wait_ge(acc_s, x * 4)
                apart(dve, passed)
                nc.vector.tensor_copy(score2[:, e:e + 1], score[:, bass.ds(x, 1), :])
                nc.vector.tensor_copy(bias2[:, e:e + 1], gubt[:, bass.ds(x, 1), :]).then_inc(stage_s, 1)
                dve.wait_ge(stage_s, x * 2 + 1)
                nc.vector.tensor_scalar(bias2[:, e, 2:4], bias2[:, e, 2:4], 1.0, None, ALU.add).then_inc(stage_s, 1)
                dve.wait_ge(stage_s, x * 2 + 2)
                take(0)
                if not first:
                    finish(x - 1, 1 - e)
                take(1)
                combine(x, 0)
                take(2)
                combine(x, 1)
                rest(x, 0)
                take(3)
                combine(x, 2)
                rest(x, 1)
                if last:
                    finish(x, e)

            each_expert(dve, expert)
            dve.wait_ge(acc_s, 4 * E + 4)
            with dve.Fori(0, NB) as b:
                link = Link(dve, link_s, 3, b)
                norm.vector(dve, link, b, acc[:, b])
                link.close()

        @block.gpsimd
        def _(pool):
            pool.sem_inc(w_rest_s, 6)

            def rest_weights(x, e, part):
                pool.wait_ge(w_high_s, x * 3 + part + 1)
                nc.gpsimd.tensor_tensor(split(w_rest, e, part), raw(e, part), split(w_high, e, part).bitcast(F32),
                                        ALU.subtract).then_inc(w_rest_s, 1)

            for part in range(3):
                rest_weights(0, 0, part)

            def expert(x, e, first, last):
                for n in range(UNITS):
                    pool.wait_ge(sig_s, x * UNITS + n + 1)
                    nc.gpsimd.tensor_tensor(gs[:, n % 2], gate[:, n % 2], sig[:, n % 2], ALU.mult).then_inc(gs_s, 1)
                    if n != 2 and not last:
                        rest_weights(x + 1, 1 - e, min(n, 2))

            each_expert(pool, expert)
            with pool.Fori(0, NB) as b:
                norm.gpsimd(pool, b)

        @block.tensor
        def _(pe):
            pe.wait_ge(small_in, 16 * 5)
            for k in range(CC):
                nc.tensor.transpose(bank(0)[:, k * E:k * E + E], rw[:, k * P:k * P + P], ident[0:E, 0:E])
            for n in range(4):
                w, kind = n % 2, n // 2
                src = gub[:, w * 2 * P:(w + 1) * 2 * P].rearrange("e (p two) -> e two p", two=2)[:, kind, :]
                mm = nc.tensor.transpose(bank(0)[:, (CC + n) * E:(CC + n + 1) * E], src, ident[0:E, 0:E])
            mm.then_inc(rt_psum, 1)
            pe.wait_ge(rt_s, 1)
            for t in range(NT):
                for k in range(CC):
                    mm = nc.tensor.matmul(bank(1)[:, t * E:t * E + E], xt[:, k, t * P:t * P + P], rwt[:, k, :], start=(k == 0), stop=(k == CC - 1))
            mm.then_inc(lg_psum, 1)
            pe.wait_ge(score_s, 2)
            for t in range(NT):
                mm = nc.tensor.transpose(bank(2, 2)[0:E, t * P:t * P + P], score[:, :, t], ident[:])
            mm.then_inc(st_psum, 1)
            pe.wait_ge(st_s, 1)
            for t in range(NT):
                mm = nc.tensor.matmul(bank(4, 4)[:, t * C:t * C + C], score_t[:, t * P:t * P + P], bd[:], start=True, stop=True)
            mm.then_inc(bd_psum, 1)
            pe.wait_ge(acc0_s, 1)
            pe.sem_inc(down_psum, 8)
            pe.wait_ge(x_rest_s, 1)

            def expert(x, e, first, last):
                def project(n):
                    half, w = n // 2, n % 2
                    part = slice(half * HT, half * HT + HT)
                    pe.wait_ge(up_s, x * UNITS + n + 1)
                    for kind, done in ((0, gate_psum), (1, up_psum)):
                        col = slice(kind * F + w * P, kind * F + w * P + P)
                        for k in range(CC):
                            for a, b in ((w_high, x_high), (w_high, x_rest), (w_rest, x_high)):
                                mm = nc.tensor.matmul(bank(2 * (n % 2) + kind), a[:, e, k, col], b[:, k, part],
                                                      start=(k == 0 and b is x_high and a is w_high),
                                                      stop=(k == CC - 1 and a is w_rest))
                        mm.then_inc(done, 1)

                def down(x, e, k):
                    if k == 0:
                        pe.wait_ge(w_rest_s, x * 3 + 9)
                    pe.wait_ge(acc_s, x * 4 + k + 1)
                    pe.wait_ge(hid_rest_s, x * UNITS + (4 if k < 2 else 6))
                    for t in (2 * k, 2 * k + 1):
                        for w in range(2):
                            for a, b in ((hid_high, w_high), (hid_high, w_rest), (hid_rest, w_high)):
                                mm = nc.tensor.matmul(bank(4 + k)[:, t % 2 * C:t % 2 * C + C], a[:, w, t * P:t * P + P],
                                                      b[:, e, 2, w * C:w * C + C], start=(w == 0 and a is hid_high and b is w_high),
                                                      stop=(w == 1 and a is hid_rest))
                    mm.then_inc(down_psum, 1)

                pe.wait_ge(w_rest_s, x * 3 + 8)
                project(0)
                if not first:
                    for k in range(4):
                        down(x - 1, 1 - e, k)
                for n in range(1, UNITS):
                    project(n)
                if last:
                    for k in range(4):
                        down(x, e, k)

            each_expert(pe, expert)
            with pe.Fori(0, NB) as b:
                norm.tensor(pe, b)


def layer1_retention(nc, io, consts, bank, g, out):
    with ExitStack() as ctx:
        layer1_retention_in(nc, io, consts, bank, g, *tools(nc, ctx, "l1r"))


def layer1_retention_in(nc, io, consts, bank, g, sb, sem, dram):
    RH, RD = 4, 64
    ROT = RD // 2
    ident, xn, xt, neg_half = (g[n] for n in ("ident", "xn", "xt", "neg_half"))
    w_nat = sb("w_nat", [P, 10, C])
    w_t = sb("w_t", [P, 10, CC, P])
    xpos = sb("xpos", [P, TB, 2, 2, ROT])
    decay = sb("decay", [P, RH, 3 * P])
    average = sb("average", [P, P])
    gnw, gnb = sb("gnw", [P, 2]), sb("gnb", [P, 2])
    xs_t = sb("xs_t", [P, CC, T])
    qk = sb("qk", [P, TB, 2, RH, RD])
    rot = sb("rot", [P, TB, 2, RH, ROT])
    v = sb("v", [P, TB, RH, RD])
    qk_t = sb("qk_t", [P, 2, 2, T])
    s_t = sb("s_t", [P, RH, 3 * P])
    st6, mom, tot = sb("st6", [P, 2, 6]), sb("mom", [P, 2, 2]), sb("tot", [P, 2, 2])
    msq, vr, aw, ab = (sb(n, [P, 2]) for n in ("msq", "vr", "aw", "ab"))
    ge, gn, gd = (sb(n, [P, 2 * T]) for n in ("ge", "gn", "gd"))
    ret = sb("ret", [P, 2, T])
    norm = Norm(nc, g, sb, bank(7), 3)
    c_in, wt_psum, wt_s = sem("c_in"), sem("wt_psum"), sem("wt_s")
    xs_s, qkv_psum, g_psum, v_s, rot_s, qkt_psum, qkt_s = (
        sem(n) for n in ("xs_s", "qkv_psum", "g_psum", "v_s", "rot_s", "qkt_psum", "qkt_s"))
    sc_psum, st_s, ret_psum, mom_s, tot_psum, gvar_s, gstd_s, gmin_s, gexp_s, ym_s, y_psum, link_s = (
        sem(n) for n in ("sc_psum", "st_s", "ret_psum", "mom_s", "tot_psum", "gvar_s", "gstd_s", "gmin_s", "gexp_s", "ym_s",
                         "y_psum", "link_s"))
    LINKS = 20

    with nc.Block() as block:
        @block.sync
        def _(sp):
            sp.dma_start(w_nat[:, 0:6], io["L1_attn_wqkv"].rearrange("(n p) c -> p n c", p=P)).then_inc(c_in, 16)
            sp.dma_start(w_nat[:, 6:8], io["L1_attn_wg"].rearrange("(n p) c -> p n c", p=P)).then_inc(c_in, 16)
            sp.dma_start(w_nat[:, 8:10], io["L1_attn_wo"].rearrange("(n p) c -> p n c", p=P)).then_inc(c_in, 16)
            sp.dma_start(xpos[:], consts["xpos"]).then_inc(c_in, 16)
            sp.dma_start(decay[:], consts["decay"]).then_inc(c_in, 16)
            sp.dma_start(average[:], consts["average"]).then_inc(c_in, 16)
            for dst, name in ((gnw, "L1_attn_gn_weight"), (gnb, "L1_attn_gn_bias")):
                for half in range(2):
                    src = io[name].rearrange("(a k two) -> a two k", a=1, two=2)[:, half, :]
                    sp.dma_start(dst[RD * half:RD * half + RD, :], src.broadcast_to([RD, 2]), allow_slow_non_contiguous=True).then_inc(c_in, 16)

        @block.scalar
        def _(act):
            for n in range(5):
                act.wait_ge(wt_psum, n + 1)
                nc.scalar.copy(w_t[:, 2 * n:2 * n + 2].rearrange("p n k c -> p (n k c)"), bank(n)).then_inc(wt_s, 1)
            with act.Fori(0, NB) as b:
                nc.scalar.copy(xs_t[:], xt[:, :, bass.ds(b * T, T)]).then_inc(xs_s, 1)
                for t in range(TB):
                    act.wait_ge(qkv_psum, b * TB + t + 1)
                    src = bank(2 * t, 2)[:, 0:3 * C].rearrange("p (h x d) -> p x h d", h=RH, x=3)
                    nc.scalar.copy(v[:, t], src[:, 2])
                    nc.scalar.copy(qk[:, t, :, :, ROT:RD], src[:, 0:2, :, ROT:RD]).then_inc(v_s, 1)
                act.wait_ge(gmin_s, b + 1)
                nc.scalar.activation(ge[:], gd[:], ACT.Exp).then_inc(gexp_s, 1)
                act.wait_ge(qkt_psum, b + 1)
                nc.scalar.copy(qk_t[:].rearrange("p x k t -> p (x k t)"), bank(5, 2)).then_inc(qkt_s, 1)
                norm.scalar(act, b)

        @block.vector
        def _(dve):
            dve.wait_ge(c_in, 16 * 10)
            with dve.Fori(0, NB) as b:
                link = Link(dve, link_s, LINKS, b)
                for t in range(TB):
                    dve.wait_ge(v_s, b * TB + t + 1)
                    src = bank(2 * t, 2)[:, 0:3 * C].rearrange("p (h x d) -> p x h d", h=RH, x=3)[:, 0:2, :, 0:ROT]
                    for x in range(2):
                        tab = xpos[:, t, x:x + 1]
                        nc.vector.tensor_tensor(qk[:, t, x, :, 0:ROT], src[:, x], tab[:, :, 0, :].broadcast_to([P, RH, ROT]), ALU.mult)
                        pair = src[:, x].rearrange("p h (n two) -> p h n two", two=2)
                        dst = rot[:, t, x].rearrange("p h (n two) -> p h n two", two=2)
                        sin = tab[:, :, 1, :].rearrange("p a (n two) -> p a n two", two=2)
                        for one in range(2):
                            mul = nc.vector.tensor_tensor(dst[:, :, :, one], pair[:, :, :, 1 - one],
                                                          sin[:, :, :, one].broadcast_to([P, RH, ROT // 2]), ALU.mult)
                    link(mul)
                    add = nc.vector.tensor_tensor(qk[:, t, :, :, 0:ROT], qk[:, t, :, :, 0:ROT], rot[:, t], ALU.add)
                add.then_inc(rot_s, 1)
                dve.wait_ge(g_psum, b + 1)
                nc.vector.tensor_scalar(gd[:], bank(4), 20.0, None, ALU.min).then_inc(gmin_s, 1)
                for h in range(RH):
                    dve.wait_ge(sc_psum, b * RH + h + 1)
                    nc.vector.tensor_tensor(s_t[:, h], bank(h)[:, 0:3 * P], decay[:, h], ALU.mult).then_inc(st_s, 1)
                dve.wait_ge(gexp_s, b + 1)
                link(nc.vector.scalar_tensor_tensor(out=gn[:], in0=ge[:], scalar=2.0, in1=ge[:], op0=ALU.add, op1=ALU.mult))
                link(nc.vector.tensor_scalar(gd[:], gn[:], 2.0, None, ALU.add))
                link(nc.vector.reciprocal(ge[:], gd[:]))
                link(nc.vector.tensor_tensor(gn[:], gn[:], ge[:], ALU.mult))
                link(nc.vector.tensor_tensor(gn[:], gn[:], bank(4), ALU.mult))
                dve.wait_ge(ret_psum, b + 1)
                for k in range(2):
                    bs = nc.vector.bn_stats(st6[:, k], bank(5)[:, k * T:k * T + T])
                link(bs)
                apart(dve, norm.passed)
                for k in range(2):
                    ag = nc.vector.bn_aggr(mom[:, k], st6[:, k])
                link(ag)
                link(nc.vector.tensor_tensor(msq[:], mom[:, :, 0], mom[:, :, 0], ALU.mult))
                nc.vector.tensor_tensor(mom[:, :, 1], mom[:, :, 1], msq[:], ALU.add).then_inc(mom_s, 1)
                dve.wait_ge(tot_psum, b + 1)
                link(nc.vector.tensor_copy(tot[:].rearrange("p k m -> p (k m)"), bank(6)[:, 0:4]))
                link(nc.vector.tensor_tensor(msq[:], tot[:, :, 0], tot[:, :, 0], ALU.mult))
                nc.vector.scalar_tensor_tensor(out=vr[:], in0=tot[:, :, 1], scalar=LN_EPS, in1=msq[:], op0=ALU.add,
                                               op1=ALU.subtract).then_inc(gvar_s, 1)
                dve.wait_ge(gstd_s, b + 1)
                link(nc.vector.tensor_tensor(aw[:], vr[:], gnw[:], ALU.mult))
                link(nc.vector.tensor_tensor(ab[:], tot[:, :, 0], aw[:], ALU.mult))
                link(nc.vector.tensor_tensor(ab[:], gnb[:], ab[:], ALU.subtract))
                for k in range(2):
                    ts = nc.vector.tensor_scalar(ret[:, k], bank(5)[:, k * T:k * T + T], aw[:, k:k + 1], ab[:, k:k + 1], ALU.mult, ALU.add)
                link(ts)
                nc.vector.tensor_tensor(ret[:].rearrange("p k t -> p (k t)"), ret[:].rearrange("p k t -> p (k t)"), gn[:],
                                        ALU.mult).then_inc(ym_s, 1)
                dve.wait_ge(y_psum, b + 1)
                y2 = bank(0, 2).rearrange("p (t c) -> p t c", t=TB)[:, :, 0:C]
                link(nc.vector.tensor_tensor(norm.y[:], y2, xn[:, b], ALU.add))
                norm.vector(dve, link, b, norm.y)
                link.close()

        @block.gpsimd
        def _(pool):
            with pool.Fori(0, NB) as b:
                pool.wait_ge(gvar_s, b + 1)
                nc.gpsimd.tensor_tensor(vr[:], vr[:], neg_half[:, 0:2], ALU.pow).then_inc(gstd_s, 1)
                norm.gpsimd(pool, b)

        @block.tensor
        def _(pe):
            pe.wait_ge(c_in, 16 * 10)
            for n in range(10):
                for k in range(CC):
                    mm = nc.tensor.transpose(bank(n // 2)[:, (n % 2) * C + k * P:(n % 2) * C + k * P + P], w_nat[:, n, k * P:k * P + P], ident[:])
                if n % 2:
                    mm.then_inc(wt_psum, 1)
            pe.wait_ge(wt_s, 5)
            with pe.Fori(0, NB) as b:
                pe.wait_ge(xs_s, b + 1)
                for t in range(TB):
                    for n0, n1 in ((0, 4), (4, 6)):
                        for k in range(CC):
                            mm = nc.tensor.matmul(bank(2 * t, 2)[:, n0 * P:n1 * P], xs_t[:, k, t * P:t * P + P], w_t[:, n0:n1, k, :],
                                                  start=(k == 0), stop=(k == CC - 1))
                    mm.then_inc(qkv_psum, 1)
                for n in range(2):
                    for k in range(CC):
                        mm = nc.tensor.matmul(bank(4)[:, n * T:n * T + T], w_t[:, 6 + n, k, :], xs_t[:, k, :], start=(k == 0), stop=(k == CC - 1))
                mm.then_inc(g_psum, 1)
                pe.wait_ge(rot_s, b + 1)
                for x in range(2):
                    for k in range(2):
                        for t in range(TB):
                            mm = nc.tensor.transpose(bank(5 + x)[:, k * T + t * P:k * T + t * P + P],
                                                     qk[:, t, x, 2 * k:2 * k + 2, :].rearrange("p h d -> p (h d)"), ident[:])
                mm.then_inc(qkt_psum, 1)
                pe.wait_ge(qkt_s, b + 1)
                for h in range(RH):
                    rows, k = slice(RD * (h % 2), RD * (h % 2) + RD), h // 2
                    nc.tensor.matmul(bank(h)[:, 0:T], qk_t[rows, 1, k, 0:P], qk_t[rows, 0, k, :], start=True, stop=True)
                    mm = nc.tensor.matmul(bank(h)[:, T:T + P], qk_t[rows, 1, k, P:T], qk_t[rows, 0, k, P:T], start=True, stop=True)
                    mm.then_inc(sc_psum, 1)
                for h in range(RH):
                    pe.wait_ge(st_s, b * RH + h + 1)
                    rows, k = slice(RD * (h % 2), RD * (h % 2) + RD), h // 2
                    dst = bank(5)[rows, k * T:k * T + T]
                    nc.tensor.matmul(dst, v[:, 0, h, :], s_t[:, h, 0:T], start=True, stop=False, tile_position=(0, RD * (h % 2)))
                    mm = nc.tensor.matmul(dst[:, P:T], v[:, 1, h, :], s_t[:, h, T:T + P], start=False, stop=True,
                                          tile_position=(0, RD * (h % 2)))
                mm.then_inc(ret_psum, 1)
                pe.wait_ge(mom_s, b + 1)
                nc.tensor.matmul(bank(6)[:, 0:4], average[:], mom[:].rearrange("p k m -> p (k m)"), start=True, stop=True).then_inc(tot_psum, 1)
                pe.wait_ge(ym_s, b + 1)
                for t in range(TB):
                    for k in range(2):
                        mm = nc.tensor.matmul(bank(t)[:, 0:C], ret[:, k, t * P:t * P + P], w_t[:, 8:10, k, :], start=(k == 0), stop=(k == 1))
                mm.then_inc(y_psum, 1)
                norm.tensor(pe, b)


def layer1_recurrence(nc, io, consts, bank, g, out):
    with ExitStack() as ctx:
        layer1_recurrence_in(nc, io, bank, g, *tools(nc, ctx, "l1w"))


def layer1_recurrence_in(nc, io, bank, g, sb, sem, dram):
    START = -1.0e38
    ident, xn, xt, ct = (g[n] for n in ("ident", "xn", "xt", "ct"))
    w, u = sb("w", [P, CC]), sb("u", [P, CC])
    o1, p1, q1 = (sb(n, [P, CC, T + 1]) for n in ("o1", "p1", "q1"))
    uk, top = sb("uk", [P, CC, T]), sb("top", [P, CC, T])
    e4 = sb("e4", [P, 4, CC, T])
    pv, ev = sb("pv", [P, CC, T]), sb("ev", [P, CC, T])
    num, dnm = sb("num", [P, CC, T]), sb("dnm", [P, CC, T])
    y_t = sb("y_t", [P, CC, T])
    norm = Norm(nc, g, sb, bank(6), 4)
    c_in, set_s, uk_s, o_s, exps_s, exp_s, ev_s, pv_s, yt_s, y_psum, link_s = (
        sem(n) for n in ("c_in", "set_s", "uk_s", "o_s", "exps_s", "exp_s", "ev_s", "pv_s", "yt_s", "y_psum", "link_s"))
    LINKS = 13

    with nc.Block() as block:
        @block.sync
        def _(sp):
            with nc.allow_non_contiguous_dma("two short vectors"):
                sp.dma_start(w[:], io["L1_xattn_w"].rearrange("(k p) -> p k", p=P)).then_inc(c_in, 16)
                sp.dma_start(u[:], io["L1_xattn_u"].rearrange("(k p) -> p k", p=P)).then_inc(c_in, 16)

        @block.scalar
        def _(act):
            with act.Fori(0, NB) as b:
                act.wait_ge(exps_s, b + 1)
                nc.scalar.activation(e4[:].rearrange("p n k t -> p (n k t)"), e4[:].rearrange("p n k t -> p (n k t)"), ACT.Exp).then_inc(exp_s, 1)
                norm.scalar(act, b)

        @block.vector
        def _(dve):
            nc.vector.memset(o1[:, :, 0:1], START).then_inc(set_s, 1)
            nc.vector.memset(p1[:, :, 0:1], 0.0).then_inc(set_s, 1)
            nc.vector.memset(q1[:, :, 0:1], 0.0).then_inc(set_s, 1)
            dve.wait_ge(set_s, 3)
            dve.wait_ge(c_in, 32)
            dve.sem_inc(yt_s, 1)
            with dve.Fori(0, NB) as b:
                link = Link(dve, link_s, LINKS, b)
                kt = xt[:, :, bass.ds(b * T, T)]
                vt = ct[:, b]
                before = o1[:, :, 0:T]
                for k in range(CC):
                    sc = nc.vector.tensor_tensor_scan(o1[:, k, 1:T + 1], w[:, k:k + 1].broadcast_to([P, T]), kt[:, k, :], START, ALU.add, ALU.max)
                link(sc)
                dve.wait_ge(uk_s, b + 1)
                link(nc.vector.tensor_tensor(top[:], before, uk[:], ALU.max))
                nc.vector.tensor_tensor(e4[:, 0], before, top[:], ALU.subtract)
                nc.vector.tensor_tensor(e4[:, 1], uk[:], top[:], ALU.subtract)
                for k in range(CC):
                    nc.vector.scalar_tensor_tensor(out=e4[:, 2, k], in0=o1[:, k, 0:T], scalar=w[:, k:k + 1], in1=o1[:, k, 1:T + 1],
                                                   op0=ALU.add, op1=ALU.subtract)
                nc.vector.tensor_tensor(e4[:, 3], kt, o1[:, :, 1:T + 1], ALU.subtract).then_inc(exps_s, 1)
                dve.wait_ge(exp_s, b + 1)
                for k in range(CC):
                    sc = nc.vector.tensor_tensor_scan(q1[:, k, 1:T + 1], e4[:, 2, k], e4[:, 3, k], 0.0, ALU.mult, ALU.add)
                link(sc)
                link(nc.vector.tensor_tensor(dnm[:], e4[:, 0], q1[:, :, 0:T], ALU.mult))
                link(nc.vector.tensor_tensor(dnm[:], dnm[:], e4[:, 1], ALU.add))
                link(nc.vector.reciprocal(dnm[:], dnm[:]))
                dve.wait_ge(pv_s, b + 1)
                for k in range(CC):
                    sc = nc.vector.tensor_tensor_scan(p1[:, k, 1:T + 1], e4[:, 2, k], pv[:, k], 0.0, ALU.mult, ALU.add)
                link(sc)
                link(nc.vector.tensor_tensor(num[:], e4[:, 0], p1[:, :, 0:T], ALU.mult))
                dve.wait_ge(ev_s, b + 1)
                link(nc.vector.tensor_tensor(num[:], num[:], ev[:], ALU.add))
                nc.vector.tensor_tensor(y_t[:], num[:], dnm[:], ALU.mult).then_inc(yt_s, 1)
                dve.wait_ge(y_psum, b + 1)
                dve.wait_ge(yt_s, b + 2)
                link(nc.vector.tensor_tensor(norm.y[:].rearrange("p t c -> p (t c)"), bank(0), xn[:, b].rearrange("p t c -> p (t c)"), ALU.add))
                norm.vector(dve, link, b, norm.y)
                link.close()

        @block.gpsimd
        def _(pool):
            pool.wait_ge(c_in, 32)
            with pool.Fori(0, NB) as b:
                pool.wait_ge(yt_s, b + 1)
                ub = u[:].rearrange("p (k a) -> p k a", a=1).broadcast_to([P, CC, T])
                nc.gpsimd.tensor_tensor(uk[:], xt[:, :, bass.ds(b * T, T)], ub, ALU.add).then_inc(uk_s, 1)
                pool.wait_ge(exp_s, b + 1)
                nc.gpsimd.tensor_tensor(pv[:], e4[:, 3], ct[:, b], ALU.mult).then_inc(pv_s, 1)
                nc.gpsimd.tensor_tensor(ev[:], e4[:, 1], ct[:, b], ALU.mult).then_inc(ev_s, 1)
                norm.gpsimd(pool, b)

        @block.tensor
        def _(pe):
            with pe.Fori(0, NB) as b:
                pe.wait_ge(yt_s, b + 2)
                for t in range(TB):
                    for k in range(CC):
                        mm = nc.tensor.transpose(bank(0)[:, t * C + k * P:t * C + k * P + P], y_t[:, k, t * P:t * P + P], ident[:])
                mm.then_inc(y_psum, 1)
                norm.tensor(pe, b)


def layer1_mixed_experts(nc, io, consts, bank, g, out):
    with ExitStack() as ctx:
        layer1_mixed_experts_in(nc, io, consts, bank, g, out, *tools(nc, ctx, "l1m"))


def layer1_mixed_experts_in(nc, io, consts, bank, g, out, sb, sem, dram):
    E, EH = 32, 64
    KE = E * EH // P
    TOP = E // 2
    GONE = -3.0e38
    ident, xn, xt, neg_half = (g[n] for n in ("ident", "xn", "xt", "neg_half"))
    wv, wo = sb("wv", [P, KE, C]), sb("wo", [P, KE, C])
    sim, sim2 = sb("sim", [P, CC, E]), sb("sim2", [P, CC, E])
    gates = sb("gates", [NB, E])
    ones = sb("ones", [P, NB])
    halves, fold, pick = sb("halves", [E, P]), sb("fold", [P, EH]), sb("pick", [E, KE])
    mean, mean2 = sb("mean", [P, CC, NB]), sb("mean2", [P, CC, NB])
    sq, rn = sb("sq", [NB, 1 + E]), sb("rn", [NB, 1 + E])
    raw, lg, gated, mask, fb, ra, rb2 = (sb(n, [NB, E]) for n in ("raw", "lg", "gated", "mask", "fb", "ra", "rb2"))
    top = sb("top", [NB, 2, 8])
    one = sb("one", [NB, 4])
    r_t, r_d, r_p = sb("r_t", [E, NB]), sb("r_d", [E, KE, NB]), sb("r_p", [P, KE, NB])
    mix = sb("mix", [P, KE, NB, EH])
    sums = sb("sums", [P, 2, 2, C])
    m = sb("m", [P, NB, CC, C])
    y, fin = sb("y", [P, NB, TB, C]), sb("fin", [P, NB, TB, C])
    stats, mv, rstd = sb("stats", [P, NB, TB, 6]), sb("mv", [P, NB, TB, 2]), sb("rstd", [P, NB * TB])
    s_in, w_in, mean_s, aff_psum, sq_s, rn_s, ex_s, exx_s, r_s, rt_psum, rt_s, rp_psum, mix_s = (
        sem(n) for n in ("s_in", "w_in", "mean_s", "aff_psum", "sq_s", "rn_s", "ex_s", "exx_s", "r_s", "rt_psum", "rt_s",
                         "rp_psum", "mix_s"))
    sum_psum, sum_s, m_psum, m_s, y_psum, var_s, rstd_s, fin_s, out_s, chain = (
        sem(n) for n in ("sum_psum", "sum_s", "m_psum", "m_s", "y_psum", "var_s", "rstd_s", "fin_s", "out_s", "chain"))

    with nc.Block() as block:
        @block.sync
        def _(sp):
            sp.dma_start(sim[:], io["L1_ffn_sim_matrix"].rearrange("(k p) e -> p k e", p=P)).then_inc(s_in, 16)
            sp.dma_start(gates[:], io["L1_ffn_gates"].rearrange("(a e) -> a e", a=1).broadcast_to([NB, E])).then_inc(s_in, 16)
            sp.dma_start(halves[:], consts["halves"]).then_inc(s_in, 16)
            sp.dma_start(fold[:], consts["fold"]).then_inc(s_in, 16)
            sp.dma_start(pick[:], consts["pick"]).then_inc(s_in, 16)
            sp.dma_start(wv[:], io["L1_ffn_w_v"].rearrange("(k e) h c -> (e h) k c", e=2)).then_inc(w_in, 16)
            sp.dma_start(wo[:], io["L1_ffn_o_weights"].rearrange("(k e) h c -> (e h) k c", e=2)).then_inc(w_in, 16)
            for b in range(NB):
                sp.wait_ge(fin_s, b + 1)
                sp.dma_start(out[b].rearrange("(t p) c -> p t c", p=P), fin[:, b]).then_inc(out_s, 16)
            sp.wait_ge(out_s, 16 * NB)

        @block.scalar
        def _(act):
            act.wait_ge(s_in, 16 * 5)
            nc.scalar.activation(gates[:], gates[:], ACT.Sigmoid).then_inc(exx_s, 1)
            act.wait_ge(ex_s, 1)
            nc.scalar.activation(ra[:], ra[:], ACT.Exp).then_inc(exx_s, 1)
            for n in range(4):
                act.wait_ge(sum_psum, n + 1)
                nc.scalar.copy(sums[:, n % 2, n // 2], bank(n)[:, 0:C]).then_inc(sum_s, 1)
            for b in range(NB):
                act.wait_ge(m_psum, b + 1)
                nc.scalar.copy(m[:, b].rearrange("p k c -> p (k c)"), bank(4 + b)).then_inc(m_s, 1)

        @block.vector
        def _(dve):
            n = [0]

            def step(ins):
                n[0] += 1
                ins.then_inc(chain, 1)
                dve.wait_ge(chain, n[0])

            step(nc.vector.memset(ones[:], 1.0))
            dve.wait_ge(s_in, 16 * 5)
            nc.vector.tensor_tensor(sim2[:], sim[:], sim[:], ALU.mult)
            step(nc.vector.tensor_reduce(mean[:], xt[:].rearrange("p k (b t) -> p k b t", b=NB), AX, ALU.add))
            step(nc.vector.tensor_scalar(mean[:], mean[:], 1.0 / T, None, ALU.mult))
            nc.vector.tensor_tensor(mean2[:], mean[:], mean[:], ALU.mult).then_inc(mean_s, 1)
            dve.wait_ge(aff_psum, 1)
            nc.vector.tensor_copy(raw[:], bank(0)[0:NB, 0:E])
            nc.vector.tensor_copy(sq[:], bank(0)[0:NB, E:2 * E + 1]).then_inc(sq_s, 1)
            dve.wait_ge(rn_s, 1)
            step(nc.vector.tensor_scalar(raw[:], raw[:], rn[:, E:E + 1], None, ALU.mult))
            step(nc.vector.tensor_tensor(raw[:], raw[:], rn[:, 0:E], ALU.mult))
            dve.wait_ge(exx_s, 1)
            step(nc.vector.tensor_tensor(lg[:], raw[:], gates[:], ALU.subtract))
            step(nc.vector.tensor_scalar(gated[:], lg[:], 0.0, None, ALU.max))
            step(nc.vector.tensor_scalar(mask[:], gated[:], 0.0, None, ALU.is_gt))
            step(nc.vector.tensor_reduce(one[:, 0:1], mask[:], AX, ALU.max))
            step(nc.vector.tensor_scalar(one[:, 0:1], one[:, 0:1], 0.0, None, ALU.is_equal))
            step(nc.vector.max(top[:, 0], lg[:]))
            step(nc.vector.match_replace(fb[:], top[:, 0], lg[:], GONE))
            step(nc.vector.max(top[:, 1], fb[:]))
            step(nc.vector.match_replace(fb[:], top[:, 1], fb[:], GONE))
            step(nc.vector.tensor_scalar(fb[:], fb[:], GONE, one[:, 0:1], ALU.is_equal, ALU.mult))
            step(nc.vector.tensor_tensor(mask[:], mask[:], fb[:], ALU.max))
            step(nc.vector.tensor_reduce(one[:, 1:2], gated[:], AX, ALU.max))
            nc.vector.tensor_scalar(ra[:], gated[:], one[:, 1:2], None, ALU.subtract).then_inc(ex_s, 1)
            dve.wait_ge(exx_s, 2)
            step(nc.vector.tensor_tensor(ra[:], ra[:], mask[:], ALU.mult))
            step(nc.vector.tensor_reduce(one[:, 2:3], ra[:], AX, ALU.add))
            step(nc.vector.reciprocal(one[:, 3:4], one[:, 2:3]))
            nc.vector.tensor_scalar(rb2[:], ra[:], one[:, 3:4], None, ALU.mult).then_inc(r_s, 1)
            dve.wait_ge(rt_psum, 1)
            step(nc.vector.tensor_copy(r_t[:], bank(1)[0:E, 0:NB]))
            nc.vector.tensor_tensor(r_d[:], r_t[:].rearrange("e (a b) -> e a b", a=1).broadcast_to([E, KE, NB]),
                                    pick[:].rearrange("e (k a) -> e k a", a=1).broadcast_to([E, KE, NB]), ALU.mult).then_inc(rt_s, 1)
            dve.wait_ge(rp_psum, 1)
            step(nc.vector.tensor_copy(r_p[:].rearrange("p k b -> p (k b)"), bank(1)[:, 64:64 + KE * NB]))
            for k in range(0, KE, 4):
                nc.vector.tensor_tensor(mix[:, k:k + 4].rearrange("p k b h -> p (k b) h"),
                                        r_p[:, k:k + 4].rearrange("p k (b a) -> p (k b) a", a=1).broadcast_to([P, 4 * NB, EH]),
                                        fold[:].rearrange("p (a h) -> p a h", a=1).broadcast_to([P, 4 * NB, EH]), ALU.mult).then_inc(mix_s, 1)
            for b in range(NB):
                dve.wait_ge(y_psum, b + 1)
                step(nc.vector.tensor_tensor(y[:, b].rearrange("p t c -> p (t c)"), bank(b), xn[:, b].rearrange("p t c -> p (t c)"), ALU.add))
                for t in range(TB):
                    st = nc.vector.bn_stats(stats[:, b, t], y[:, b, t])
                step(st)
                for t in range(TB):
                    ag = nc.vector.bn_aggr(mv[:, b, t], stats[:, b, t])
                step(ag)
                nc.vector.tensor_scalar(rstd[:, 2 * b:2 * b + 2], mv[:, b, :, 1], LN_EPS, None, ALU.add).then_inc(var_s, 1)
                dve.wait_ge(rstd_s, b + 1)
                for t in range(TB):
                    ts = nc.vector.tensor_scalar(fin[:, b, t], y[:, b, t], mv[:, b, t, 0:1], rstd[:, 2 * b + t:2 * b + t + 1],
                                                 ALU.subtract, ALU.mult)
                ts.then_inc(fin_s, 1)

        @block.gpsimd
        def _(pool):
            pool.wait_ge(sq_s, 1)
            nc.gpsimd.tensor_tensor(rn[:], sq[:], neg_half[0:NB, 0:1].broadcast_to([NB, 1 + E]), ALU.pow).then_inc(rn_s, 1)
            for b in range(NB):
                pool.wait_ge(var_s, b + 1)
                nc.gpsimd.tensor_tensor(rstd[:, 2 * b:2 * b + 2], rstd[:, 2 * b:2 * b + 2], neg_half[:, 0:TB], ALU.pow).then_inc(rstd_s, 1)

        @block.tensor
        def _(pe):
            pe.wait_ge(mean_s, 1)
            for dst, lhs, rhs in ((bank(0)[0:NB, 0:E], mean, sim), (bank(0)[0:NB, E:2 * E], None, sim2),
                                  (bank(0)[0:NB, 2 * E:2 * E + 1], mean2, None)):
                for k in range(CC):
                    mm = nc.tensor.matmul(dst, ones[:] if lhs is None else lhs[:, k], ones[:, 0:1] if rhs is None else rhs[:, k],
                                          start=(k == 0), stop=(k == CC - 1))
            mm.then_inc(aff_psum, 1)
            pe.wait_ge(r_s, 1)
            nc.tensor.transpose(bank(1)[0:E, 0:NB], rb2[:], ident[0:NB, 0:NB]).then_inc(rt_psum, 1)
            pe.wait_ge(rt_s, 1)
            nc.tensor.matmul(bank(1)[:, 64:64 + KE * NB], halves[:], r_d[:].rearrange("e k b -> e (k b)"), start=True, stop=True).then_inc(rp_psum, 1)
            pe.wait_ge(w_in, 32)
            pe.wait_ge(mix_s, KE // 4)
            for n in range(4):
                pair, w = n // 2, (wv, wo)[n % 2]
                for k in range(KE):
                    mm = nc.tensor.matmul(bank(n)[:, 0:C], mix[:, k, 2 * pair:2 * pair + 2].rearrange("p b h -> p (b h)"), w[:, k],
                                          start=(k == 0), stop=(k == KE - 1))
                mm.then_inc(sum_psum, 1)
            for b in range(NB):
                pe.wait_ge(sum_s, 2 * (b // 2) + 2)
                rows = slice(EH * (b % 2), EH * (b % 2) + EH)
                for k in range(CC):
                    mm = nc.tensor.matmul(bank(4 + b)[:, k * C:k * C + C], sums[rows, 0, b // 2, k * P:k * P + P], sums[rows, 1, b // 2, :],
                                          start=True, stop=True)
                mm.then_inc(m_psum, 1)
            for b in range(NB):
                pe.wait_ge(m_s, b + 1)
                for t in range(TB):
                    for k in range(CC):
                        mm = nc.tensor.matmul(bank(b)[:, t * C:t * C + C], xt[:, k, b * T + t * P:b * T + t * P + P], m[:, b, k],
                                              start=(k == 0), stop=(k == CC - 1))
                mm.then_inc(y_psum, 1)


_OUT = (NB, T, C)


def kernel(**inputs):
    import concourse.bacc as bacc
    from concourse.bass_utils import run_bass_kernel_spmd

    nc = bacc.Bacc("TRN2", target_bir_lowering=False, num_devices=1)
    arrays, io = {}, {}
    for name, a in inputs.items():
        a = np.ascontiguousarray(a)
        arrays[f"in_{name}"] = a
        io[name] = nc.dram_tensor(f"in_{name}", a.shape, mybir.dt.from_np(a.dtype), kind="ExternalInput").ap()
    consts = {}
    for name, a in constants().items():
        arrays[f"const_{name}"] = a
        consts[name] = nc.dram_tensor(f"const_{name}", a.shape, mybir.dt.from_np(a.dtype), kind="ExternalInput").ap()
    out = nc.dram_tensor("out", _OUT, F32, kind="ExternalOutput").ap()
    build(nc, io, consts, out)
    return run_bass_kernel_spmd(nc, [arrays], core_ids=[0]).results[0]["out"]
```

```python
from contextlib import ExitStack

import numpy as np

import concourse.bass as bass
from concourse import mybir
from concourse.alu_op_type import AluOpType as ALU

ACT = mybir.ActivationFunctionType
F32 = mybir.dt.float32
BF16 = mybir.dt.bfloat16
F32R = mybir.dt.float32r
I32 = mybir.dt.int32
AX = mybir.AxisListType.X

P = 128
NB, T, C = 4, 256, 256
TB = T // P
CC = C // P
H, D = 16, 16
NP = H // 2
Q = 32
NQ = P // Q
LN_EPS = 1e-5
NEG = -1.0e30
FLOOR = -1.0e28
SLOTS = (0, 1, 4), (2, 3), (5,)
SLOTS_B = (0, 2, 5), (1, 3), (4,)


class Link:

    def __init__(self, eng, sem, per, it):
        self.eng, self.sem, self.per, self.it, self.n = eng, sem, per, it, 0

    def __call__(self, ins, behind=0):
        self.n += 1
        ins.then_inc(self.sem, 1)
        self.eng.wait_ge(self.sem, self.it * self.per + self.n - behind)

    def wait(self):
        self.eng.wait_ge(self.sem, self.it * self.per + self.n)

    def close(self):
        assert self.n == self.per, ("links", self.n, self.per)


def apart(eng, passed):
    eng.sem_inc(passed, 1)


def deferred(eng, stage, norm):
    stage(0, False)
    with eng.Fori(1, NB) as b:
        stage(b, True)
    norm(NB - 1)


def constants():
    f32 = np.float32
    half = D // 2
    inv = (f32(1.0) / np.power(f32(10000.0), np.arange(half, dtype=f32) / f32(half), dtype=f32)).astype(f32)
    ang = (np.arange(T, dtype=f32)[:, None] * inv[None, :]).astype(f32)
    cos, sin = np.cos(ang).astype(f32), np.sin(ang).astype(f32)
    rope = np.concatenate([cos, cos, -sin, sin], 1).reshape(TB, P, 4 * half).transpose(1, 0, 2)
    out = {"ident": np.eye(P, dtype=f32), "rope": np.ascontiguousarray(rope)}
    i, j = np.arange(P)[:, None], np.arange(P)[None, :]
    masks = np.zeros((P, 4, 2, P), f32)
    for n, ok in enumerate((j < i, j <= i, i < j, i <= j)):
        masks[:, n] = np.where(ok, 0.0, NEG)[:, None, :]
    out["masks"] = masks.reshape(P, -1)
    resets = np.ones((P, NB * TB, 16), f32)
    resets[:, :, 0] = 0.0
    out["resets"] = resets.reshape(P, -1)
    dim, heads = 32, 4
    inv = (f32(1.0) / np.power(f32(10000.0), np.arange(0, dim, 2, dtype=f32) / f32(dim), dtype=f32)).astype(f32)
    t = np.arange(T, dtype=f32)
    ang = np.repeat((t[:, None] * inv[None, :]).astype(f32), 2, axis=-1)
    base = ((np.arange(0, dim, 2, dtype=f32) + f32(0.4 * dim)) / f32(1.4 * dim)).astype(f32)
    scale = np.power(base[None, :], ((t - T // 2) / f32(512.0))[:, None], dtype=f32)
    scale = np.concatenate([scale, scale], axis=-1)
    sign = np.where(np.arange(dim) % 2, f32(1.0), f32(-1.0))
    xpos = np.stack([np.stack([np.cos(ang) * sc, np.sin(ang) * sc * sign], 1) for sc in (scale, f32(1.0) / scale)], 1)
    out["xpos"] = np.ascontiguousarray(xpos.astype(f32).reshape(TB, P, 2, 2, dim).transpose(1, 0, 2, 3, 4))
    gamma = (1.0 - 2.0 ** (-5.0 - np.arange(heads))).astype(f32)
    q, k = np.arange(T), np.arange(T)[:, None]
    dist = np.maximum(q - k, 0).astype(f32)
    full = np.stack([np.where(q >= k, np.power(gm, dist, dtype=f32), f32(0.0)) for gm in gamma], 1).astype(f32)
    out["decay"] = np.ascontiguousarray(np.concatenate([full[:P], full[P:, :, P:]], axis=-1))
    out["average"] = np.kron(np.eye(2, dtype=f32), np.full((64, 64), 1.0 / 64, f32))
    p2 = np.arange(P)
    out["halves"] = (np.arange(32)[:, None] % 2 == p2[None, :] // 64).astype(f32)
    out["fold"] = (p2[:, None] % 64 == np.arange(64)[None, :]).astype(f32)
    out["pick"] = (np.arange(32)[:, None] // 2 == np.arange(16)[None, :]).astype(f32)
    out["eye32"] = np.tile(np.eye(Q, dtype=f32).reshape(1, -1), (P, 1))
    return out


def build(nc, io, consts, out, debug=None):
    with ExitStack() as ctx:
        def sb(name, shape, dt=F32):
            return ctx.enter_context(nc.sbuf_tensor(name, shape, dt))

        ps = ctx.enter_context(nc.psum_tensor("ps", [P, 8 * 512], F32))

        def bank(n, k=1):
            return ps[:, 512 * n:512 * (n + k)]

        g = {
            "ident": sb("ident", [P, P]), "neg_half": sb("neg_half", [P, 8]),
            "xn": sb("xn", [P, NB, TB, C]), "xt": sb("xt", [P, CC, NB * T]),
            "ct": sb("ct", [P, NB, CC, T]),
        }
        g["passed"] = ctx.enter_context(nc.semaphore("passed"))
        g["ready"] = ctx.enter_context(nc.semaphore("ready"))
        g["norm_sems"] = [ctx.enter_context(nc.semaphore(f"norm_{n}")) for n in ("var_s", "rstd_s", "ys_s", "turn_s", "xt_s", "link_s")]
        def layer(run, stage):
            run(nc, io, consts, bank, g, out)
            if debug != stage or stage == "all":
                return True
            with nc.semaphore("finish") as finish, nc.Block() as block:
                @block.sync
                def _(sp):
                    sp.dma_start(out.rearrange("b (t p) c -> p b t c", p=P), g["xn"][:]).then_inc(finish, 16)
                    sp.wait_ge(finish, 16)
            return False

        if not layer(layer0_attention, "attn"):
            return
        with ExitStack() as early:
            g["routed"] = routed_inputs(io, consts, *tools(nc, early, "l0f"))
            if not layer(layer0_experts_by_token, "xattn"):
                return
            with ExitStack() as later:
                g["retention"] = retention_inputs(io, consts, *tools(nc, later, "l1r"))
                if not layer(layer0_experts_by_router, "ffn"):
                    return
                g["mixed"] = mixed_inputs(io, consts, *tools(nc, later, "l1m"))
                for run, stage in ((layer1_retention, "attn1"), (layer1_recurrence, "wkv"), (layer1_mixed_experts, "all")):
                    if not layer(run, stage):
                        return


def tools(nc, ctx, tag):
    def sb(name, shape, dt=F32):
        return ctx.enter_context(nc.sbuf_tensor(f"{tag}_{name}", shape, dt))

    def sem(name):
        return ctx.enter_context(nc.semaphore(f"{tag}_{name}"))

    def dram(name, shape, dt=F32):
        return nc.dram_tensor(f"{tag}_{name}", shape, dt, kind="Internal").ap()

    return sb, sem, dram


def layer0_attention(nc, io, consts, bank, g, out):
    with ExitStack() as ctx:
        layer0_attention_in(nc, io, consts, bank, g, *tools(nc, ctx, "l0a"))


def layer0_attention_in(nc, io, consts, bank, g, sb, sem, dram):
    ident, xn, xt, neg_half = (g[n] for n in ("ident", "xn", "xt", "neg_half"))
    identb, ready, passed = sb("identb", [P, P], BF16), g["ready"], g["passed"]
    rope = sb("rope", [P, TB, 2 * D])
    masks = sb("masks", [P, 4, 2 * P], BF16)
    eye32 = sb("eye32", [P, Q * Q])
    wqk = sb("wqk", [P, CC, 2 * C])
    wvb = sb("wvb", [P, CC, C + H])
    wo = sb("wo", [P, CC, C])
    bb = sb("bb", [P, H])
    x_in = sb("x_in", [P, TB, C])
    x_res = sb("x_res", [P, TB, C])
    xs_t = sb("xs_t", [P, CC, T])
    v_first = sb("v_first", [P, TB, H, D])
    v_next = sb("v_next", [P, TB, H, D])
    v = sb("v", [P, TB, H, D])
    beta = sb("beta", [P, TB, H])
    roped = sb("roped", [P, TB, 2 * C])
    ropet = sb("ropet", [P, TB, 2 * C])
    left = sb("left", [P, TB, 2 * H, 6, D], BF16)
    right = sb("right", [P, TB, H, 6, D], BF16)
    left_t = sb("left_t", [99, 2, H, T], BF16)
    right_t = sb("right_t", [99, H, T], BF16)
    rowmax = sb("rowmax", [P, TB, 2, H])
    negmax = sb("negmax", [P, 2, H])
    nmf = sb("nmf", [P, TB, 2, H])
    nmr = sb("nmr", [P, TB, 2, H])
    nm3 = sb("nm3", [P, TB, 2, 3, H], BF16)
    nm_t = sb("nm_t", [96, T], BF16)
    e_nat = sb("e_nat", [P, H, 3 * P])
    e_t = sb("e_t", [P, 2, H, 3 * P])
    den = sb("den", [P, 2, H])
    gain = sb("gain", [P, 2, H])
    gtmp = sb("gtmp", [P, 2, H])
    gain_next = sb("gain_next", [P, 2 * H])
    gain_rows = sb("gain_rows", [P, Q])
    diag = sb("diag", [P, 2 * H, Q])
    low = sb("low", [P, Q, Q])
    inv = sb("inv", [P, Q, Q])
    invt = sb("invt", [P, 2, 136])
    inv_t = sb("inv_t", [P, 2, H, Q])
    u1 = sb("u1", [P, TB, H, 2 * D])
    rhs = sb("rhs", [P, H, D])
    rden = sb("rden", [P, TB, H])
    maskf = e_nat[:].rearrange("p h c -> p (h c)")[:, 0:8 * P]
    o_t = g["ct"][:].rearrange("p b k t -> p (b k t)")[:, 0:4 * T].rearrange("p (a t) -> p a t", a=4)
    o_nat = g["ct"][:, 2].rearrange("p k t -> p (k t)").rearrange("p (t c) -> p t c", t=TB)
    on_t = g["ct"][:, 3]

    consts_in, x_loaded, x_res_in, moved = (sem(n) for n in ("consts_in", "x_loaded", "x_res_in", "moved"))
    xt_psum, xt_sbuf = sem("xt_psum"), sem("xt_sbuf")
    qkv_psum, v_sbuf, part_s = sem("qkv_psum"), sem("v_sbuf"), sem("part_s")
    beta_s, stack_s = sem("beta_s"), sem("stack_s")
    turned, turned_act, turned_dve = sem("turned"), sem("turned_act"), sem("turned_dve")
    scores, neg_s, e_nat_s, max_q = sem("scores"), sem("neg_s"), sem("e_nat_s"), sem("max_q")
    nm3_s, nmt_psum, nmt_sbuf, nm_rows = sem("nm3_s"), sem("nmt_psum"), sem("nmt_sbuf"), sem("nm_rows")
    e_t_s = sem("e_t_s")
    diag_s, inv_s = sem("diag_s"), sem("inv_s")
    res_psum, rhs_s, sol_psum, sol_s = sem("res_psum"), sem("rhs_s"), sem("sol_psum"), sem("sol_s")
    o_psum, o_sbuf, ot_psum, onat_s, on_psum, on_sbuf, wo_psum = (sem(n) for n in (
        "o_psum", "o_sbuf", "ot_psum", "onat_s", "on_psum", "on_sbuf", "wo_psum"))
    project_link, front_link, back_link, setup_s = (sem(n) for n in ("project_link", "front_link", "back_link", "setup_s"))

    TURNS = 3 * TB * 2
    TURN_BANKS = (5, 0, 1, 2)
    SLOT = (0, 2, 4)
    NG = 2
    HG = H // NG
    SOLVE_BANK = (6, 7)
    STEPS = TB * NQ
    DESCENT = (0, 4, 7, 10, 13, 16, 19, 22, 25, 28, Q - 1)
    PROJECT_LINKS, FRONT_LINKS, BACK_LINKS = 5, 143, 16
    norm = Norm(nc, g, sb, bank(6), 0)

    x_dram = io["x"].rearrange("b (t p) c -> b p t c", p=P)

    BESIDE_SOLVE = ((("turn", 2),), (("scores", 0),), (("scores", 1),), (("scores", 2),), (("scores", 3),), (("scores", 4),),
                    (("scores", 5), ("weigh",)), (("scores", 6),), (("scores", 7), ("descend", 0)), (("project", 0),),
                    (("project", 1), ("descend", 1)), (("project", 2), ("descend", 2)), (("project", 3),), (("descend", 3),),
                    (("descend", 4),), ())
    SCORED = 8
    BESIDE_NUMERATORS = (0, 1, 2, 4)

    with nc.Block() as block:
        def run(**stages):
            eng = stages.pop("eng")

            def go(name, *at):
                if name in stages:
                    stages[name](*at)

            def beside_solve(i, stage, third):
                for name, *at in stage:
                    if name != "project":
                        go(name, i, *at)
                    elif third:
                        go(name, i + 1, *at)

            def body(b, second=True, third=True):
                if second:
                    go("turn", b + 1, 0)
                    go("turn", b + 1, 1)
                for c in range(STEPS):
                    for half, name in ((0, "residual"), (1, "solution")):
                        go(name, b, c)
                        if second:
                            beside_solve(b + 1, BESIDE_SOLVE[2 * c + half], third)
                go("outputs", b, 0)
                if second:
                    after_scores(b + 1, third, lambda n: n in BESIDE_NUMERATORS and go("outputs", b, 1 + BESIDE_NUMERATORS.index(n)))
                else:
                    for n in range(1, 5):
                        go("outputs", b, n)

            def after_scores(i, third, beside=None):
                go("invert", i, third)
                go("descend", i, 5)
                for n in range(NP):
                    if beside:
                        beside(n)
                    go("numerators", i, n)
                    if n < 4:
                        go("descend", i, n + 6)

            for n in range(4):
                go("project", 0, n)
            for n in range(2):
                go("turn", 0, n)
            for stage in BESIDE_SOLVE[:SCORED]:
                beside_solve(0, stage, True)
            go("scores", 0, 7)
            go("invert", 0, False)
            go("project", 1, 0)
            go("descend", 0, 0)
            go("descend", 0, 1)
            go("project", 1, 1)
            go("project", 1, 2)
            go("descend", 0, 2)
            go("project", 1, 3)
            go("cleared", 1)
            for n in range(NP):
                go("numerators", 0, n)
                if n < 7:
                    go("descend", 0, n + 3)
            go("carry", 1)
            with eng.Fori(0, NB - 2) as b:
                body(b)
            body(NB - 2, third=False)
            body(NB - 1, second=False)

        @block.sync
        def _(sp):
            sp.dma_start(x_in[:], x_dram[0]).then_inc(x_loaded, 16)
            sp.dma_start(ident[:], consts["ident"]).then_inc(consts_in, 16)
            for n, name in enumerate(("L0_attn_Wq", "L0_attn_Wk")):
                sp.dma_start(wqk[:, :, n * C:(n + 1) * C], io[name].rearrange("(k p) n -> p k n", p=P)).then_inc(consts_in, 16)
            sp.dma_start(wvb[:, :, 0:C], io["L0_attn_Wv"].rearrange("(k p) n -> p k n", p=P)).then_inc(consts_in, 16)
            sp.dma_start(wvb[:, :, C:C + H], io["L0_attn_Wb"].rearrange("(k p) n -> p k n", p=P)).then_inc(consts_in, 16)
            sp.dma_start(rope[:], consts["rope"]).then_inc(consts_in, 16)
            sp.dma_start(maskf, consts["masks"]).then_inc(consts_in, 16)
            sp.dma_start(eye32[:], consts["eye32"]).then_inc(consts_in, 16)
            sp.dma_start(wo[:], io["L0_attn_Wo"].rearrange("(k p) n -> p k n", p=P)).then_inc(consts_in, 16)
            sp.dma_start(bb[:], io["L0_attn_bb"].rearrange("(a h) -> a h", a=1).broadcast_to([P, H])).then_inc(consts_in, 16)

            def residual(b, c):
                if c == 0:
                    sp.wait_ge(norm.turn_s, b + 1)
                    sp.dma_start(x_res[:], x_dram[b]).then_inc(x_res_in, 16)

            def weigh(i):
                if type(i) is not int or i < NB - 1:
                    sp.wait_ge(xt_psum, i + 1)
                    sp.dma_start(x_in[:], x_dram[i + 1]).then_inc(x_loaded, 16)

            def invert(i, third):
                sp.wait_ge(nmt_sbuf, i + 1)
                for k in range(2):
                    sp.dma_start(left_t[96:99, k, :, :], nm_t[48 * k:48 * k + 48, :]).then_inc(nm_rows, 16)

            run(eng=sp, residual=residual, weigh=weigh, invert=invert)

        @block.scalar
        def _(act):
            act.wait_ge(consts_in, 16 * 10)
            nc.scalar.copy(masks[:].rearrange("p a b -> p (a b)"), maskf).then_inc(setup_s, 1)
            nc.scalar.copy(identb[:], ident[:]).then_inc(setup_s, 1)
            act.sem_inc(norm.xt_s, 1)

            def project(i, n):
                if n == 0:
                    act.wait_ge(xt_psum, i + 1)
                    nc.scalar.copy(xs_t[:].rearrange("p a b -> p (a b)"), bank(0)).then_inc(xt_sbuf, 1)
                elif n == 2:
                    act.wait_ge(beta_s, i + 1)
                    if type(i) is not int or i:
                        act.wait_ge(moved, 2 * i - 1)
                    for t in range(TB):
                        cp = nc.scalar.copy(v_first[:, t].rearrange("p h d -> p (h d)"), bank(3 + t)[:, 0:C])
                    cp.then_inc(v_sbuf, 1)
                elif n == 3:
                    for k in range(2):
                        act.wait_ge(part_s, i * 3 + k + 1)
                        for s in SLOTS[k][1:]:
                            for t in range(TB):
                                cp = nc.scalar.copy(left[:, t, :, s, :], left[:, t, :, SLOTS[k][0], :])
                    cp.then_inc(stack_s, 1)

            def turn(i, n):
                for gr in (4 * n, 4 * n + 2):
                    act.wait_ge(turned, i * TURNS + gr + 1)
                    turn_out(nc.scalar.copy, gr, left_t, right_t, bank, TURN_BANKS).then_inc(turned_act, 1)

            def weigh(i):
                act.wait_ge(e_nat_s, i * NP + NP)
                for q in range(NQ):
                    src = e_nat[Q * q:Q * q + Q, :, P:3 * P].rearrange("r h (s c) -> r s h c", s=2)[:, :, :, Q * q:Q * q + Q]
                    cp = nc.scalar.copy(diag[Q * q:Q * q + Q].rearrange("r (s h) j -> r s h j", s=2), src)
                cp.then_inc(diag_s, 1)

            def scores_(i, n):
                if n < 4:
                    for p in (2 * n, 2 * n + 1):
                        act.wait_ge(neg_s, i * NP + p + 1)
                        for h in (2 * p, 2 * p + 1):
                            sc = bank(SLOT[p % 3] + h % 2)
                            for s, (lo, hi) in enumerate(((0, 2 * P), (2 * P, 3 * P))):
                                ex = nc.scalar.activation(e_nat[:, h, lo:hi], sc[:, lo:hi], ACT.Exp, scale=0.25,
                                                          bias=negmax[:, s, h:h + 1], accum_out=den[:, s, h:h + 1])
                        ex.then_inc(e_nat_s, 1)

            def solution(i, c):
                t, q = divmod(c, NQ)
                for gr in range(NG):
                    act.wait_ge(sol_psum, i * 16 + c * NG + gr + 1)
                    nc.scalar.copy(u1[Q * q:Q * q + Q, t, HG * gr:HG * gr + HG, 0:D],
                                   bank(SOLVE_BANK[gr])[Q * q:Q * q + Q, 0:HG * D].rearrange("p (h d) -> p h d", d=D)).then_inc(sol_s, 1)

            def invert(i, third):
                act.wait_ge(nmt_psum, i + 1)
                nc.scalar.copy(nm_t[:], bank(2).bitcast(BF16)[0:96, 0:T]).then_inc(nmt_sbuf, 1)

            def numerators(i, n):
                for m in (2 * n, 2 * n + 1):
                    k, p = divmod(m, NP)
                    act.wait_ge(scores, i * 4 * NP + 2 * NP + m + 1)
                    src = bank(SLOT[(m + 2 * NP) % 3], 2).rearrange("p (h c) -> p h c", h=2)[:, :, 0:3 * P]
                    nc.scalar.activation(e_t[:, k, 2 * p:2 * p + 2, :], src, ACT.Exp, scale=0.25).then_inc(e_t_s, 1)

            def outputs(b, n):
                if n == 0:
                    act.wait_ge(o_psum, b + 1)
                    nc.scalar.copy(o_t.rearrange("p a b -> p (a b)"), bank(6, 2)).then_inc(o_sbuf, 1)
                elif n == 2:
                    act.wait_ge(on_psum, b + 1)
                    nc.scalar.copy(on_t.rearrange("p a b -> p (a b)"), bank(6)).then_inc(on_sbuf, 1)
                elif n == 4:
                    norm.scalar(act, b)

            run(eng=act, project=project, turn=turn, scores=scores_, weigh=weigh, solution=solution, invert=invert,
                numerators=numerators, outputs=outputs)

        @block.vector
        def _(dve):
            nc.vector.memset(right_t[96:99], 1.0).then_inc(setup_s, 1)
            nc.vector.memset(u1[:, :, :, D:2 * D], 1.0).then_inc(setup_s, 1)
            nc.vector.memset(neg_half[:], -0.5).then_inc(ready, 1)
            dve.wait_ge(consts_in, 16 * 10)
            plink, flink, blink = (Link(dve, link, per, 0) for link, per in (
                (project_link, PROJECT_LINKS), (front_link, FRONT_LINKS), (back_link, BACK_LINKS)))

            def project(i, n):
                if n == 0:
                    if plink.n:
                        plink.close()
                    plink.it, plink.n = i, 0
                if n in (1, 2):
                    t = n - 1
                    dve.wait_ge(qkv_psum, i * 4 + 2 * n)
                    add = nc.vector.tensor_tensor(beta[:, 1 - t, :], bank(3 + t)[:, C:C + H], bb[:], ALU.add)
                    if n == 2:
                        add.then_inc(beta_s, 1)
                    src = bank(1 + t).rearrange("p (h d) -> p h d", d=D)
                    dst = roped[:, t].rearrange("p (h d) -> p h d", d=D)
                    tmp = ropet[:, t].rearrange("p (h d) -> p h d", d=D)
                    tab = rope[:, t:t + 1, :]
                    nc.vector.tensor_tensor(dst, src, tab[:, :, 0:D].broadcast_to([P, 2 * H, D]), ALU.mult)
                    for a, z in ((0, D // 2), (D // 2, 0)):
                        mul = nc.vector.tensor_tensor(tmp[:, :, a:a + D // 2], src[:, :, z:z + D // 2],
                                                      tab[:, :, D + a:D + a + D // 2].broadcast_to([P, 2 * H, D // 2]), ALU.mult)
                    plink(mul)
                    plink(nc.vector.tensor_tensor(dst, dst, tmp, ALU.add))
                elif n == 3:
                    rq = roped[:].rearrange("p t (h d) -> p (t h) d", d=D)
                    rr = ropet[:].rearrange("p t (h d) -> p (t h) d", d=D)
                    lf = left[:].rearrange("p t h s d -> p (t h) s d")
                    nc.vector.tensor_copy(lf[:, :, 0, :], rq).then_inc(part_s, 1)
                    dve.wait_ge(part_s, i * 3 + 1)
                    plink(nc.vector.tensor_tensor(rr, rq, lf[:, :, 0, :], ALU.subtract))
                    nc.vector.tensor_copy(lf[:, :, 2, :], rr).then_inc(part_s, 1)
                    dve.wait_ge(part_s, i * 3 + 2)
                    nc.vector.tensor_tensor(lf[:, :, 5, :], rr, lf[:, :, 2, :], ALU.subtract).then_inc(part_s, 1)

            def turn(i, n):
                if n == 0:
                    if flink.n:
                        flink.close()
                    flink.it, flink.n = i, 0
                for gr in (4 * n + 1, 4 * n + 3):
                    dve.wait_ge(turned, i * TURNS + gr + 1)
                    turn_out(nc.vector.tensor_copy, gr, left_t, right_t, bank, TURN_BANKS).then_inc(turned_dve, 1)

            def scores_(i, n):
                if n >= 0:
                    for m in (2 * n, 2 * n + 1):
                        k, p = divmod(m, NP)
                        dve.wait_ge(scores, i * 4 * NP + m + 1)
                        sc = bank(SLOT[m % 3], 2).rearrange("p (h c) -> p h c", h=2)
                        nc.vector.tensor_reduce(rowmax[:, 0, k, 2 * p:2 * p + 2], sc[:, :, 0:2 * P], AX, ALU.max)
                        rd = nc.vector.tensor_reduce(rowmax[:, 1, k, 2 * p:2 * p + 2], sc[:, :, 2 * P:3 * P], AX, ALU.max)
                        if k == 1:
                            rd.then_inc(max_q, 1)
                        else:
                            flink(rd)
                            nc.vector.tensor_scalar(negmax[:, :, 2 * p:2 * p + 2], rowmax[:, :, 0, 2 * p:2 * p + 2], FLOOR, -0.25,
                                                    ALU.max, ALU.mult).then_inc(neg_s, 1)

            def residual(b, c):
                if c == 0:
                    if blink.n:
                        blink.close()
                    blink.it, blink.n = b, 0
                    return
                t, q = divmod(c, NQ)
                rows = slice(Q * q, Q * q + Q)
                for gr in range(NG):
                    hs = slice(HG * gr, HG * gr + HG)
                    dve.wait_ge(res_psum, b * 14 + (c - 1) * NG + gr + 1)
                    src = bank(SOLVE_BANK[gr])[rows, 0:HG * D].rearrange("p (h d) -> p h d", d=D)
                    gn = gain[rows, 1 - t, hs].rearrange("p (h a) -> p h a", a=1).broadcast_to([Q, HG, D])
                    blink(nc.vector.tensor_tensor(rhs[rows, hs, :], src, gn, ALU.mult))
                    nc.vector.tensor_tensor(rhs[rows, hs, :], rhs[rows, hs, :], v[rows, t, hs, :], ALU.add).then_inc(rhs_s, 1)

            def weigh(i):
                dve.wait_ge(e_nat_s, i * NP + NP)
                flink(nc.vector.tensor_scalar(gtmp[:], den[:], 0.0, None, ALU.is_equal))
                flink(nc.vector.tensor_tensor(gtmp[:], gtmp[:], den[:], ALU.add))
                flink(nc.vector.reciprocal(gtmp[:], gtmp[:]))
                flink(nc.vector.scalar_tensor_tensor(out=gain_next[:].rearrange("p (s h) -> p s h", s=2), in0=gtmp[:], scalar=-1.0,
                                                     in1=beta[:], op0=ALU.mult, op1=ALU.mult))
                flink(nc.vector.transpose(gain_rows[:], gain_next[:]))

            def invert(i, third):
                flink(nc.vector.tensor_copy(gain[:].rearrange("p s h -> p (s h)"), gain_next[:]))
                dve.wait_ge(max_q, i * NP + NP)
                for s in range(2):
                    ts = nc.vector.tensor_scalar(nmf[:, 1 - s], rowmax[:, s], FLOOR, -1.0, ALU.max, ALU.mult)
                flink(ts)
                flink(nc.vector.tensor_copy(nm3[:, :, :, 0, :], nmf[:]))
                flink(nc.vector.tensor_tensor(nmr[:], nmf[:], nm3[:, :, :, 0, :], ALU.subtract))
                flink(nc.vector.tensor_copy(nm3[:, :, :, 1, :], nmr[:]))
                nc.vector.tensor_tensor(nm3[:, :, :, 2, :], nmr[:], nm3[:, :, :, 1, :], ALU.subtract).then_inc(nm3_s, 1)

            def descend(i, n):
                if n == 0:
                    flink(nc.vector.tensor_copy(inv[:].rearrange("p k r -> p (k r)"), eye32[:]))
                    dve.wait_ge(diag_s, i + 1)
                    flink(nc.vector.transpose(low[:].rearrange("p r j -> p j r"), diag[:].rearrange("p g j -> p j g")))
                    flink(nc.vector.tensor_tensor(low[:], low[:], gain_rows[:].rearrange("p (r a) -> p r a", a=1).broadcast_to([P, Q, Q]),
                                                  ALU.mult))
                for j in range(DESCENT[n], DESCENT[n + 1]):
                    k, mid = j + 1, (j + 1 + Q) // 2
                    parts = [(lo, hi, tmp) for lo, hi, tmp in ((j + 1, mid, invt[:, 0]), (mid, Q, invt[:, 1])) if hi > lo]
                    if len(parts) == 1:
                        flink.wait()
                    for op in (0, 1):
                        for lo, hi, tmp in parts:
                            tmp = tmp[:, 0:k * (hi - lo)].rearrange("p (k r) -> p k r", k=k)
                            part = inv[:, 0:k, lo:hi]
                            if op:
                                ins = nc.vector.tensor_tensor(part, part, tmp, ALU.add)
                            else:
                                col = low[:, lo:hi, j:j + 1].rearrange("p r a -> p a r").broadcast_to([P, k, hi - lo])
                                ins = nc.vector.tensor_tensor(tmp, inv[:, 0:k, j:j + 1].broadcast_to([P, k, hi - lo]), col, ALU.mult)
                            flink(ins, behind=len(parts) - 1)
                flink.wait()
                if n == 9:
                    nc.vector.transpose(inv_t[:].rearrange("p s h r -> p r (s h)"), inv[:].rearrange("p k r -> p r k")).then_inc(inv_s, 1)

            def outputs(b, n):
                if n == 1:
                    dve.wait_ge(ot_psum, b + 1)
                    ot = bank(6, 2).rearrange("p (t h d) -> p t h d", t=TB, h=H)
                    blink(nc.vector.reciprocal(rden[:], ot[:, :, :, D]))
                    nc.vector.tensor_tensor(o_nat.rearrange("p t (h d) -> p t h d", d=D), ot[:, :, :, 0:D],
                                            rden[:].rearrange("p t (h a) -> p t h a", a=1).broadcast_to([P, TB, H, D]), ALU.mult).then_inc(onat_s, 1)
                elif n == 3:
                    dve.wait_ge(wo_psum, b + 1)
                    dve.wait_ge(x_res_in, b * 16 + 16)
                    blink(nc.vector.tensor_tensor(norm.y[:].rearrange("p t c -> p (t c)"), bank(7), x_res[:].rearrange("p t c -> p (t c)"), ALU.add))
                    norm.vector(dve, b)

            run(eng=dve, project=project, turn=turn, scores=scores_, weigh=weigh, residual=residual, invert=invert,
                descend=descend, outputs=outputs)
            plink.close()
            flink.close()
            blink.close()

        @block.gpsimd
        def _(pool):
            pool.wait_ge(ready, 1)

            def invert(i, third):
                if type(i) is not int or i:
                    pool.wait_ge(sol_s, i * 16)
                else:
                    carry(0)
                pool.wait_ge(moved, 2 * i + 1)
                apart(pool, passed)
                nc.gpsimd.tensor_copy(v[:], v_next[:]).then_inc(moved, 1)
                if third:
                    carry(i + 1)

            def carry(i):
                if type(i) is not int or i:
                    pool.wait_ge(moved, 2 * i)
                pool.wait_ge(v_sbuf, i + 1)
                apart(pool, passed)
                nc.gpsimd.tensor_copy(v_next[:], v_first[:]).then_inc(moved, 1)

            def project(i, n):
                if n == 3:
                    for k in range(3):
                        pool.wait_ge(part_s, i * 3 + k + 1)
                        apart(pool, passed)
                        src = left[:, :, H:2 * H, SLOTS[k][0], :]
                        for s in SLOTS_B[k]:
                            cp = nc.gpsimd.tensor_copy(right[:, :, :, s, :], src)
                    cp.then_inc(stack_s, 1)

            def outputs(b, n):
                if n == 3:
                    norm.gpsimd(pool, b)

            run(eng=pool, project=project, invert=invert, carry=carry, outputs=outputs)

        @block.tensor
        def _(pe):
            pe.wait_ge(consts_in, 16 * 10)
            pe.wait_ge(setup_s, 4)
            pe.wait_ge(ready, 1)
            pe.sem_inc(norm.turn_s, 1)

            def free_slot(i, n):
                if n < NP:
                    pe.wait_ge(e_nat_s, i * NP + n + 1)
                elif n < 2 * NP:
                    pe.wait_ge(max_q, i * NP + n - NP + 1)
                else:
                    pe.wait_ge(e_t_s, i * 2 * NP + n - 2 * NP + 1)

            def project(i, n):
                if n == 0:
                    if type(i) is not int or i:
                        pe.wait_ge(max_q, i * NP)
                    pe.wait_ge(x_loaded, i * 16 + 16)
                    for c in range(CC):
                        for t in range(TB):
                            mm = nc.tensor.transpose(bank(0)[:, c * T + t * P:c * T + t * P + P], x_in[:, t, c * P:c * P + P], ident[:])
                    mm.then_inc(xt_psum, 1)
                elif n in (1, 2):
                    pe.wait_ge(xt_sbuf, i + 1)
                    if n == 2 and type(i) is int and i == 1:
                        pe.wait_ge(nmt_sbuf, 1)
                    for t in (n - 1,):
                        for w, dst in ((wqk, bank(1 + t)), (wvb, bank(3 + t)[:, 0:C + H])):
                            for c in range(CC):
                                mm = nc.tensor.matmul(dst, xs_t[:, c, t * P:t * P + P], w[:, c, :], start=(c == 0), stop=(c == CC - 1))
                            mm.then_inc(qkv_psum, 1)

            def turn(i, n):
                if n >= 0:
                    if n == 0 and (type(i) is not int or i):
                        pe.wait_ge(e_t_s, i * 2 * NP)
                    pe.wait_ge(stack_s, i * 2 + 2)
                    for gr in range(4 * n, 4 * n + 4):
                        a, t, hh = gr // 4, gr // 2 % 2, gr % 2
                        if gr >= 4:
                            done, m = (turned_act, turned_dve)[gr % 2], (gr - 4) // 2 + 1
                            pe.wait_ge(done, i * (TURNS // 2) + m)
                        dst = bank(TURN_BANKS[gr % 4]).bitcast(BF16)
                        for j in range(8):
                            h = 8 * hh + j
                            src = right[:, t, h] if a == 2 else left[:, t, (H if a == 0 else 0) + h]
                            mm = nc.tensor.transpose(dst[0:96, j * P:j * P + P], src.rearrange("p s d -> p (s d)"), identb[:])
                        mm.then_inc(turned, 1)

            def scores_(i, n):
                if n >= 0:
                    if n == 0:
                        pe.wait_ge(turned_act, i * (TURNS // 2) + TURNS // 2)
                        pe.wait_ge(turned_dve, i * (TURNS // 2) + TURNS // 2)
                    for m in (2 * n, 2 * n + 1):
                        k, p = divmod(m, NP)
                        if m >= 3:
                            free_slot(i, m - 3)
                        for h in (2 * p, 2 * p + 1):
                            dst = bank(SLOT[m % 3] + h % 2)
                            nc.tensor.matmul(dst[:, P:3 * P], identb[:], masks[:, k, :], start=True, stop=False, skip_group_check=True)
                            nc.tensor.matmul(dst[:, 0:2 * P], left_t[0:96, k, h, P:T], right_t[0:96, h, :], start=False, stop=True,
                                             skip_group_check=True)
                            mm = nc.tensor.matmul(dst[:, 2 * P:3 * P], left_t[0:96, k, h, 0:P], right_t[0:96, h, 0:P], start=False,
                                                  stop=True, skip_group_check=True)
                        mm.then_inc(scores, 1)

            def cleared(i):
                pe.wait_ge(v_sbuf, i + 1)
                pe.wait_ge(part_s, i * 3 + 1)

            def invert(i, third):
                if third:
                    cleared(i + 1)
                pe.wait_ge(nm3_s, i + 1)
                for t in range(TB):
                    mm = nc.tensor.transpose(bank(2).bitcast(BF16)[0:96, t * P:t * P + P], nm3[:, t].rearrange("p k a h -> p (k a h)"), identb[:])
                mm.then_inc(nmt_psum, 1)

            def numerators(i, n):
                if n == 0:
                    pe.wait_ge(nm_rows, i * 32 + 32)
                for m in (2 * n, 2 * n + 1):
                    k, p = divmod(m, NP)
                    free_slot(i, 2 * NP + m - 3)
                    for h in (2 * p, 2 * p + 1):
                        dst = bank(SLOT[(m + 2 * NP) % 3] + h % 2)
                        two = dst[:, 0:4 * P].rearrange("p (a c) -> p a c", a=2)[:, :, 0:P]
                        nc.tensor.matmul(two, identb[:], masks[:, 2 + k, :].rearrange("p (a c) -> p a c", a=2), start=True, stop=False,
                                         skip_group_check=True)
                        nc.tensor.matmul(dst[:, 0:2 * P], right_t[:, h, 0:P], left_t[:, k, h, :], start=False, stop=True, skip_group_check=True)
                        mm = nc.tensor.matmul(dst[:, 2 * P:3 * P], right_t[:, h, P:T], left_t[:, k, h, P:T], start=False, stop=True,
                                              skip_group_check=True)
                    mm.then_inc(scores, 1)

            def residual(b, c):
                if c == 0:
                    pe.wait_ge(inv_s, b + 1)
                    pe.wait_ge(e_t_s, b * 2 * NP + 2 * NP)
                    pe.wait_ge(moved, 2 * b + 2)
                    return
                t, q = divmod(c, NQ)
                rows = slice(Q * q, Q * q + Q)
                for gr in range(NG):
                    pe.wait_ge(sol_s, b * 16 + (c - 1) * NG + gr + 1)
                    apart(pe, passed)
                    for i in range(HG):
                        h = HG * gr + i
                        dst = bank(SOLVE_BANK[gr])[rows, i * D:i * D + D]
                        if t:
                            mm = nc.tensor.matmul(dst, e_t[:, 0, h, P + Q * q:P + Q * q + Q], u1[:, 0, h, 0:D], start=True,
                                                  stop=(q == 0), tile_position=(0, Q * q))
                        if q:
                            lo = 2 * P * t + Q * q
                            mm = nc.tensor.matmul(dst, e_t[0:Q * q, 0, h, lo:lo + Q], u1[0:Q * q, t, h, 0:D], start=(t == 0),
                                                  stop=True, tile_position=(0, Q * q))
                    mm.then_inc(res_psum, 1)

            def solution(b, c):
                t, q = divmod(c, NQ)
                rows = slice(Q * q, Q * q + Q)
                for gr in range(NG):
                    if c:
                        pe.wait_ge(rhs_s, b * 14 + (c - 1) * NG + gr + 1)
                    apart(pe, passed)
                    for i in range(HG):
                        h = HG * gr + i
                        src = rhs[rows, h, :] if c else v[rows, 0, h, :]
                        mm = nc.tensor.matmul(bank(SOLVE_BANK[gr])[rows, i * D:i * D + D], inv_t[rows, 1 - t, h, :], src, start=True,
                                              stop=True, tile_position=(Q * q, Q * q))
                    mm.then_inc(sol_psum, 1)

            def outputs(b, n):
                if n == 0:
                    pe.wait_ge(sol_s, b * 16 + 16)
                    for h in range(H):
                        dst = bank(6, 2)[Q * (h % 4):Q * (h % 4) + Q, (h // 4) * T:(h // 4) * T + T]
                        nc.tensor.matmul(dst, u1[:, 0, h, :], e_t[:, 1, h, 0:T], start=True, stop=False, tile_position=(0, Q * (h % 4)))
                        mm = nc.tensor.matmul(dst[:, P:T], u1[:, 1, h, :], e_t[:, 1, h, T:T + P], start=False, stop=True,
                                              tile_position=(0, Q * (h % 4)))
                    mm.then_inc(o_psum, 1)
                elif n == 1:
                    pe.wait_ge(o_sbuf, b + 1)
                    for t in range(TB):
                        for gr in range(4):
                            mm = nc.tensor.transpose(bank(6 + t)[:, gr * P:gr * P + P], o_t[:, gr, t * P:t * P + P], ident[:])
                    mm.then_inc(ot_psum, 1)
                elif n == 2:
                    pe.wait_ge(onat_s, b + 1)
                    for c in range(CC):
                        for t in range(TB):
                            mm = nc.tensor.transpose(bank(6)[:, c * T + t * P:c * T + t * P + P], o_nat[:, t, c * P:c * P + P], ident[:])
                    mm.then_inc(on_psum, 1)
                elif n == 3:
                    pe.wait_ge(on_sbuf, b + 1)
                    for t in range(TB):
                        for c in range(CC):
                            mm = nc.tensor.matmul(bank(7)[:, t * C:t * C + C], on_t[:, c, t * P:t * P + P], wo[:, c, :], start=(c == 0),
                                                  stop=(c == CC - 1))
                    mm.then_inc(wo_psum, 1)
                elif n == 4:
                    norm.tensor(pe, b)

            run(eng=pe, project=project, turn=turn, scores=scores_, residual=residual, solution=solution,
                invert=invert, cleared=cleared, numerators=numerators, outputs=outputs)


def turn_out(copy, g, left_t, right_t, bank, banks):
    a, t, hh = g // 4, g // 2 % 2, g % 2
    src = bank(banks[g % 4]).bitcast(BF16)[0:96, :].rearrange("p (h t) -> p h t", h=8)
    dst = right_t[0:96] if a == 2 else left_t[0:96, a]
    return copy(dst[:, 8 * hh:8 * hh + 8, t * P:t * P + P], src)


class Norm:

    def __init__(self, nc, g, sb, out_bank, before, links_before=None):
        self.nc, self.bank = nc, out_bank
        self.xn, self.xt, self.ident, self.neg_half, self.passed = (g[n] for n in ("xn", "xt", "ident", "neg_half", "passed"))
        self.y, self.ys = sb("y", [P, TB, C]), sb("ys", [P, TB, C])
        self.stats, self.mv, self.rstd = sb("stats", [P, TB, 6]), sb("mv", [P, TB, 2]), sb("rstd", [P, TB])
        self.var_s, self.rstd_s, self.ys_s, self.turn_s, self.xt_s, self.link_s = g["norm_sems"]
        self.before = NB * before
        self.links_before = NB * (before if links_before is None else links_before)

    def vector(self, dve, b):
        norm_measure(self, dve, b)
        norm_scale(self, dve, b)
        norm_keep(self, dve, b)

    def gpsimd(self, pool, b):
        pool.wait_ge(self.var_s, b + (self.before + 1))
        self.nc.gpsimd.tensor_tensor(self.rstd[:], self.rstd[:], self.neg_half[:, 0:TB], ALU.pow).then_inc(self.rstd_s, 1)

    def tensor(self, pe, b):
        pe.wait_ge(self.ys_s, b + (self.before + 1))
        pe.wait_ge(self.xt_s, b + (self.before + 1))
        for c in range(CC):
            for t in range(TB):
                mm = self.nc.tensor.transpose(self.bank[:, c * T + t * P:c * T + t * P + P], self.ys[:, t, c * P:c * P + P],
                                              self.ident[:])
        mm.then_inc(self.turn_s, 1)

    def scalar(self, act, b):
        act.wait_ge(self.turn_s, b + (self.before + 2))
        apart(act, self.passed)
        self.nc.scalar.copy(self.xt[:, :, bass.ds(b * T, T)], self.bank.rearrange("p (c t) -> p c t", c=CC)).then_inc(self.xt_s, 1)


def norm_measure(norm, dve, b):
    nc = norm.nc
    link = Link(dve, norm.link_s, 3, norm.links_before + b)
    for t in range(TB):
        st = nc.vector.bn_stats(norm.stats[:, t, :], norm.y[:, t, :])
    link(st)
    apart(dve, norm.passed)
    for t in range(TB):
        ag = nc.vector.bn_aggr(norm.mv[:, t, :], norm.stats[:, t, :])
    link(ag)
    nc.vector.tensor_scalar(norm.rstd[:], norm.mv[:, :, 1], LN_EPS, None, ALU.add).then_inc(norm.var_s, 1)


def norm_scale(norm, dve, b):
    dve.wait_ge(norm.rstd_s, b + (norm.before + 1))
    dve.wait_ge(norm.turn_s, b + (norm.before + 1))
    for t in range(TB):
        sc = norm.nc.vector.tensor_scalar(norm.ys[:, t, :], norm.y[:, t, :], norm.mv[:, t, 0:1], norm.rstd[:, t:t + 1],
                                          ALU.subtract, ALU.mult)
    sc.then_inc(norm.ys_s, 1)


def norm_keep(norm, dve, b):
    dve.wait_ge(norm.ys_s, b + (norm.before + 1))
    apart(dve, norm.passed)
    norm.nc.vector.tensor_copy(norm.xn[:, b], norm.ys[:]).then_inc(norm.link_s, 1)
    dve.wait_ge(norm.link_s, (b + (norm.links_before + 1)) * 3)


def layer0_experts_by_token(nc, io, consts, bank, g, out):
    with ExitStack() as ctx:
        layer0_experts_by_token_in(nc, io, bank, g, *tools(nc, ctx, "l0x"))


def layer0_experts_by_token_in(nc, io, bank, g, sb, sem, dram):
    E, VOCAB = NB, 12500
    SHARE = VOCAB // E
    ident, xn, xt, ct = (g[n] for n in ("ident", "xn", "xt", "ct"))
    ctx_n = sb("ctx_n", [P, E, TB, C])
    ids = sb("ids", [P, NB * T], I32)
    idf = sb("idf", [P, NB * T])
    mask = sb("mask", [P, E, NB * T])
    z = sb("z", [P, E, 2 * T])
    sz = sb("sz", [P, E, 2 * T])
    hid = sb("hid", [P, E, 2, T])
    norm = Norm(nc, g, sb, bank(6), 1)
    ctx_in, ids_in, ct_psum, ct_s, mask_s = (sem(n) for n in ("ctx_in", "ids_in", "ct_psum", "ct_s", "mask_s"))
    z_psum, z_s, sz_s, hid_s, y_psum, y_s = (sem(n) for n in ("z_psum", "z_s", "sz_s", "hid_s", "y_psum", "y_s"))

    with nc.Block() as block:
        @block.sync
        def _(sp):
            sp.dma_start(ctx_n[:], io["ctx_2048"].rearrange("e (t p) c -> p e t c", p=P)).then_inc(ctx_in, 16)
            sp.dma_start(ids[:], io["itok_BxS_13_99985"].rearrange("(a b) t -> a (b t)", a=1).broadcast_to([P, NB * T])).then_inc(ids_in, 16)
            g["routed"][1](sp)

        @block.scalar
        def _(act):
            for e in range(E):
                act.wait_ge(ct_psum, e + 1)
                nc.scalar.copy(ct[:, e].rearrange("p k q -> p (k q)"), bank(e)).then_inc(ct_s, 1)

            def stage(b, before):
                for e in range(E):
                    act.wait_ge(z_s, b * E + e + 1 + E)
                    nc.scalar.activation(sz[:, e], z[:, e], ACT.Silu).then_inc(sz_s, 1)
                    if before and e == E - 1:
                        norm.scalar(act, b - 1)

            deferred(act, stage, lambda b: norm.scalar(act, b))

        @block.vector
        def _(dve):
            dve.wait_ge(ids_in, 16)
            nc.vector.tensor_copy(idf[:], ids[:]).then_inc(mask_s, 1)
            dve.wait_ge(mask_s, 1)
            nc.vector.tensor_scalar(mask[:, 0], idf[:], float(SHARE), None, ALU.is_lt)
            for e in range(1, E):
                nc.vector.tensor_scalar(mask[:, e], idf[:], float(SHARE * e), None, ALU.is_ge).then_inc(mask_s, 1)
            dve.wait_ge(mask_s, E)
            for e in range(1, E - 1):
                nc.vector.scalar_tensor_tensor(out=mask[:, e], in0=idf[:], scalar=float(SHARE * (e + 1)), in1=mask[:, e],
                                               op0=ALU.is_lt, op1=ALU.mult).then_inc(mask_s, 1)
            dve.wait_ge(mask_s, 2 * E - 2)
            dve.sem_inc(z_s, E)
            dve.sem_inc(y_s, 1)

            def stage(b, before):
                def keep(e):
                    dve.wait_ge(z_psum, b * E + e + 1)
                    m = mask[:, e:e + 1, bass.ds(b * T, T)].broadcast_to([P, 2, T])
                    nc.vector.tensor_tensor(z[:, e].rearrange("p (f t) -> p f t", f=2), bank(e).rearrange("p (f t) -> p f t", f=2),
                                            m, ALU.mult).then_inc(z_s, 1)

                def gate(e):
                    dve.wait_ge(sz_s, b * E + e + 1)
                    dve.wait_ge(y_psum, b + 1)
                    nc.vector.tensor_tensor(hid[:, e].rearrange("p f t -> p (f t)"), sz[:, e], z[:, e], ALU.mult).then_inc(hid_s, 1)

                if before:
                    norm_measure(norm, dve, b - 1)
                keep(0)
                if before:
                    norm_scale(norm, dve, b - 1)
                for e in range(1, E):
                    keep(e)
                    gate(e - 1)
                    if before and e == 1:
                        norm_keep(norm, dve, b - 1)
                gate(E - 1)
                dve.wait_ge(y_psum, b + 2)
                y2 = bank(4, 2).rearrange("p (t c) -> p t c", t=TB)[:, :, 0:C]
                nc.vector.tensor_tensor(norm.y[:], y2, xn[:, b], ALU.add).then_inc(y_s, 1)
                dve.wait_ge(y_s, b + 2)

            deferred(dve, stage, lambda b: norm.vector(dve, b))

        @block.gpsimd
        def _(pool):
            with pool.Fori(0, NB) as b:
                norm.gpsimd(pool, b)

        @block.tensor
        def _(pe):
            pe.wait_ge(ctx_in, 16)
            for e in range(E):
                for k in range(CC):
                    for t in range(TB):
                        mm = nc.tensor.transpose(bank(e)[:, k * T + t * P:k * T + t * P + P], ctx_n[:, e, t, k * P:k * P + P], ident[:])
                mm.then_inc(ct_psum, 1)
            pe.wait_ge(ct_s, E)
            pe.sem_inc(y_psum, 1)

            def stage(b, before):
                for e in range(E):
                    pe.wait_ge(z_s, b * E + e + 1)
                    for f in range(2):
                        for k in range(CC):
                            mm = nc.tensor.matmul(bank(e)[:, f * T:f * T + T], ct[:, e, k, f * P:f * P + P], xt[:, k, bass.ds(b * T, T)],
                                                  start=(k == 0), stop=(k == CC - 1))
                    mm.then_inc(z_psum, 1)
                if before:
                    norm.tensor(pe, b - 1)
                pe.wait_ge(y_s, b + 1)
                for e in range(E):
                    pe.wait_ge(hid_s, b * E + e + 1)
                    for t in range(TB):
                        for f in range(2):
                            mm = nc.tensor.matmul(bank(4 + t)[:, 0:C], hid[:, e, f, t * P:t * P + P], ct[:, e, f, :],
                                                  start=(e == 0 and f == 0), stop=(e == E - 1 and f == 1))
                mm.then_inc(y_psum, 1)

            deferred(pe, stage, lambda b: norm.tensor(pe, b))


def routed_inputs(io, consts, sb, sem, dram):
    E, F = 16, 256
    n = {
        "rw": sb("rw", [E, C]), "rb": sb("rb", [P, E]), "gub": sb("gub", [E, 2 * F]), "bd": sb("bd", [E, C]),
        "resets": sb("resets", [P, NB * TB * E]), "wgu": sb("wgu", [P, 2, CC, 2 * F]), "wd": sb("wd", [P, 2, 2, C]),
        "small_in": sem("small_in"), "w_in": [sem("w_in_even"), sem("w_in_odd")],
    }

    def load_expert(sp, x, e):
        sp.dma_start(n["wgu"][:, e], io["L0_ffn_gate_up_proj"].rearrange("e (k p) n -> e p k n", p=P)[x]).then_inc(n["w_in"][e], 16)
        sp.dma_start(n["wd"][:, e], io["L0_ffn_down_proj"].rearrange("e (k p) n -> e p k n", p=P)[x]).then_inc(n["w_in"][e], 16)

    def load(sp):
        sp.dma_start(n["rw"][:], io["L0_ffn_router_weight"]).then_inc(n["small_in"], 16)
        sp.dma_start(n["rb"][:], io["L0_ffn_router_bias"].rearrange("(a e) -> a e", a=1).broadcast_to([P, E])).then_inc(n["small_in"], 16)
        sp.dma_start(n["gub"][:], io["L0_ffn_gate_up_proj_bias"]).then_inc(n["small_in"], 16)
        sp.dma_start(n["bd"][:], io["L0_ffn_down_proj_bias"]).then_inc(n["small_in"], 16)
        sp.dma_start(n["resets"][:], consts["resets"]).then_inc(n["small_in"], 16)
        load_expert(sp, 0, 0)
        load_expert(sp, 1, 1)

    return n, load, load_expert


def layer0_experts_by_router(nc, io, consts, bank, g, out):
    with ExitStack() as ctx:
        layer0_experts_by_router_in(nc, io, consts, bank, g, *tools(nc, ctx, "l0f"))


def layer0_experts_by_router_in(nc, io, consts, bank, g, sb, sem, dram):
    E, F, K_TOP, ALPHA, LIMIT = 16, 256, 4, 1.702, 7.0
    NT = NB * TB
    HT = NB * T // 2
    ident, xn, xt, neg_half, passed = (g[n] for n in ("ident", "xn", "xt", "neg_half", "passed"))
    loaded, _, load_expert = g["routed"]
    rw, rb, gub, bd, resets, wgu, wd, small_in, w_in = (
        loaded[n] for n in ("rw", "rb", "gub", "bd", "resets", "wgu", "wd", "small_in", "w_in"))
    rwt, gubt = sb("rwt", [P, CC, E]), sb("gubt", [P, E, 4])
    logits, eq, gt, cum, sel = (sb(n, [P, NT, E]) for n in ("logits", "eq", "gt", "cum", "sel"))
    top = sb("top", [P, NT, 8])
    count = sb("count", [P, NT])
    score = sb("score", [P, E, NT])
    score_t = sb("score_t", [E, NT * P])
    acc = sb("acc", [P, NB, TB, C])
    x_high, x_rest = sb("x_high", [P, CC, NB * T], F32R), sb("x_rest", [P, CC, NB * T], F32R)
    w_high, w_rest = sb("w_high", [P, 2, 3, 2 * F], F32R), sb("w_rest", [P, 2, 3, 2 * F], F32R)
    hid_high, hid_rest = sb("hid_high", [P, 2, NB * T], F32R), sb("hid_rest", [P, 2, NB * T], F32R)
    bias2, score2 = sb("bias2", [P, 2, 4]), sb("score2", [P, 2, NT])
    gate, sig, gs, up = (sb(n, [P, 2, HT]) for n in ("gate", "sig", "gs", "up"))
    hid = sb("hid", [P, 2, HT])
    norm = Norm(nc, g, sb, bank(6), 2)
    stats, mv, rstd = sb("norm_stats", [P, NT, 6]), sb("norm_mv", [P, NT, 2]), sb("norm_rstd", [P, NT])
    rt_psum, rt_s, lg_psum, score_s, st_psum, st_s, bd_psum = (
        sem(n) for n in ("rt_psum", "rt_s", "lg_psum", "score_s", "st_psum", "st_s", "bd_psum"))
    gate_psum, up_psum, gate_s, sig_s, gs_s, up_s, hid_s, down_psum, acc_s = (
        sem(n) for n in ("gate_psum", "up_psum", "gate_s", "sig_s", "gs_s", "up_s", "hid_s", "down_psum", "acc_s"))
    route_s, stage_s, link_s = sem("route_s"), sem("stage_s"), sem("link_s")
    x_high_s, x_rest_s, w_high_s, w_rest_s, hid_high_s, hid_rest_s = (
        sem(n) for n in ("x_high_s", "x_rest_s", "w_high_s", "w_rest_s", "hid_high_s", "hid_rest_s"))
    UNITS = 4

    def each_expert(eng, expert):
        expert(0, 0, True, False)
        expert(1, 1, False, False)
        with eng.Fori(1, E // 2 - 1) as it:
            for e in range(2):
                expert(it * 2 + e, e, False, False)
        expert(E - 2, 0, False, False)
        expert(E - 1, 1, False, True)

    def raw(e, part):
        if part < CC:
            return wgu[:, e, part].rearrange("p (n two) -> p two n", two=2)
        return wd[:, e].rearrange("p w c -> p (w c)").rearrange("p (a n) -> p a n", a=2)

    def split(buf, e, part):
        return buf[:, e, part].rearrange("p (a n) -> p a n", a=2)

    with nc.Block() as block:
        @block.sync
        def _(sp):
            with sp.Fori(1, E // 2) as it:
                for e in range(2):
                    sp.wait_ge(w_rest_s, it * 6 + (e * 3 - 3))
                    load_expert(sp, it * 2 + e, e)
            g["retention"][1](sp)

        @block.scalar
        def _(act):
            nc.scalar.copy(x_high[:], xt[:]).then_inc(x_high_s, 1)

            def high_weights(x, e, part):
                if part == 0:
                    act.wait_ge(w_in[e], (x - e) * 16 + 32)
                    if type(x) is not int or x > 1:
                        act.wait_ge(down_psum, x * 4 + 4)
                    apart(act, passed)
                nc.scalar.copy(split(w_high, e, part), raw(e, part)).then_inc(w_high_s, 1)

            for part in range(3):
                high_weights(0, 0, part)
            act.wait_ge(rt_psum, 1)
            nc.scalar.copy(rwt[:].rearrange("p k e -> p (k e)"), bank(0)[:, 0:CC * E]).then_inc(rt_s, 1)
            nc.scalar.copy(gubt[:].rearrange("p e n -> p n e"), bank(0)[:, CC * E:(CC + 4) * E].rearrange("p (n e) -> p n e", e=E)).then_inc(rt_s, 1)
            act.wait_ge(route_s, 9)
            nc.scalar.activation(eq[:], cum[:], ACT.Exp).then_inc(score_s, 1)

            def expert(x, e, first, last):
                def high(x, n):
                    half, w = n // 2, n % 2
                    act.wait_ge(hid_s, x * UNITS + n + 3)
                    apart(act, passed)
                    nc.scalar.copy(hid_high[:, w, half * HT:half * HT + HT], hid[:, n % 2]).then_inc(hid_high_s, 1)

                for n in range(UNITS):
                    if not n and not first:
                        high(x - 1, UNITS - 1)
                    act.wait_ge(gate_s, x * UNITS + n + 1)
                    nc.scalar.activation(sig[:, n % 2], gate[:, n % 2], ACT.Sigmoid, scale=ALPHA).then_inc(sig_s, 1)
                    if n:
                        high(x, n - 1)
                    if n < 3 and not last:
                        high_weights(x + 1, 1 - e, n)
                    if first and n == 1:
                        act.wait_ge(st_psum, 1)
                        nc.scalar.copy(score_t[:], bank(4, 2)[0:E, :]).then_inc(st_s, 1)
                if last:
                    high(x, UNITS - 1)

            each_expert(act, expert)
            for b in range(NB):
                act.wait_ge(norm.turn_s, norm.before + b + 2)
                nc.scalar.copy(xt[:, :, b * T:b * T + T], bank(4 + b).rearrange("p (c t) -> p c t", c=CC)).then_inc(norm.xt_s, 1)

        @block.vector
        def _(dve):
            n = [0]

            def route(ins):
                n[0] += 1
                ins.then_inc(route_s, 1)
                dve.wait_ge(route_s, n[0])

            dve.sem_inc(up_s, 2)
            dve.sem_inc(hid_s, 2)
            dve.sem_inc(hid_rest_s, 2)
            dve.wait_ge(x_high_s, 1)
            nc.vector.tensor_tensor(x_rest[:], xt[:], x_high[:].bitcast(F32), ALU.subtract).then_inc(x_rest_s, 1)
            dve.wait_ge(lg_psum, 1)
            route(nc.vector.tensor_tensor(logits[:], bank(1)[:, 0:NT * E].rearrange("p (t e) -> p t e", e=E),
                                          rb[:].rearrange("p (a e) -> p a e", a=1).broadcast_to([P, NT, E]), ALU.add))
            for t in range(NT):
                mx = nc.vector.max(top[:, t, :], logits[:, t, :])
            route(mx)
            fourth = top[:, :, K_TOP - 1:K_TOP].broadcast_to([P, NT, E])
            nc.vector.tensor_tensor(gt[:], logits[:], fourth, ALU.is_gt)
            route(nc.vector.tensor_tensor(eq[:], logits[:], fourth, ALU.is_equal))
            route(nc.vector.tensor_reduce(count[:], gt[:], AX, ALU.add))
            route(nc.vector.tensor_tensor_scan(cum[:].rearrange("p t e -> p (t e)"), resets[:], eq[:].rearrange("p t e -> p (t e)"),
                                               0.0, ALU.mult, ALU.add))
            route(nc.vector.tensor_tensor(cum[:], cum[:], count[:].rearrange("p (t a) -> p t a", a=1).broadcast_to([P, NT, E]), ALU.add))
            route(nc.vector.scalar_tensor_tensor(out=sel[:], in0=cum[:], scalar=float(K_TOP), in1=eq[:], op0=ALU.is_le, op1=ALU.mult))
            route(nc.vector.tensor_tensor(sel[:], sel[:], gt[:], ALU.add))
            route(nc.vector.tensor_tensor(cum[:], logits[:], top[:, :, 0:1].broadcast_to([P, NT, E]), ALU.subtract))
            dve.wait_ge(score_s, 1)
            route(nc.vector.tensor_tensor(sel[:], sel[:], eq[:], ALU.mult))
            route(nc.vector.tensor_reduce(count[:], sel[:], AX, ALU.add))
            route(nc.vector.reciprocal(count[:], count[:]))
            nc.vector.tensor_tensor(score[:].rearrange("p e t -> p t e"), sel[:],
                                    count[:].rearrange("p (t a) -> p t a", a=1).broadcast_to([P, NT, E]), ALU.mult).then_inc(score_s, 1)
            dve.wait_ge(rt_s, 2)
            dve.wait_ge(score_s, 2)

            def stage(x, e):
                if type(x) is not int or x:
                    dve.wait_ge(acc_s, x * 4)
                apart(dve, passed)
                nc.vector.tensor_copy(score2[:, e:e + 1], score[:, bass.ds(x, 1), :])
                nc.vector.tensor_copy(bias2[:, e:e + 1], gubt[:, bass.ds(x, 1), :]).then_inc(stage_s, 1)
                dve.wait_ge(stage_s, x * 2 + 1)
                nc.vector.tensor_scalar(bias2[:, e, 2:4], bias2[:, e, 2:4], 1.0, None, ALU.add).then_inc(stage_s, 1)

            stage(0, 0)

            def expert(x, e, first, last):
                def take(n):
                    w = n % 2
                    dve.wait_ge(gate_psum, x * UNITS + n + 1)
                    nc.vector.tensor_scalar(gate[:, n % 2], bank(2 * (n % 2)), bias2[:, e, w:w + 1], LIMIT, ALU.add, ALU.min).then_inc(gate_s, 1)
                    dve.wait_ge(hid_s, x * UNITS + n + 1)
                    dve.wait_ge(up_psum, x * UNITS + n + 1)
                    nc.vector.tensor_scalar(up[:, n % 2], bank(2 * (n % 2) + 1), bias2[:, e, 2 + w:3 + w], 1.0 - LIMIT, ALU.add,
                                            ALU.max).then_inc(up_s, 1)

                def combine(x, n):
                    dve.wait_ge(up_s, x * UNITS + n + 3)
                    dve.wait_ge(hid_rest_s, x * UNITS + n + 1)
                    dve.wait_ge(gs_s, x * UNITS + n + 1)
                    nc.vector.scalar_tensor_tensor(out=hid[:, n % 2], in0=up[:, n % 2], scalar=1.0 + LIMIT,
                                                   in1=gs[:, n % 2], op0=ALU.min, op1=ALU.mult).then_inc(hid_s, 1)

                def rest(x, n):
                    half, w = n // 2, n % 2
                    part = slice(half * HT, half * HT + HT)
                    dve.wait_ge(hid_high_s, x * UNITS + n + 1)
                    nc.vector.tensor_tensor(hid_rest[:, w, part], hid[:, n % 2], hid_high[:, w, part].bitcast(F32),
                                            ALU.subtract).then_inc(hid_rest_s, 1)

                def accumulate(x, e, k):
                    dve.wait_ge(down_psum, x * 4 + k + 9)
                    dve.wait_ge(acc_s, x * 4 + k + 1)
                    for t in range(TB):
                        add = nc.vector.scalar_tensor_tensor(out=acc[:, k, t, :], in0=bank(4 + k)[:, t * C:t * C + C],
                                                             scalar=score2[:, e, 2 * k + t:2 * k + t + 1], in1=acc[:, k, t, :],
                                                             op0=ALU.mult, op1=ALU.add)
                    add.then_inc(acc_s, 1)

                def finish(x, e):
                    rest(x, 3)
                    for k in range(4):
                        accumulate(x, e, k)

                dve.wait_ge(stage_s, x * 2 + 2)
                if not first:
                    combine(x - 1, 3)
                    rest(x - 1, 2)
                take(0)
                if not first:
                    finish(x - 1, 1 - e)
                take(1)
                combine(x, 0)
                if first:
                    dve.wait_ge(bd_psum, 1)
                    nc.vector.tensor_tensor(acc[:].rearrange("p b t c -> p (b t c)"), bank(4, 4),
                                            xn[:].rearrange("p b t c -> p (b t c)"), ALU.add).then_inc(acc_s, 4)
                take(2)
                combine(x, 1)
                rest(x, 0)
                if not last:
                    stage(x + 1, 1 - e)
                take(3)
                combine(x, 2)
                rest(x, 1)
                if last:
                    combine(x, 3)
                    rest(x, 2)
                    finish(x, e)

            each_expert(dve, expert)
            dve.wait_ge(acc_s, 4 * E + 4)
            link = Link(dve, link_s, 2, 0)
            for b in range(NB):
                for t in range(TB):
                    st = nc.vector.bn_stats(stats[:, TB * b + t], acc[:, b, t])
            link(st)
            for n in range(NT):
                ag = nc.vector.bn_aggr(mv[:, n], stats[:, n])
            link(ag)
            nc.vector.tensor_scalar(rstd[:], mv[:, :, 1], LN_EPS, None, ALU.add).then_inc(norm.var_s, NB)
            dve.wait_ge(norm.rstd_s, norm.before + NB)
            for b in range(NB):
                for t in range(TB):
                    n = TB * b + t
                    sc = nc.vector.tensor_scalar(xn[:, b, t], acc[:, b, t], mv[:, n, 0:1], rstd[:, n:n + 1], ALU.subtract, ALU.mult)
                sc.then_inc(norm.ys_s, 1)

        @block.gpsimd
        def _(pool):
            def rest_weights(x, e, part):
                pool.wait_ge(w_high_s, x * 3 + part + 1)
                nc.gpsimd.tensor_tensor(split(w_rest, e, part), raw(e, part), split(w_high, e, part).bitcast(F32),
                                        ALU.subtract).then_inc(w_rest_s, 1)

            for part in range(3):
                rest_weights(0, 0, part)

            def expert(x, e, first, last):
                for n in range(UNITS):
                    pool.wait_ge(sig_s, x * UNITS + n + 1)
                    nc.gpsimd.tensor_tensor(gs[:, n % 2], gate[:, n % 2], sig[:, n % 2], ALU.mult).then_inc(gs_s, 1)
                    if n != 2 and not last:
                        rest_weights(x + 1, 1 - e, min(n, 2))

            each_expert(pool, expert)
            pool.wait_ge(norm.var_s, norm.before + NB)
            nc.gpsimd.tensor_tensor(rstd[:], rstd[:], neg_half[:, 0:NT], ALU.pow).then_inc(norm.rstd_s, NB)

        @block.tensor
        def _(pe):
            pe.wait_ge(small_in, 16 * 5)
            for k in range(CC):
                nc.tensor.transpose(bank(0)[:, k * E:k * E + E], rw[:, k * P:k * P + P], ident[0:E, 0:E])
            for n in range(4):
                w, kind = n % 2, n // 2
                src = gub[:, w * 2 * P:(w + 1) * 2 * P].rearrange("e (p two) -> e two p", two=2)[:, kind, :]
                mm = nc.tensor.transpose(bank(0)[:, (CC + n) * E:(CC + n + 1) * E], src, ident[0:E, 0:E])
            mm.then_inc(rt_psum, 1)
            pe.wait_ge(rt_s, 1)
            for t in range(NT):
                for k in range(CC):
                    mm = nc.tensor.matmul(bank(1)[:, t * E:t * E + E], xt[:, k, t * P:t * P + P], rwt[:, k, :], start=(k == 0), stop=(k == CC - 1))
            mm.then_inc(lg_psum, 1)

            def biases():
                pe.wait_ge(score_s, 2)
                for t in range(NT):
                    mm = nc.tensor.transpose(bank(4, 2)[0:E, t * P:t * P + P], score[:, :, t], ident[:])
                mm.then_inc(st_psum, 1)
                pe.wait_ge(st_s, 1)
                for t in range(NT):
                    mm = nc.tensor.matmul(bank(4, 4)[:, t * C:t * C + C], score_t[:, t * P:t * P + P], bd[:], start=True, stop=True)
                mm.then_inc(bd_psum, 1)

            pe.wait_ge(rt_s, 2)
            pe.wait_ge(route_s, 1)
            pe.sem_inc(down_psum, 8)
            pe.wait_ge(x_rest_s, 1)

            def expert(x, e, first, last):
                def project(n):
                    half, w = n // 2, n % 2
                    part = slice(half * HT, half * HT + HT)
                    pe.wait_ge(up_s, x * UNITS + n + 1)
                    for kind, done in ((0, gate_psum), (1, up_psum)):
                        col = slice(kind * F + w * P, kind * F + w * P + P)
                        for k in range(CC):
                            for a, b in ((w_high, x_high), (w_high, x_rest), (w_rest, x_high)):
                                mm = nc.tensor.matmul(bank(2 * (n % 2) + kind), a[:, e, k, col], b[:, k, part],
                                                      start=(k == 0 and b is x_high and a is w_high),
                                                      stop=(k == CC - 1 and a is w_rest))
                        mm.then_inc(done, 1)

                def down(x, e, k):
                    if k == 0:
                        pe.wait_ge(w_rest_s, x * 3 + 3)
                    pe.wait_ge(acc_s, x * 4 + k + 1)
                    pe.wait_ge(hid_rest_s, x * UNITS + (4 if k < 2 else 6))
                    for t in (2 * k, 2 * k + 1):
                        for w in range(2):
                            for a, b in ((hid_high, w_high), (hid_high, w_rest), (hid_rest, w_high)):
                                mm = nc.tensor.matmul(bank(4 + k)[:, t % 2 * C:t % 2 * C + C], a[:, w, t * P:t * P + P],
                                                      b[:, e, 2, w * C:w * C + C], start=(w == 0 and a is hid_high and b is w_high),
                                                      stop=(w == 1 and a is hid_rest))
                    mm.then_inc(down_psum, 1)

                pe.wait_ge(w_rest_s, x * 3 + 2)
                project(0)
                if not first:
                    for k in range(4):
                        down(x - 1, 1 - e, k)
                for n in range(1, UNITS):
                    project(n)
                    if first and n == 1:
                        biases()
                if last:
                    for k in range(4):
                        down(x, e, k)

            each_expert(pe, expert)
            for b in range(NB):
                pe.wait_ge(norm.ys_s, norm.before + b + 1)
                for c in range(CC):
                    for t in range(TB):
                        mm = nc.tensor.transpose(bank(4 + b)[:, c * T + t * P:c * T + t * P + P], xn[:, b, t, c * P:c * P + P], ident[:])
                mm.then_inc(norm.turn_s, 1)


def retention_inputs(io, consts, sb, sem, dram):
    RH, RD = 4, 64
    n = {
        "w_nat": sb("w_nat", [P, 10, C]),
        "xpos": sb("xpos", [P, TB, 2, 2, RD // 2]),
        "decay": sb("decay", [P, RH, 3 * P]),
        "average": sb("average", [P, P]),
        "gnw": sb("gnw", [P, 2]), "gnb": sb("gnb", [P, 2]), "c_in": sem("c_in"),
    }

    def load(sp):
        c_in = n["c_in"]
        for rows, name in ((slice(0, 6), "L1_attn_wqkv"), (slice(6, 8), "L1_attn_wg"), (slice(8, 10), "L1_attn_wo")):
            sp.dma_start(n["w_nat"][:, rows], io[name].rearrange("(n p) c -> p n c", p=P)).then_inc(c_in, 16)
        for name in ("xpos", "decay", "average"):
            sp.dma_start(n[name][:], consts[name]).then_inc(c_in, 16)
        for dst, name in (("gnw", "L1_attn_gn_weight"), ("gnb", "L1_attn_gn_bias")):
            for half in range(2):
                src = io[name].rearrange("(a k two) -> a two k", a=1, two=2)[:, half, :]
                sp.dma_start(n[dst][RD * half:RD * half + RD, :], src.broadcast_to([RD, 2]), allow_slow_non_contiguous=True).then_inc(c_in, 16)

    return n, load


def layer1_retention(nc, io, consts, bank, g, out):
    with ExitStack() as ctx:
        layer1_retention_in(nc, io, consts, bank, g, *tools(nc, ctx, "l1r"))


def layer1_retention_in(nc, io, consts, bank, g, sb, sem, dram):
    RH, RD = 4, 64
    ROT = RD // 2
    ident, xn, xt, neg_half, passed = (g[n] for n in ("ident", "xn", "xt", "neg_half", "passed"))
    w_nat, xpos, decay, average, gnw, gnb, c_in = (g["retention"][0][n] for n in ("w_nat", "xpos", "decay", "average", "gnw", "gnb", "c_in"))
    w_t = sb("w_t", [P, 10, CC, P])
    xs_t = sb("xs_t", [P, CC, T])
    qk = sb("qk", [P, TB, 2, RH, RD])
    rot = sb("rot", [P, TB, 2, RH, ROT])
    v = sb("v", [P, TB, RH, RD])
    qk_t = sb("qk_t", [P, 2, 2, T])
    s_t = sb("s_t", [P, RH, 3 * P])
    st6, mom, tot = sb("st6", [P, 2, 6]), sb("mom", [P, 2, 2]), sb("tot", [P, 2, 2])
    msq, vr, aw, ab = (sb(n, [P, 2]) for n in ("msq", "vr", "aw", "ab"))
    ge, gn, gd = (sb(n, [P, 2 * T]) for n in ("ge", "gn", "gd"))
    ret = sb("ret", [P, 2, T])
    norm = Norm(nc, g, sb, bank(7), 3, 2)
    wt_psum, wt_s, rot_link, y_s = sem("wt_psum"), sem("wt_s"), sem("rot_link"), sem("y_s")
    xs_s, qkv_psum, g_psum, v_s, rot_s, qkt_psum, qkt_s = (
        sem(n) for n in ("xs_s", "qkv_psum", "g_psum", "v_s", "rot_s", "qkt_psum", "qkt_s"))
    sc_psum, st_s, ret_psum, mom_s, tot_psum, gvar_s, gstd_s, gmin_s, gexp_s, ym_s, y_psum, link_s = (
        sem(n) for n in ("sc_psum", "st_s", "ret_psum", "mom_s", "tot_psum", "gvar_s", "gstd_s", "gmin_s", "gexp_s", "ym_s",
                         "y_psum", "link_s"))
    LINKS = 14

    def staged(eng, stage, norm):
        stage(0, False, True)
        with eng.Fori(1, NB - 1) as b:
            stage(b, True, True)
        stage(NB - 1, True, False)
        norm(NB - 1)

    with nc.Block() as block:
        @block.sync
        def _(sp):
            g["mixed"][1](sp)

        @block.scalar
        def _(act):
            for n in range(5):
                act.wait_ge(wt_psum, n + 1)
                nc.scalar.copy(w_t[:, 2 * n:2 * n + 2].rearrange("p n k c -> p (n k c)"), bank(n)).then_inc(wt_s, 1)

            nc.scalar.copy(xs_t[:], xt[:, :, 0:T]).then_inc(xs_s, 1)

            def stage(b, before, after):
                for t in range(TB):
                    act.wait_ge(qkv_psum, b * TB + t + 1)
                    src = bank(2 * t, 2)[:, 0:3 * C].rearrange("p (h x d) -> p x h d", h=RH, x=3)
                    nc.scalar.copy(v[:, t], src[:, 2])
                    nc.scalar.copy(qk[:, t, :, :, ROT:RD], src[:, 0:2, :, ROT:RD]).then_inc(v_s, 1)
                act.wait_ge(gmin_s, b + 1)
                nc.scalar.activation(ge[:], gd[:], ACT.Exp).then_inc(gexp_s, 1)
                act.wait_ge(qkt_psum, b + 1)
                nc.scalar.copy(qk_t[:].rearrange("p x k t -> p (x k t)"), bank(5, 2)).then_inc(qkt_s, 1)
                if after:
                    act.wait_ge(g_psum, b + 1)
                    apart(act, passed)
                    nc.scalar.copy(xs_t[:], xt[:, :, bass.ds((b + 1) * T, T)]).then_inc(xs_s, 1)
                if before:
                    norm.scalar(act, b - 1)

            staged(act, stage, lambda b: norm.scalar(act, b))

        @block.vector
        def _(dve):
            dve.wait_ge(c_in, 16 * 10)

            def rotate(b):
                link = Link(dve, rot_link, 2, b)
                for t in range(TB):
                    dve.wait_ge(v_s, b * TB + t + 1)
                    src = bank(2 * t, 2)[:, 0:3 * C].rearrange("p (h x d) -> p x h d", h=RH, x=3)[:, 0:2, :, 0:ROT]
                    for x in range(2):
                        tab = xpos[:, t, x:x + 1]
                        nc.vector.tensor_tensor(qk[:, t, x, :, 0:ROT], src[:, x], tab[:, :, 0, :].broadcast_to([P, RH, ROT]), ALU.mult)
                        pair = src[:, x].rearrange("p h (n two) -> p h n two", two=2)
                        dst = rot[:, t, x].rearrange("p h (n two) -> p h n two", two=2)
                        sin = tab[:, :, 1, :].rearrange("p a (n two) -> p a n two", two=2)
                        for one in range(2):
                            mul = nc.vector.tensor_tensor(dst[:, :, :, one], pair[:, :, :, 1 - one],
                                                          sin[:, :, :, one].broadcast_to([P, RH, ROT // 2]), ALU.mult)
                    link(mul)
                    add = nc.vector.tensor_tensor(qk[:, t, :, :, 0:ROT], qk[:, t, :, :, 0:ROT], rot[:, t], ALU.add)
                add.then_inc(rot_s, 1)
                link.close()

            rotate(0)

            def stage(b, before, after):
                link = Link(dve, link_s, LINKS, b)
                if before:
                    norm_measure(norm, dve, b - 1)
                dve.wait_ge(g_psum, b + 1)
                nc.vector.tensor_scalar(gd[:], bank(4), 20.0, None, ALU.min).then_inc(gmin_s, 1)
                if before:
                    norm_scale(norm, dve, b - 1)
                for h in range(RH):
                    dve.wait_ge(sc_psum, b * RH + h + 1)
                    nc.vector.tensor_tensor(s_t[:, h], bank(h)[:, 0:3 * P], decay[:, h], ALU.mult).then_inc(st_s, 1)
                if before:
                    norm_keep(norm, dve, b - 1)
                dve.wait_ge(gexp_s, b + 1)
                link(nc.vector.scalar_tensor_tensor(out=gn[:], in0=ge[:], scalar=2.0, in1=ge[:], op0=ALU.add, op1=ALU.mult))
                link(nc.vector.tensor_scalar(gd[:], gn[:], 2.0, None, ALU.add))
                dve.wait_ge(ret_psum, b + 1)
                for k in range(2):
                    bs = nc.vector.bn_stats(st6[:, k], bank(5)[:, k * T:k * T + T])
                link(bs)
                apart(dve, norm.passed)
                for k in range(2):
                    ag = nc.vector.bn_aggr(mom[:, k], st6[:, k])
                link(ag)
                link(nc.vector.tensor_tensor(msq[:], mom[:, :, 0], mom[:, :, 0], ALU.mult))
                nc.vector.tensor_tensor(mom[:, :, 1], mom[:, :, 1], msq[:], ALU.add).then_inc(mom_s, 1)
                link(nc.vector.reciprocal(ge[:], gd[:]))
                dve.wait_ge(tot_psum, b + 1)
                link(nc.vector.tensor_copy(tot[:].rearrange("p k m -> p (k m)"), bank(6)[:, 0:4]))
                link(nc.vector.tensor_tensor(msq[:], tot[:, :, 0], tot[:, :, 0], ALU.mult))
                nc.vector.scalar_tensor_tensor(out=vr[:], in0=tot[:, :, 1], scalar=LN_EPS, in1=msq[:], op0=ALU.add,
                                               op1=ALU.subtract).then_inc(gvar_s, 1)
                link(nc.vector.tensor_tensor(gn[:], gn[:], ge[:], ALU.mult))
                link(nc.vector.tensor_tensor(gn[:], gn[:], bank(4), ALU.mult))
                dve.wait_ge(gstd_s, b + 1)
                link(nc.vector.tensor_tensor(aw[:], vr[:], gnw[:], ALU.mult))
                link(nc.vector.tensor_tensor(ab[:], tot[:, :, 0], aw[:], ALU.mult))
                link(nc.vector.tensor_tensor(ab[:], gnb[:], ab[:], ALU.subtract))
                for k in range(2):
                    ts = nc.vector.tensor_scalar(ret[:, k], bank(5)[:, k * T:k * T + T], aw[:, k:k + 1], ab[:, k:k + 1], ALU.mult, ALU.add)
                link(ts)
                nc.vector.tensor_tensor(ret[:].rearrange("p k t -> p (k t)"), ret[:].rearrange("p k t -> p (k t)"), gn[:],
                                        ALU.mult).then_inc(ym_s, 1)
                if after:
                    rotate(b + 1)
                dve.wait_ge(y_psum, b + 1)
                y2 = bank(5).rearrange("p (t c) -> p t c", t=TB)
                nc.vector.tensor_tensor(norm.y[:], y2, xn[:, b], ALU.add).then_inc(y_s, 1)
                dve.wait_ge(y_s, b + 1)
                link.close()

            staged(dve, stage, lambda b: norm.vector(dve, b))

        @block.gpsimd
        def _(pool):
            def stage(b, before, after):
                if before:
                    norm.gpsimd(pool, b - 1)
                pool.wait_ge(gvar_s, b + 1)
                nc.gpsimd.tensor_tensor(vr[:], vr[:], neg_half[:, 0:2], ALU.pow).then_inc(gstd_s, 1)

            staged(pool, stage, lambda b: norm.gpsimd(pool, b))

        @block.tensor
        def _(pe):
            pe.wait_ge(c_in, 16 * 10)
            for n in range(10):
                for k in range(CC):
                    mm = nc.tensor.transpose(bank(n // 2)[:, (n % 2) * C + k * P:(n % 2) * C + k * P + P], w_nat[:, n, k * P:k * P + P], ident[:])
                if n % 2:
                    mm.then_inc(wt_psum, 1)
            pe.wait_ge(wt_s, 5)

            def project(b):
                pe.wait_ge(xs_s, b + 1)
                for t in range(TB):
                    for n0, n1 in ((0, 4), (4, 6)):
                        for k in range(CC):
                            mm = nc.tensor.matmul(bank(2 * t, 2)[:, n0 * P:n1 * P], xs_t[:, k, t * P:t * P + P], w_t[:, n0:n1, k, :],
                                                  start=(k == 0), stop=(k == CC - 1))
                    mm.then_inc(qkv_psum, 1)

            project(0)

            def stage(b, before, after):
                for n in range(2):
                    for k in range(CC):
                        mm = nc.tensor.matmul(bank(4)[:, n * T:n * T + T], w_t[:, 6 + n, k, :], xs_t[:, k, :], start=(k == 0), stop=(k == CC - 1))
                mm.then_inc(g_psum, 1)
                if before:
                    pe.wait_ge(y_s, b)
                pe.wait_ge(rot_s, b + 1)
                for x in range(2):
                    for k in range(2):
                        for t in range(TB):
                            mm = nc.tensor.transpose(bank(5 + x)[:, k * T + t * P:k * T + t * P + P],
                                                     qk[:, t, x, 2 * k:2 * k + 2, :].rearrange("p h d -> p (h d)"), ident[:])
                mm.then_inc(qkt_psum, 1)
                pe.wait_ge(qkt_s, b + 1)
                for h in range(RH):
                    rows, k = slice(RD * (h % 2), RD * (h % 2) + RD), h // 2
                    nc.tensor.matmul(bank(h)[:, 0:T], qk_t[rows, 1, k, 0:P], qk_t[rows, 0, k, :], start=True, stop=True)
                    mm = nc.tensor.matmul(bank(h)[:, T:T + P], qk_t[rows, 1, k, P:T], qk_t[rows, 0, k, P:T], start=True, stop=True)
                    mm.then_inc(sc_psum, 1)
                for h in range(RH):
                    pe.wait_ge(st_s, b * RH + h + 1)
                    rows, k = slice(RD * (h % 2), RD * (h % 2) + RD), h // 2
                    dst = bank(5)[rows, k * T:k * T + T]
                    nc.tensor.matmul(dst, v[:, 0, h, :], s_t[:, h, 0:T], start=True, stop=False, tile_position=(0, RD * (h % 2)))
                    mm = nc.tensor.matmul(dst[:, P:T], v[:, 1, h, :], s_t[:, h, T:T + P], start=False, stop=True,
                                          tile_position=(0, RD * (h % 2)))
                mm.then_inc(ret_psum, 1)
                pe.wait_ge(mom_s, b + 1)
                nc.tensor.matmul(bank(6)[:, 0:4], average[:], mom[:].rearrange("p k m -> p (k m)"), start=True, stop=True).then_inc(tot_psum, 1)
                if after:
                    project(b + 1)
                if before:
                    norm.tensor(pe, b - 1)
                pe.wait_ge(ym_s, b + 1)
                for t in range(TB):
                    for k in range(2):
                        mm = nc.tensor.matmul(bank(5)[:, t * C:t * C + C], ret[:, k, t * P:t * P + P], w_t[:, 8:10, k, :], start=(k == 0), stop=(k == 1))
                mm.then_inc(y_psum, 1)

            staged(pe, stage, lambda b: norm.tensor(pe, b))


def layer1_recurrence(nc, io, consts, bank, g, out):
    with ExitStack() as ctx:
        layer1_recurrence_in(nc, io, bank, g, *tools(nc, ctx, "l1w"))


def layer1_recurrence_in(nc, io, bank, g, sb, sem, dram):
    START = -1.0e38
    ident, xn, xt, ct = (g[n] for n in ("ident", "xn", "xt", "ct"))
    w, u = sb("w", [P, CC]), sb("u", [P, CC])
    o1, p1, q1 = (sb(n, [P, CC, T + 1]) for n in ("o1", "p1", "q1"))
    uk, top = sb("uk", [P, CC, T]), sb("top", [P, CC, T])
    e4 = sb("e4", [P, 4, CC, T])
    pv, ev = sb("pv", [P, CC, T]), sb("ev", [P, CC, T])
    num, dnm = sb("num", [P, CC, T]), sb("dnm", [P, CC, T])
    y_t = sb("y_t", [P, CC, T])
    norm = Norm(nc, g, sb, bank(6), 4, 3)
    c_in, set_s, uk_s, o_s, exps_s, exp_s, ev_s, pv_s, yt_s, y_psum, link_s = (
        sem(n) for n in ("c_in", "set_s", "uk_s", "o_s", "exps_s", "exp_s", "ev_s", "pv_s", "yt_s", "y_psum", "link_s"))
    LINKS = 10

    with nc.Block() as block:
        @block.sync
        def _(sp):
            with nc.allow_non_contiguous_dma("two short vectors"):
                sp.dma_start(w[:], io["L1_xattn_w"].rearrange("(k p) -> p k", p=P)).then_inc(c_in, 16)
                sp.dma_start(u[:], io["L1_xattn_u"].rearrange("(k p) -> p k", p=P)).then_inc(c_in, 16)

        @block.scalar
        def _(act):
            def stage(b, before):
                act.wait_ge(exps_s, b + 1)
                nc.scalar.activation(e4[:].rearrange("p n k t -> p (n k t)"), e4[:].rearrange("p n k t -> p (n k t)"), ACT.Exp).then_inc(exp_s, 1)
                if before:
                    norm.scalar(act, b - 1)

            deferred(act, stage, lambda b: norm.scalar(act, b))

        @block.vector
        def _(dve):
            nc.vector.memset(o1[:, :, 0:1], START).then_inc(set_s, 1)
            nc.vector.memset(p1[:, :, 0:1], 0.0).then_inc(set_s, 1)
            nc.vector.memset(q1[:, :, 0:1], 0.0).then_inc(set_s, 1)
            dve.wait_ge(set_s, 3)
            dve.wait_ge(c_in, 32)
            dve.sem_inc(yt_s, 1)

            def stage(b, before):
                link = Link(dve, link_s, LINKS, b)
                if before:
                    norm_measure(norm, dve, b - 1)
                kt = xt[:, :, bass.ds(b * T, T)]
                vt = ct[:, b]
                prior = o1[:, :, 0:T]
                for k in range(CC):
                    sc = nc.vector.tensor_tensor_scan(o1[:, k, 1:T + 1], w[:, k:k + 1].broadcast_to([P, T]), kt[:, k, :], START, ALU.add, ALU.max)
                link(sc)
                dve.wait_ge(uk_s, b + 1)
                link(nc.vector.tensor_tensor(top[:], prior, uk[:], ALU.max))
                nc.vector.tensor_tensor(e4[:, 0], prior, top[:], ALU.subtract)
                nc.vector.tensor_tensor(e4[:, 1], uk[:], top[:], ALU.subtract)
                for k in range(CC):
                    nc.vector.scalar_tensor_tensor(out=e4[:, 2, k], in0=o1[:, k, 0:T], scalar=w[:, k:k + 1], in1=o1[:, k, 1:T + 1],
                                                   op0=ALU.add, op1=ALU.subtract)
                nc.vector.tensor_tensor(e4[:, 3], kt, o1[:, :, 1:T + 1], ALU.subtract).then_inc(exps_s, 1)
                if before:
                    norm_scale(norm, dve, b - 1)
                    norm_keep(norm, dve, b - 1)
                dve.wait_ge(exp_s, b + 1)
                for k in range(CC):
                    sc = nc.vector.tensor_tensor_scan(q1[:, k, 1:T + 1], e4[:, 2, k], e4[:, 3, k], 0.0, ALU.mult, ALU.add)
                link(sc)
                link(nc.vector.tensor_tensor(dnm[:], e4[:, 0], q1[:, :, 0:T], ALU.mult))
                link(nc.vector.tensor_tensor(dnm[:], dnm[:], e4[:, 1], ALU.add))
                link(nc.vector.reciprocal(dnm[:], dnm[:]))
                dve.wait_ge(pv_s, b + 1)
                for k in range(CC):
                    sc = nc.vector.tensor_tensor_scan(p1[:, k, 1:T + 1], e4[:, 2, k], pv[:, k], 0.0, ALU.mult, ALU.add)
                link(sc)
                link(nc.vector.tensor_tensor(num[:], e4[:, 0], p1[:, :, 0:T], ALU.mult))
                dve.wait_ge(ev_s, b + 1)
                link(nc.vector.tensor_tensor(num[:], num[:], ev[:], ALU.add))
                nc.vector.tensor_tensor(y_t[:], num[:], dnm[:], ALU.mult).then_inc(yt_s, 1)
                dve.wait_ge(y_psum, b + 1)
                dve.wait_ge(yt_s, b + 2)
                link(nc.vector.tensor_tensor(norm.y[:].rearrange("p t c -> p (t c)"), bank(0), xn[:, b].rearrange("p t c -> p (t c)"), ALU.add))
                link.close()

            deferred(dve, stage, lambda b: norm.vector(dve, b))

        @block.gpsimd
        def _(pool):
            pool.wait_ge(c_in, 32)

            def stage(b, before):
                pool.wait_ge(yt_s, b + 1)
                ub = u[:].rearrange("p (k a) -> p k a", a=1).broadcast_to([P, CC, T])
                nc.gpsimd.tensor_tensor(uk[:], xt[:, :, bass.ds(b * T, T)], ub, ALU.add).then_inc(uk_s, 1)
                if before:
                    norm.gpsimd(pool, b - 1)
                pool.wait_ge(exp_s, b + 1)
                nc.gpsimd.tensor_tensor(pv[:], e4[:, 3], ct[:, b], ALU.mult).then_inc(pv_s, 1)
                nc.gpsimd.tensor_tensor(ev[:], e4[:, 1], ct[:, b], ALU.mult).then_inc(ev_s, 1)

            deferred(pool, stage, lambda b: norm.gpsimd(pool, b))

        @block.tensor
        def _(pe):
            def stage(b, before):
                if before:
                    norm.tensor(pe, b - 1)
                pe.wait_ge(yt_s, b + 2)
                for t in range(TB):
                    for k in range(CC):
                        mm = nc.tensor.transpose(bank(0)[:, t * C + k * P:t * C + k * P + P], y_t[:, k, t * P:t * P + P], ident[:])
                mm.then_inc(y_psum, 1)

            deferred(pe, stage, lambda b: norm.tensor(pe, b))


def mixed_inputs(io, consts, sb, sem, dram):
    E, EH = 32, 64
    KE = E * EH // P
    n = {
        "wv": sb("wv", [P, KE, C]), "wo": sb("wo", [P, KE, C]), "sim": sb("sim", [P, CC, E]), "gates": sb("gates", [NB, E]),
        "halves": sb("halves", [E, P]), "fold": sb("fold", [P, EH]), "pick": sb("pick", [E, KE]),
        "s_in": sem("s_in"), "w_in": sem("w_in"),
    }

    def load(sp):
        sp.dma_start(n["sim"][:], io["L1_ffn_sim_matrix"].rearrange("(k p) e -> p k e", p=P)).then_inc(n["s_in"], 16)
        sp.dma_start(n["gates"][:], io["L1_ffn_gates"].rearrange("(a e) -> a e", a=1).broadcast_to([NB, E])).then_inc(n["s_in"], 16)
        for name in ("halves", "fold", "pick"):
            sp.dma_start(n[name][:], consts[name]).then_inc(n["s_in"], 16)
        for dst, name in (("wv", "L1_ffn_w_v"), ("wo", "L1_ffn_o_weights")):
            sp.dma_start(n[dst][:], io[name].rearrange("(k e) h c -> (e h) k c", e=2)).then_inc(n["w_in"], 16)

    return n, load


def layer1_mixed_experts(nc, io, consts, bank, g, out):
    with ExitStack() as ctx:
        layer1_mixed_experts_in(nc, io, consts, bank, g, out, *tools(nc, ctx, "l1m"))


def layer1_mixed_experts_in(nc, io, consts, bank, g, out, sb, sem, dram):
    E, EH = 32, 64
    KE = E * EH // P
    TOP = E // 2
    GONE = -3.0e38
    ident, xn, xt, neg_half = (g[n] for n in ("ident", "xn", "xt", "neg_half"))
    wv, wo, sim, gates, halves, fold, pick, s_in, w_in = (
        g["mixed"][0][n] for n in ("wv", "wo", "sim", "gates", "halves", "fold", "pick", "s_in", "w_in"))
    sim2 = sb("sim2", [P, CC, E])
    ones = sb("ones", [P, NB])
    mean, mean2 = sb("mean", [P, CC, NB]), sb("mean2", [P, CC, NB])
    sq, rn = sb("sq", [NB, 1 + E]), sb("rn", [NB, 1 + E])
    raw, lg, gated, mask, fb, ra, rb2 = (sb(n, [NB, E]) for n in ("raw", "lg", "gated", "mask", "fb", "ra", "rb2"))
    top = sb("top", [NB, 2, 8])
    one = sb("one", [NB, 4])
    r_t, r_d, r_p = sb("r_t", [E, NB]), sb("r_d", [E, KE, NB]), sb("r_p", [P, KE, NB])
    mix = sb("mix", [P, KE, NB, EH])
    sums = sb("sums", [P, 2, 2, C])
    m = sb("m", [P, NB, CC, C])
    y, fin = sb("y", [P, NB, TB, C]), sb("fin", [P, NB, TB, C])
    stats, mv, rstd = sb("stats", [P, NB, TB, 6]), sb("mv", [P, NB, TB, 2]), sb("rstd", [P, NB * TB])
    mean_s, aff_psum, sq_s, rn_s, ex_s, exx_s, r_s, rt_psum, rt_s, rp_psum, mix_s = (
        sem(n) for n in ("mean_s", "aff_psum", "sq_s", "rn_s", "ex_s", "exx_s", "r_s", "rt_psum", "rt_s",
                         "rp_psum", "mix_s"))
    sum_psum, sum_s, m_psum, m_s, y_psum, var_s, rstd_s, fin_s, out_s, chain = (
        sem(n) for n in ("sum_psum", "sum_s", "m_psum", "m_s", "y_psum", "var_s", "rstd_s", "fin_s", "out_s", "chain"))

    with nc.Block() as block:
        @block.sync
        def _(sp):
            for b in range(NB):
                sp.wait_ge(fin_s, b + 1)
                sp.dma_start(out[b].rearrange("(t p) c -> p t c", p=P), fin[:, b]).then_inc(out_s, 16)
            sp.wait_ge(out_s, 16 * NB)

        @block.scalar
        def _(act):
            act.wait_ge(s_in, 16 * 5)
            nc.scalar.activation(gates[:], gates[:], ACT.Sigmoid).then_inc(exx_s, 1)
            act.wait_ge(ex_s, 1)
            nc.scalar.activation(ra[:], ra[:], ACT.Exp).then_inc(exx_s, 1)
            for n in range(4):
                act.wait_ge(sum_psum, n + 1)
                nc.scalar.copy(sums[:, n % 2, n // 2], bank(n)[:, 0:C]).then_inc(sum_s, 1)
            for b in range(NB):
                act.wait_ge(m_psum, b + 1)
                nc.scalar.copy(m[:, b].rearrange("p k c -> p (k c)"), bank(4 + b)).then_inc(m_s, 1)

        @block.vector
        def _(dve):
            n = [0]

            def step(ins):
                n[0] += 1
                ins.then_inc(chain, 1)
                dve.wait_ge(chain, n[0])

            step(nc.vector.memset(ones[:], 1.0))
            dve.wait_ge(s_in, 16 * 5)
            nc.vector.tensor_tensor(sim2[:], sim[:], sim[:], ALU.mult)
            step(nc.vector.tensor_reduce(mean[:], xt[:].rearrange("p k (b t) -> p k b t", b=NB), AX, ALU.add))
            step(nc.vector.tensor_scalar(mean[:], mean[:], 1.0 / T, None, ALU.mult))
            nc.vector.tensor_tensor(mean2[:], mean[:], mean[:], ALU.mult).then_inc(mean_s, 1)
            dve.wait_ge(aff_psum, 1)
            nc.vector.tensor_copy(raw[:], bank(0)[0:NB, 0:E])
            nc.vector.tensor_copy(sq[:], bank(0)[0:NB, E:2 * E + 1]).then_inc(sq_s, 1)
            dve.wait_ge(rn_s, 1)
            step(nc.vector.tensor_scalar(raw[:], raw[:], rn[:, E:E + 1], None, ALU.mult))
            step(nc.vector.tensor_tensor(raw[:], raw[:], rn[:, 0:E], ALU.mult))
            dve.wait_ge(exx_s, 1)
            step(nc.vector.tensor_tensor(lg[:], raw[:], gates[:], ALU.subtract))
            step(nc.vector.tensor_scalar(gated[:], lg[:], 0.0, None, ALU.max))
            step(nc.vector.tensor_scalar(mask[:], gated[:], 0.0, None, ALU.is_gt))
            step(nc.vector.tensor_reduce(one[:, 0:1], mask[:], AX, ALU.max))
            step(nc.vector.tensor_scalar(one[:, 0:1], one[:, 0:1], 0.0, None, ALU.is_equal))
            step(nc.vector.max(top[:, 0], lg[:]))
            step(nc.vector.match_replace(fb[:], top[:, 0], lg[:], GONE))
            step(nc.vector.max(top[:, 1], fb[:]))
            step(nc.vector.match_replace(fb[:], top[:, 1], fb[:], GONE))
            step(nc.vector.tensor_scalar(fb[:], fb[:], GONE, one[:, 0:1], ALU.is_equal, ALU.mult))
            step(nc.vector.tensor_tensor(mask[:], mask[:], fb[:], ALU.max))
            step(nc.vector.tensor_reduce(one[:, 1:2], gated[:], AX, ALU.max))
            nc.vector.tensor_scalar(ra[:], gated[:], one[:, 1:2], None, ALU.subtract).then_inc(ex_s, 1)
            dve.wait_ge(exx_s, 2)
            step(nc.vector.tensor_tensor(ra[:], ra[:], mask[:], ALU.mult))
            step(nc.vector.tensor_reduce(one[:, 2:3], ra[:], AX, ALU.add))
            step(nc.vector.reciprocal(one[:, 3:4], one[:, 2:3]))
            nc.vector.tensor_scalar(rb2[:], ra[:], one[:, 3:4], None, ALU.mult).then_inc(r_s, 1)
            dve.wait_ge(rt_psum, 1)
            step(nc.vector.tensor_copy(r_t[:], bank(1)[0:E, 0:NB]))
            nc.vector.tensor_tensor(r_d[:], r_t[:].rearrange("e (a b) -> e a b", a=1).broadcast_to([E, KE, NB]),
                                    pick[:].rearrange("e (k a) -> e k a", a=1).broadcast_to([E, KE, NB]), ALU.mult).then_inc(rt_s, 1)
            dve.wait_ge(rp_psum, 1)
            step(nc.vector.tensor_copy(r_p[:].rearrange("p k b -> p (k b)"), bank(1)[:, 64:64 + KE * NB]))
            for k in range(0, KE, 4):
                nc.vector.tensor_tensor(mix[:, k:k + 4].rearrange("p k b h -> p (k b) h"),
                                        r_p[:, k:k + 4].rearrange("p k (b a) -> p (k b) a", a=1).broadcast_to([P, 4 * NB, EH]),
                                        fold[:].rearrange("p (a h) -> p a h", a=1).broadcast_to([P, 4 * NB, EH]), ALU.mult).then_inc(mix_s, 1)
            for b in range(NB):
                dve.wait_ge(y_psum, b + 1)
                step(nc.vector.tensor_tensor(y[:, b].rearrange("p t c -> p (t c)"), bank(b), xn[:, b].rearrange("p t c -> p (t c)"), ALU.add))
                for t in range(TB):
                    st = nc.vector.bn_stats(stats[:, b, t], y[:, b, t])
                step(st)
                for t in range(TB):
                    ag = nc.vector.bn_aggr(mv[:, b, t], stats[:, b, t])
                step(ag)
                nc.vector.tensor_scalar(rstd[:, 2 * b:2 * b + 2], mv[:, b, :, 1], LN_EPS, None, ALU.add).then_inc(var_s, 1)
                dve.wait_ge(rstd_s, b + 1)
                for t in range(TB):
                    ts = nc.vector.tensor_scalar(fin[:, b, t], y[:, b, t], mv[:, b, t, 0:1], rstd[:, 2 * b + t:2 * b + t + 1],
                                                 ALU.subtract, ALU.mult)
                ts.then_inc(fin_s, 1)

        @block.gpsimd
        def _(pool):
            pool.wait_ge(sq_s, 1)
            nc.gpsimd.tensor_tensor(rn[:], sq[:], neg_half[0:NB, 0:1].broadcast_to([NB, 1 + E]), ALU.pow).then_inc(rn_s, 1)
            for b in range(NB):
                pool.wait_ge(var_s, b + 1)
                nc.gpsimd.tensor_tensor(rstd[:, 2 * b:2 * b + 2], rstd[:, 2 * b:2 * b + 2], neg_half[:, 0:TB], ALU.pow).then_inc(rstd_s, 1)

        @block.tensor
        def _(pe):
            pe.wait_ge(mean_s, 1)
            for dst, lhs, rhs in ((bank(0)[0:NB, 0:E], mean, sim), (bank(0)[0:NB, E:2 * E], None, sim2),
                                  (bank(0)[0:NB, 2 * E:2 * E + 1], mean2, None)):
                for k in range(CC):
                    mm = nc.tensor.matmul(dst, ones[:] if lhs is None else lhs[:, k], ones[:, 0:1] if rhs is None else rhs[:, k],
                                          start=(k == 0), stop=(k == CC - 1))
            mm.then_inc(aff_psum, 1)
            pe.wait_ge(r_s, 1)
            nc.tensor.transpose(bank(1)[0:E, 0:NB], rb2[:], ident[0:NB, 0:NB]).then_inc(rt_psum, 1)
            pe.wait_ge(rt_s, 1)
            nc.tensor.matmul(bank(1)[:, 64:64 + KE * NB], halves[:], r_d[:].rearrange("e k b -> e (k b)"), start=True, stop=True).then_inc(rp_psum, 1)
            pe.wait_ge(w_in, 32)
            for n in range(4):
                pair, w = n // 2, (wv, wo)[n % 2]
                for k in range(KE):
                    if n == 0 and k % 4 == 0:
                        pe.wait_ge(mix_s, k // 4 + 1)
                    mm = nc.tensor.matmul(bank(n)[:, 0:C], mix[:, k, 2 * pair:2 * pair + 2].rearrange("p b h -> p (b h)"), w[:, k],
                                          start=(k == 0), stop=(k == KE - 1))
                mm.then_inc(sum_psum, 1)
            for b in range(NB):
                pe.wait_ge(sum_s, 2 * (b // 2) + 2)
                rows = slice(EH * (b % 2), EH * (b % 2) + EH)
                for k in range(CC):
                    mm = nc.tensor.matmul(bank(4 + b)[:, k * C:k * C + C], sums[rows, 0, b // 2, k * P:k * P + P], sums[rows, 1, b // 2, :],
                                          start=True, stop=True)
                mm.then_inc(m_psum, 1)
            for b in range(NB):
                pe.wait_ge(m_s, b + 1)
                for t in range(TB):
                    for k in range(CC):
                        mm = nc.tensor.matmul(bank(b)[:, t * C:t * C + C], xt[:, k, b * T + t * P:b * T + t * P + P], m[:, b, k],
                                              start=(k == 0), stop=(k == CC - 1))
                mm.then_inc(y_psum, 1)


_OUT = (NB, T, C)


def kernel(**inputs):
    import concourse.bacc as bacc
    from concourse.bass_utils import run_bass_kernel_spmd

    nc = bacc.Bacc("TRN2", target_bir_lowering=False, num_devices=1)
    arrays, io = {}, {}
    for name, a in inputs.items():
        a = np.ascontiguousarray(a)
        arrays[f"in_{name}"] = a
        io[name] = nc.dram_tensor(f"in_{name}", a.shape, mybir.dt.from_np(a.dtype), kind="ExternalInput").ap()
    consts = {}
    for name, a in constants().items():
        arrays[f"const_{name}"] = a
        consts[name] = nc.dram_tensor(f"const_{name}", a.shape, mybir.dt.from_np(a.dtype), kind="ExternalInput").ap()
    out = nc.dram_tensor("out", _OUT, F32, kind="ExternalOutput").ap()
    build(nc, io, consts, out)
    return run_bass_kernel_spmd(nc, [arrays], core_ids=[0]).results[0]["out"]
```
